# Optimizing a Trainium2 kernel written in Bass

```python
import numpy as np
import jax
import jax.numpy as jnp

def _softmax(x, axis=-1):
    return jax.nn.softmax(x, axis=axis)

def _gelu(x):
    return jax.nn.gelu(x, approximate=True)

def _silu(x):
    return jax.nn.silu(x)

def _sigmoid(x):
    return jax.nn.sigmoid(x)

def _layernorm(x, axis=-1, eps=1e-05):
    m = jnp.mean(x, axis=axis, keepdims=True)
    v = jnp.var(x, axis=axis, keepdims=True)
    return (x - m) / jnp.sqrt(v + eps)

def _scatter_add(tgt, idx, src, axis=0):
    return tgt.at[idx].add(src)

def _segment_sum(src, seg, n):
    return jax.ops.segment_sum(src, seg, n)
kernel_name = 'mk_perceiver_d1_seqx_r4_ddf743'

def setup_inputs(seed: int=0):
    np.random.seed(seed)
    _w = jnp.asarray

    def _rec_inputs():
        import jax
        import jax.numpy as jnp
        _rk = jax.random.key(seed)
        x = -0.0003929 + 0.9999 * jax.random.normal(jax.random.fold_in(_rk, 1), (8, 64, 512), jnp.float32)
        _lenS = 64 - jax.random.randint(jax.random.fold_in(_rk, 7), (8,), 0, max(1, 64 // 4) + 1, jnp.int32)
        _lenS2 = 256 - jax.random.randint(jax.random.fold_in(_rk, 8), (8,), 0, max(1, 256 // 4) + 1, jnp.int32)
        _ctx_1024P = jax.random.normal(jax.random.fold_in(_rk, 11), (8, 16, 256), jnp.float32)
        _ctx_1024c = jax.random.dirichlet(jax.random.fold_in(_rk, 511), 0.3 * jnp.ones((16,), jnp.float32), (8, 256))
        _ctx_1024t = jnp.einsum('bsk,bkd->bsd', _ctx_1024c, _ctx_1024P)
        _ctx_1024t = _ctx_1024t * jax.lax.rsqrt(jnp.mean(jnp.square(_ctx_1024t)) + 1e-12) * 0.953939
        ctx_1024 = 0.000227908 + 0.99994 * (_ctx_1024t + 0.3 * jax.random.normal(jax.random.fold_in(_rk, 611), (8, 256, 256), jnp.float32))
        return (x, ctx_1024)
    x, ctx_1024 = _rec_inputs()

    def _L0_xattn_setup():
        import jax, jax.numpy as jnp
        import numpy as np
        EPS = 1e-05

        def rmsnorm(x, g, eps=EPS):
            var = jnp.mean(jnp.square(x), axis=-1, keepdims=True)
            return x * jax.lax.rsqrt(var + eps) * g
        key = jax.random.key(seed)
        ks = jax.random.split(key, 8)
        B, Sq, Skv = (2, 1024, 128)
        dim, cdim, H, D = (512, 256, 16, 128)
        inner = H * D
        s = lambda f: 1.0 / np.sqrt(f)
        return {'hidden_states': jax.random.normal(ks[0], (B, Sq, dim), jnp.float32), 'encoder_hidden_states': jax.random.normal(ks[1], (B, Skv, cdim), jnp.float32), 'Wq': jax.random.normal(ks[2], (dim, inner), jnp.float32) * s(dim), 'Wk': jax.random.normal(ks[3], (cdim, inner), jnp.float32) * s(cdim), 'Wv': jax.random.normal(ks[4], (cdim, inner), jnp.float32) * s(cdim), 'Wo': jax.random.normal(ks[5], (inner, dim), jnp.float32) * s(inner), 'gq': jnp.ones((D,), jnp.float32), 'gk': jnp.ones((D,), jnp.float32)}
    _L0_xattn_all = _L0_xattn_setup()
    _L0_xattn_in = {k: v for k, v in _L0_xattn_all.items() if k in ('Wq', 'Wk', 'Wv', 'Wo', 'gq', 'gk')}
    del _L0_xattn_all

    def _L0_attn_setup():
        import jax, jax.numpy as jnp
        import numpy as np
        NH = 16
        D = 128
        C = 64
        EPS = 1e-12

        def _l2norm(x):
            n = jnp.linalg.norm(x, axis=-1, keepdims=True)
            return x / jnp.maximum(n, EPS)
        key = jax.random.key(seed)
        ks = jax.random.split(key, 12)
        B, L, H = (4, 1024, 512)
        std = 0.02
        f32 = jnp.float32
        inp = {'hidden_states': jax.random.normal(ks[0], (B, L, H), f32), 'q_w': jax.random.normal(ks[1], (NH * D, H), f32) * std, 'q_b': jnp.zeros((NH * D,), f32), 'k_w': jax.random.normal(ks[2], (NH * D, H), f32) * std, 'k_b': jnp.zeros((NH * D,), f32), 'v_w': jax.random.normal(ks[3], (NH * D, H), f32) * std, 'v_b': jnp.zeros((NH * D,), f32), 'a_w': jax.random.normal(ks[4], (NH, H), f32) * std, 'a_b': jnp.zeros((NH,), f32), 'b_w': jax.random.normal(ks[5], (NH, H), f32) * std, 'b_b': jnp.zeros((NH,), f32), 'og_w': jax.random.normal(ks[6], (NH * D, H), f32) * std, 'o_w': jax.random.normal(ks[7], (H, NH * D), f32) * std, 'o_b': jnp.zeros((H,), f32)}
        return inp
    _L0_attn_all = _L0_attn_setup()
    _L0_attn_in = {k: v for k, v in _L0_attn_all.items() if k in ('q_w', 'q_b', 'k_w', 'k_b', 'v_w', 'v_b', 'a_w', 'a_b', 'b_w', 'b_b', 'og_w', 'o_w', 'o_b')}
    del _L0_attn_all

    def _L0_ffn_setup():
        import jax, jax.numpy as jnp
        import numpy as np
        from jax import lax
        DIM = 512
        INTER = 352
        N_EXPERTS = 32
        TOP_K = 6
        N_SHARED = 2
        CAPACITY = 512
        ROUTE_SCALE = 1.0

        def _gate(xf, gate_w):
            logits = xf @ gate_w.T
            scores = jax.nn.softmax(logits.astype(jnp.float32), axis=-1)
            top_w, top_i = lax.top_k(scores, TOP_K)
            return ((top_w * ROUTE_SCALE).astype(xf.dtype), top_i)

        def _moe(xf, gate_w, w1, w2, w3):
            T, D = xf.shape
            E, CAP = (N_EXPERTS, CAPACITY)
            top_w, top_i = _gate(xf, gate_w)
            e_flat = top_i.reshape(-1)
            t_flat = jnp.repeat(jnp.arange(T), TOP_K)
            w_flat = top_w.reshape(-1)
            order = jnp.argsort(e_flat)
            e_s, t_s, w_s = (e_flat[order], t_flat[order], w_flat[order])
            counts = jnp.zeros((E,), jnp.int32).at[e_s].add(1)
            starts = jnp.concatenate([jnp.zeros((1,), jnp.int32), jnp.cumsum(counts)[:-1]])
            pos = jnp.arange(T * TOP_K, dtype=jnp.int32) - starts[e_s]
            valid = pos < CAP
            buf_idx = jnp.where(valid, e_s * CAP + pos, E * CAP)
            xbuf = jnp.zeros((E * CAP + 1, D), xf.dtype).at[buf_idx].set(xf[t_s])
            xb = xbuf[:E * CAP].reshape(E, CAP, D)
            h = jax.nn.silu(jnp.einsum('ecd,edi->eci', xb, w1)) * jnp.einsum('ecd,edi->eci', xb, w3)
            ob = jnp.einsum('eci,eid->ecd', h, w2).reshape(E * CAP, D)
            ob = jnp.concatenate([ob, jnp.zeros((1, D), ob.dtype)], axis=0)
            y_pairs = ob[buf_idx] * w_s[:, None]
            y = jnp.zeros((T, D), xf.dtype).at[t_s].add(y_pairs)
            return y
        key = jax.random.key(seed)
        ks = jax.random.split(key, 9)
        B, S = (4, 512)
        si = INTER * N_SHARED
        inputs = {'x': jax.random.normal(ks[0], (B, S, DIM), jnp.float32), 'gate_w': jax.random.normal(ks[1], (N_EXPERTS, DIM), jnp.float32), 'w1': jax.random.normal(ks[2], (N_EXPERTS, DIM, INTER), jnp.float32) * DIM ** (-0.5), 'w2': jax.random.normal(ks[3], (N_EXPERTS, INTER, DIM), jnp.float32) * INTER ** (-0.5), 'w3': jax.random.normal(ks[4], (N_EXPERTS, DIM, INTER), jnp.float32) * DIM ** (-0.5), 'sw1': jax.random.normal(ks[5], (DIM, si), jnp.float32) * DIM ** (-0.5), 'sw2': jax.random.normal(ks[6], (si, DIM), jnp.float32) * si ** (-0.5), 'sw3': jax.random.normal(ks[7], (DIM, si), jnp.float32) * DIM ** (-0.5)}
        return inputs
    _L0_ffn_all = _L0_ffn_setup()
    _L0_ffn_in = {k: v for k, v in _L0_ffn_all.items() if k in ('gate_w', 'w1', 'w2', 'w3', 'sw1', 'sw2', 'sw3')}
    del _L0_ffn_all
    return {'x': x, 'ctx_1024': ctx_1024, 'L0_xattn_Wq': _L0_xattn_in['Wq'], 'L0_xattn_Wk': _L0_xattn_in['Wk'], 'L0_xattn_Wv': _L0_xattn_in['Wv'], 'L0_xattn_Wo': _L0_xattn_in['Wo'], 'L0_xattn_gq': _L0_xattn_in['gq'], 'L0_xattn_gk': _L0_xattn_in['gk'], 'L0_attn_q_w': _L0_attn_in['q_w'], 'L0_attn_q_b': _L0_attn_in['q_b'], 'L0_attn_k_w': _L0_attn_in['k_w'], 'L0_attn_k_b': _L0_attn_in['k_b'], 'L0_attn_v_w': _L0_attn_in['v_w'], 'L0_attn_v_b': _L0_attn_in['v_b'], 'L0_attn_a_w': _L0_attn_in['a_w'], 'L0_attn_a_b': _L0_attn_in['a_b'], 'L0_attn_b_w': _L0_attn_in['b_w'], 'L0_attn_b_b': _L0_attn_in['b_b'], 'L0_attn_og_w': _L0_attn_in['og_w'], 'L0_attn_o_w': _L0_attn_in['o_w'], 'L0_attn_o_b': _L0_attn_in['o_b'], 'L0_ffn_gate_w': _L0_ffn_in['gate_w'], 'L0_ffn_w1': _L0_ffn_in['w1'], 'L0_ffn_w2': _L0_ffn_in['w2'], 'L0_ffn_w3': _L0_ffn_in['w3'], 'L0_ffn_sw1': _L0_ffn_in['sw1'], 'L0_ffn_sw2': _L0_ffn_in['sw2'], 'L0_ffn_sw3': _L0_ffn_in['sw3']}

def reference(x, ctx_1024, L0_xattn_Wq, L0_xattn_Wk, L0_xattn_Wv, L0_xattn_Wo, L0_xattn_gq, L0_xattn_gk, L0_attn_q_w, L0_attn_q_b, L0_attn_k_w, L0_attn_k_b, L0_attn_v_w, L0_attn_v_b, L0_attn_a_w, L0_attn_a_b, L0_attn_b_w, L0_attn_b_b, L0_attn_og_w, L0_attn_o_w, L0_attn_o_b, L0_ffn_gate_w, L0_ffn_w1, L0_ffn_w2, L0_ffn_w3, L0_ffn_sw1, L0_ffn_sw2, L0_ffn_sw3):
    import jax
    import jax.numpy as jnp

    def _L0_xattn_ref(hidden_states, encoder_hidden_states, Wq, Wk, Wv, Wo, gq, gk):
        import jax, jax.numpy as jnp
        import numpy as np
        EPS = 1e-05

        def rmsnorm(x, g, eps=EPS):
            var = jnp.mean(jnp.square(x), axis=-1, keepdims=True)
            return x * jax.lax.rsqrt(var + eps) * g
        B, Sq, _ = hidden_states.shape
        Skv = encoder_hidden_states.shape[1]
        D = gq.shape[0]
        H = Wq.shape[1] // D
        scale = 1.0 / np.sqrt(D)
        q = (hidden_states @ Wq).reshape(B, Sq, H, D)
        k = (encoder_hidden_states @ Wk).reshape(B, Skv, H, D)
        v = (encoder_hidden_states @ Wv).reshape(B, Skv, H, D)
        q = rmsnorm(q, gq)
        k = rmsnorm(k, gk)
        scores = jnp.einsum('bqhd,bkhd->bhqk', q, k) * scale
        attn = jax.nn.softmax(scores, axis=-1)
        out = jnp.einsum('bhqk,bkhd->bqhd', attn, v)
        out = out.reshape(B, Sq, H * D)
        return out @ Wo

    def _L0_attn_ref(hidden_states, q_w, q_b, k_w, k_b, v_w, v_b, a_w, a_b, b_w, b_b, og_w, o_w, o_b):
        import jax, jax.numpy as jnp
        import numpy as np
        NH = 16
        D = 128
        C = 64
        EPS = 1e-12

        def _l2norm(x):
            n = jnp.linalg.norm(x, axis=-1, keepdims=True)
            return x / jnp.maximum(n, EPS)
        B, L, H = hidden_states.shape
        nh, d, c = (NH, D, C)
        hs = hidden_states
        q = (hs @ q_w.T + q_b).reshape(B, L, nh, d)
        k = (hs @ k_w.T + k_b).reshape(B, L, nh, d)
        v = (hs @ v_w.T + v_b).reshape(B, L, nh, d)
        beta = jax.nn.softplus(hs @ b_w.T + b_b)
        scale = float(d) ** 0.5
        qn = _l2norm(q / scale)
        kn = _l2norm(k / scale)
        gv = beta[..., None] * v
        nchunks = L // c

        def to_chunks(x):
            return x.reshape(B, nchunks, c, nh, d).transpose(0, 1, 3, 2, 4)
        qc, kc, gvc = (to_chunks(qn), to_chunks(kn), to_chunks(gv))
        attn = jnp.einsum('bnhid,bnhjd->bnhij', qc, kc)
        pos = jnp.arange(c, dtype=jnp.float32)
        dist = jnp.clip(pos[None, :] - pos[:, None], 0.0, None)
        decay = jnp.exp(-0.1 * dist)
        causal = pos[None, :] <= pos[:, None]
        mask = jnp.where(causal, decay, 0.0)
        out = jnp.einsum('bnhij,bnhjd->bnhid', attn * mask, gvc)
        out = out.transpose(0, 1, 3, 2, 4).reshape(B, L, nh * d)
        gate = jax.nn.silu(hs @ og_w.T)
        out = out * gate
        return out @ o_w.T + o_b

    def _L0_ffn_ref(x, gate_w, w1, w2, w3, sw1, sw2, sw3):
        import jax, jax.numpy as jnp
        import numpy as np
        from jax import lax
        DIM = 512
        INTER = 352
        N_EXPERTS = 32
        TOP_K = 6
        N_SHARED = 2
        CAPACITY = 512
        ROUTE_SCALE = 1.0

        def _gate(xf, gate_w):
            logits = xf @ gate_w.T
            scores = jax.nn.softmax(logits.astype(jnp.float32), axis=-1)
            top_w, top_i = lax.top_k(scores, TOP_K)
            return ((top_w * ROUTE_SCALE).astype(xf.dtype), top_i)

        def _moe(xf, gate_w, w1, w2, w3):
            T, D = xf.shape
            E, CAP = (N_EXPERTS, CAPACITY)
            top_w, top_i = _gate(xf, gate_w)
            e_flat = top_i.reshape(-1)
            t_flat = jnp.repeat(jnp.arange(T), TOP_K)
            w_flat = top_w.reshape(-1)
            order = jnp.argsort(e_flat)
            e_s, t_s, w_s = (e_flat[order], t_flat[order], w_flat[order])
            counts = jnp.zeros((E,), jnp.int32).at[e_s].add(1)
            starts = jnp.concatenate([jnp.zeros((1,), jnp.int32), jnp.cumsum(counts)[:-1]])
            pos = jnp.arange(T * TOP_K, dtype=jnp.int32) - starts[e_s]
            valid = pos < CAP
            buf_idx = jnp.where(valid, e_s * CAP + pos, E * CAP)
            xbuf = jnp.zeros((E * CAP + 1, D), xf.dtype).at[buf_idx].set(xf[t_s])
            xb = xbuf[:E * CAP].reshape(E, CAP, D)
            h = jax.nn.silu(jnp.einsum('ecd,edi->eci', xb, w1)) * jnp.einsum('ecd,edi->eci', xb, w3)
            ob = jnp.einsum('eci,eid->ecd', h, w2).reshape(E * CAP, D)
            ob = jnp.concatenate([ob, jnp.zeros((1, D), ob.dtype)], axis=0)
            y_pairs = ob[buf_idx] * w_s[:, None]
            y = jnp.zeros((T, D), xf.dtype).at[t_s].add(y_pairs)
            return y
        shape = x.shape
        xf = x.reshape(-1, DIM)
        y = _moe(xf, gate_w, w1, w2, w3)
        shared = jax.nn.silu(xf @ sw1) * (xf @ sw3) @ sw2
        return (y + shared).reshape(shape)
    x = x + _L0_xattn_ref(_layernorm(x, axis=-1), ctx_1024, L0_xattn_Wq, L0_xattn_Wk, L0_xattn_Wv, L0_xattn_Wo, L0_xattn_gq, L0_xattn_gk)
    x = x + _L0_attn_ref(_layernorm(x, axis=-1), L0_attn_q_w, L0_attn_q_b, L0_attn_k_w, L0_attn_k_b, L0_attn_v_w, L0_attn_v_b, L0_attn_a_w, L0_attn_a_b, L0_attn_b_w, L0_attn_b_b, L0_attn_og_w, L0_attn_o_w, L0_attn_o_b)
    x = x + _L0_ffn_ref(_layernorm(x, axis=-1), L0_ffn_gate_w, L0_ffn_w1, L0_ffn_w2, L0_ffn_w3, L0_ffn_sw1, L0_ffn_sw2, L0_ffn_sw3)
    return x

_drawn_inputs = setup_inputs


def setup_inputs(seed=0):
    import zlib

    import numpy as np

    out = dict(_drawn_inputs(seed))
    spreads = {'L0_xattn_gq': (1.0, 0.2),
     'L0_xattn_gk': (1.0, 0.2),
     'L0_attn_q_b': (0.0, 0.356),
     'L0_attn_k_b': (0.0, 0.1),
     'L0_attn_v_b': (0.0, 0.1),
     'L0_attn_a_b': (0.0, 0.1),
     'L0_attn_b_b': (0.0, 0.8),
     'L0_attn_o_b': (0.0, 0.1)}
    factors = {}
    for name, (base, spread) in spreads.items():
        noise = np.random.default_rng([zlib.crc32(name.encode()), seed]).standard_normal(out[name].shape)
        drawn = base * np.exp(spread * noise) if base else spread * noise
        out[name] = jnp.asarray(drawn.astype(out[name].dtype))
    for name, factor in factors.items():
        out[name] = (out[name] * factor).astype(out[name].dtype)
    return out
```

```python
from contextlib import ExitStack

import concourse.bass as bass
from concourse import mybir

ALU = mybir.AluOpType
ACT = mybir.ActivationFunctionType
AX = mybir.AxisListType
F32 = mybir.dt.float32
F32R = mybir.dt.float32r
I32 = mybir.dt.int32

P = 128
LN_EPS = 1e-5
RMS_EPS = 1e-5
L2_EPS = 1e-12
TOP_K = 6


def perceiver_block(nc, x_in, ctx_in, ctxT_in, Wq, Wk, WkT, Wv, Wo, gq, gk,
                    qwT, q_b, kwT, k_b, vwT, v_b, bwT, b_b, ogwT, owT, o_b,
                    gwT, w1, w2, w3, out):
    T, D = x_in.shape
    NKV, C = ctx_in.shape
    INNER = Wq.shape[1]
    H = INNER // P
    B = 8
    SQ = T // B
    SKV = NKV // B
    TT, DC, CC, KT = T // P, D // P, C // P, NKV // P
    KPB = SKV // P
    HP = H // 2
    JB = 4
    G4 = 512
    RSD = float(P) ** -0.5

    stack = ExitStack()
    with stack:
        def sem(name):
            return stack.enter_context(nc.semaphore(name))

        def sbuf(where, name, shape, dt=F32):
            return where.enter_context(nc.sbuf_tensor(name, shape, dt))

        ps = stack.enter_context(nc.psum_tensor("ps", [P, 8, 512], F32))

        x = sbuf(stack, "x", [P, TT, D])
        xT_hi = sbuf(stack, "xT_hi", [P, DC, T], F32R)
        xT_lo = sbuf(stack, "xT_lo", [P, DC, T], F32R)
        ident = sbuf(stack, "ident", [P, P])
        zeros = sbuf(stack, "zeros", [P, D])
        ones = sbuf(stack, "ones", [P, P])
        eps = sbuf(stack, "eps", [P, 1])
        ln_std = sbuf(stack, "ln_std", [P, TT])
        ln_stat = sbuf(stack, "ln_stat", [P, TT, 6])
        ln_mv = sbuf(stack, "ln_mv", [P, TT, 2])
        ln_rstd = sbuf(stack, "ln_rstd", [P, TT])

        attn = ExitStack()
        aoT = sbuf(attn, "aoT", [P, H, T])
        wo_raw = sbuf(attn, "wo_raw", [P, 2, D])
        wo_h = sbuf(attn, "wo_h", [P, 2, D], F32R)
        wo_l = sbuf(attn, "wo_l", [P, 2, D], F32R)
        ao_h = sbuf(attn, "ao_h", [P, 2, T], F32R)
        ao_l = sbuf(attn, "ao_l", [P, 2, T], F32R)

        xat = ExitStack()
        ctxT = sbuf(xat, "ctxT", [P, CC, NKV])
        ctx = sbuf(xat, "ctx", [P, KT, C])
        gqk = sbuf(xat, "gqk", [P, 3])
        kn = ExitStack()
        ssk = sbuf(kn, "ssk", [P, KT, H])
        rk_ln = sbuf(kn, "rk_ln", [P, KT, H])
        rkT = sbuf(kn, "rkT", [P, 2, P])
        xn_a = sbuf(kn, "xn_a", [P, TT, D])
        wk_raw = sbuf(kn, "wk_raw", [P, CC, INNER])
        wk_h = sbuf(kn, "wk_h", [P, CC, INNER], F32R)
        wk_l = sbuf(kn, "wk_l", [P, CC, INNER], F32R)
        cT_h = sbuf(kn, "cT_h", [P, CC, NKV], F32R)
        cT_l = sbuf(kn, "cT_l", [P, CC, NKV], F32R)
        sqk = sbuf(kn, "sqk", [P, 2, G4])
        kn.close()
        hd = ExitStack()
        wq_raw = sbuf(hd, "wq_raw", [P, DC, 2 * P])
        wq_h = sbuf(hd, "wq_h", [P, DC, 2 * P], F32R)
        wq_l = sbuf(hd, "wq_l", [P, DC, 2 * P], F32R)
        wkT_raw = sbuf(hd, "wkT_raw", [P, 2, C])
        wkT_h = sbuf(hd, "wkT_h", [P, 2, C], F32R)
        wkT_l = sbuf(hd, "wkT_l", [P, 2, C], F32R)
        wv_raw = sbuf(hd, "wv_raw", [P, CC, 2 * P])
        wv_h = sbuf(hd, "wv_h", [P, CC, 2 * P], F32R)
        wv_l = sbuf(hd, "wv_l", [P, CC, 2 * P], F32R)
        sq = sbuf(hd, "sq", [P, 2, T])
        qg = sbuf(hd, "qg", [P, 2, T])
        rB = sbuf(hd, "rB", [P, 2, T])
        qn_h = sbuf(hd, "qn_h", [P, 2, T], F32R)
        qn_l = sbuf(hd, "qn_l", [P, 2, T], F32R)
        qpT = sbuf(hd, "qpT", [P, CC, B, 2, SQ])
        rkB = sbuf(hd, "rkB", [P, B, SKV])
        sc = sbuf(hd, "sc", [P, B, SKV])
        nmx = sbuf(hd, "nmx", [P, B])
        sm = sbuf(hd, "sm", [P, B])
        rsm = sbuf(hd, "rsm", [P, B])
        pT = sbuf(hd, "pT", [P, B, KPB, P])
        u_h = sbuf(hd, "u_h", [P, CC, B, 2, SQ], F32R)
        u_l = sbuf(hd, "u_l", [P, CC, B, 2, SQ], F32R)
        hd.close()
        xat.close()

        lin = ExitStack()
        xn_b = sbuf(lin, "xn_b", [P, TT, D])
        lw_raw = [sbuf(lin, f"lw_raw{n}", [P, DC, 2 * P]) for n in range(4)]
        lw_h = [sbuf(lin, f"lw_h{n}", [P, DC, 2 * P], F32R) for n in range(4)]
        lw_l = [sbuf(lin, f"lw_l{n}", [P, DC, 2 * P], F32R) for n in range(4)]
        kq = sbuf(lin, "kq", [P, 4, T])
        kq_sq = sbuf(lin, "kq_sq", [P, 4, T])
        kq_r = sbuf(lin, "kq_r", [P, 4, T])
        kq_b = sbuf(lin, "kq_b", [P, 2, H])
        vt = sbuf(lin, "vt", [P, TT, 2 * P])
        v_bias = sbuf(lin, "v_bias", [P, INNER])
        at = sbuf(lin, "at", [P, 2, T])
        sg = sbuf(lin, "sg", [P, 2, T])
        mask = sbuf(lin, "mask", [P, P])
        ob_B = sbuf(lin, "ob_B", [P, D])
        bw_raw = sbuf(lin, "bw_raw", [P, DC, H])
        bw_h = sbuf(lin, "bw_h", [P, DC, H], F32R)
        bw_l = sbuf(lin, "bw_l", [P, DC, H], F32R)
        bb_B = sbuf(lin, "bb_B", [P, H])
        beta = sbuf(lin, "beta", [P, TT, H])
        sp = sbuf(lin, "sp", [P, 6, TT * H])
        lin.close()
        attn.close()

        E = gwT.shape[1]
        FF = w1.shape[2]
        FC = -(-FF // P)
        FW = [min(P, FF - c * P) for c in range(FC)]
        CAP = T
        CT = CAP // P
        MI = E + T * TOP_K // P
        ML = MI + 2
        moe = ExitStack()
        xn_c = sbuf(moe, "xn_c", [P, TT, D])
        GB = 8
        gb = sbuf(moe, "gb", [P, GB, D])
        xe = sbuf(moe, "xe", [P, 2, D])
        xeT_h = sbuf(moe, "xeT_h", [P, 2, DC, P], F32R)
        xeT_l = sbuf(moe, "xeT_l", [P, 2, DC, P], F32R)
        h1 = sbuf(moe, "h1", [P, 2, FF])
        h = sbuf(moe, "h", [P, 2, FF])
        hT_h = sbuf(moe, "hT_h", [P, 2, FC, P], F32R)
        hT_l = sbuf(moe, "hT_l", [P, 2, FC, P], F32R)
        ob = sbuf(moe, "ob", [P, 2, D])
        idx_col = sbuf(moe, "idx_col", [P, 2], I32)
        gw_raw = sbuf(moe, "gw_raw", [P, DC, E])
        gw_h = sbuf(moe, "gw_h", [P, DC, E], F32R)
        gw_l = sbuf(moe, "gw_l", [P, DC, E], F32R)
        gate = sbuf(moe, "gate", [P, TT, E])
        r_small = sbuf(moe, "r_small", [P, 3, TT])
        top_w = sbuf(moe, "top_w", [P, TT, 8])
        top_i = sbuf(moe, "top_i", [P, TT, 8], mybir.dt.uint32)
        top_f = sbuf(moe, "top_f", [P, TT, 8])
        hot = sbuf(moe, "hot", [P, TT, TOP_K, E])
        hotp = sbuf(moe, "hotp", [P, TT, TOP_K, E])
        chosen = sbuf(moe, "chosen", [P, TT, E])
        chosen4 = sbuf(moe, "chosen4", [P, TT, E, CT])
        pos = sbuf(moe, "pos", [P, TT, E])
        slot_f = sbuf(moe, "slot_f", [P, TT, TOP_K])
        slot_i = sbuf(moe, "slot_i", [P, TT, TOP_K], I32)
        iota_e = sbuf(moe, "iota_e", [P, ML])
        strict = sbuf(moe, "strict", [P, P])
        part = sbuf(moe, "part", [P, 2])
        part_i = sbuf(moe, "part_i", [P, 3], I32)
        tok_id = sbuf(moe, "tok_id", [P, TT])
        tl_rows = sbuf(moe, "tl_rows", [P, P])
        tl = sbuf(moe, "tl", [P, ML], I32)
        valid_B = sbuf(moe, "valid_B", [P, P])
        below = sbuf(moe, "below", [P, E])
        start = sbuf(moe, "start", [P, E])
        cnt = sbuf(moe, "cnt", [P, 4])
        m_hot = sbuf(moe, "m_hot", [P, ML])
        lst_f = sbuf(moe, "lst_f", [1, ML + 1])
        lst = sbuf(moe, "lst", [1, ML + 1], I32)
        w13_raw = sbuf(moe, "w13_raw", [P, 2, DC, 2 * FF])
        w13_h = sbuf(moe, "w13_h", [P, 2, DC, 2 * FF], F32R)
        w13_l = sbuf(moe, "w13_l", [P, 2, DC, 2 * FF], F32R)
        w2_raw = sbuf(moe, "w2_raw", [P, 2, FC, D])
        w2_h = sbuf(moe, "w2_h", [P, 2, FC, D], F32R)
        w2_l = sbuf(moe, "w2_l", [P, 2, FC, D], F32R)
        moe.close()

        xn_dram = nc.dram_tensor("xn_scratch", [T, D], F32)
        tl_dram = nc.dram_tensor("token_list_scratch", [ML * P, 1], F32)
        ob_dram = nc.dram_tensor("expert_out_scratch", [MI * P, D], F32)
        rk_dram = nc.dram_tensor("rk_scratch", [H, NKV], F32)

        consts = sem("consts")
        x_in_s, ctx_in_s, ctxT_in_s, g_in_s = sem("x_in"), sem("ctx_in_s"), sem("ctxT_in_s"), sem("g_in")
        wk_in = sem("wk_in")
        dve_step = sem("dve_step")
        xn_ready, xT_ps, xT_hi_s, xT_ready = sem("xn_ready"), sem("xT_ps"), sem("xT_hi_s"), sem("xT_ready")
        cT_hi_s, cT_ready, wk_hi_s, wk_ready = sem("cT_hi_s"), sem("cT_ready"), sem("wk_hi_s"), sem("wk_ready")
        k_ps, sqk_ready, sqk_free = sem("k_ps"), sem("sqk_ready"), sem("sqk_free")
        rkT_ready, scratch_io = sem("rkT_ready"), sem("scratch_io")
        small_ps, small_dve, small_hi, small_lo = sem("small_ps"), sem("small_dve"), sem("small_hi"), sem("small_lo")
        PS_RKT, PS_BETA, PS_LOGITS, PS_POS, PS_PREFIX, PS_LIST, PS_TOKENS = 2, 3, 4, 5, 6, 7, 8
        DV_SSK, DV_RK, DV_KQB, DV_VALID, DV_ORDER, DV_SLOTS, DV_LISTS, DV_TOKENS = 1, 3, 4, 5, 6, 7, 8, 9
        SP_BETA, SP_ROUTER = 1, 2
        IO_RK, IO_CLEARED, IO_LISTS = 32, 64, 80
        wq_in, wq_hi_s, wq_ready = sem("wq_in"), sem("wq_hi_s"), sem("wq_ready")
        wkT_in, wkT_hi_s, wkT_ready = sem("wkT_in"), sem("wkT_hi_s"), sem("wkT_ready")
        wv_in, wv_hi_s, wv_ready = sem("wv_in"), sem("wv_hi_s"), sem("wv_ready")
        rkB_in = [sem(f"rkB_in{j}") for j in range(JB)]
        q_ps, sq_ready, qg_ready, ss_ps = sem("q_ps"), sem("sq_ready"), sem("qg_ready"), sem("ss_ps")
        qn_ready, qn_hi_s, qn_split = sem("qn_ready"), sem("qn_hi_s"), sem("qn_split")
        qp_ps, qp_ready = sem("qp_ps"), sem("qp_ready")
        s_ps, s_ready, nmx_ready, p_ready, pn_ready = sem("s_ps"), sem("s_ready"), sem("nmx_ready"), sem("p_ready"), sem("pn_ready")
        pT_ps, pT_ready, u_ps, u_hi_s, u_ready = sem("pT_ps"), sem("pT_ready"), sem("u_ps"), sem("u_hi_s"), sem("u_ready")
        ao_ps, ao_ready = sem("ao_ps"), sem("ao_ready")
        wo_in = [sem("wo_in0"), sem("wo_in1")]
        wo_hi_s, wo_ready, ao_split, wo_mm, y_ps = sem("wo_hi_s"), sem("wo_ready"), sem("ao_split"), sem("wo_mm"), sem("y_ps")
        x_ready = sem("x_ready")
        out_done = sem("out_done")
        lw_in = [sem(f"lw_in{n}") for n in range(4)]
        lw_hi_s = [sem(f"lw_hi_s{n}") for n in range(4)]
        lw_ready = [sem(f"lw_ready{n}") for n in range(4)]
        lin_in = sem("lin_in")
        mask_ready = sem("mask_ready")
        sp_dve, sp_act, beta_ready = sem("sp_dve"), sem("sp_act"), sem("beta_ready")
        kq_ps, kq_ready, kq_sq_ready, kq_ss_ps, kq_norm, kq_recip, kq_n = (
            sem("kq_ps"), sem("kq_ready"), sem("kq_sq_ready"), sem("kq_ss_ps"), sem("kq_norm"), sem("kq_recip"), sem("kq_n"))
        v_ps, v_biased, v_ready = sem("v_ps"), sem("v_biased"), sem("v_ready")
        og_ps, sg_ready, at_ps, at_ready, o_ps = sem("og_ps"), sem("sg_ready"), sem("at_ps"), sem("at_ready"), sem("o_ps")
        moe_in, pool_consts, rt_dve, rt_act, tl_scattered = (
            sem("moe_in"), sem("pool_consts"), sem("rt_dve"), sem("rt_act"), sem("tl_scattered"))
        shd_ps, sh_x = sem("shd_ps"), sem("sh_x")
        w13_in, w2_in = [sem("w13_in0"), sem("w13_in1")], [sem("w2_in0"), sem("w2_in1")]
        w13_hi_s, w13_ready, w2_hi_s, w2_ready = sem("w13_hi_s"), sem("w13_ready"), sem("w2_hi_s"), sem("w2_ready")
        idx_ready, xe_in = sem("idx_ready"), [sem("xe_in0"), sem("xe_in1")]
        xeT_ps, xeT_hi_s, xeT_ready, h1_ps, h3_ps, h1_ready, h_ready = (
            sem("xeT_ps"), sem("xeT_hi_s"), sem("xeT_ready"), sem("h1_ps"), sem("h3_ps"), sem("h1_ready"), sem("h_ready"))
        hT_ps, hT_hi_s, hT_ready, d_ps, ob_ready = sem("hT_ps"), sem("hT_hi_s"), sem("hT_ready"), sem("d_ps"), sem("ob_ready")
        ob_out = [sem("ob_out0"), sem("ob_out1")]
        gb_in, gb_used = [sem(f"gb_in{n}") for n in range(GB)], sem("gb_used")

        steps = [0]

        def mm3(out_ap, lh, ll, rh, rl, first=True, last=True):
            nc.tensor.matmul(out_ap, lh, rh, start=first, stop=False)
            nc.tensor.matmul(out_ap, lh, rl, start=False, stop=False)
            return nc.tensor.matmul(out_ap, ll, rh, start=False, stop=last)

        def layernorm_dve(e, n, xn):
            def step():
                e.wait_ge(dve_step, steps[0])
            for t in range(TT):
                e.bn_stats(ln_stat[:, t, :], x[:, t, :]).then_inc(dve_step, 1)
            steps[0] += TT
            step()
            for t in range(TT):
                e.bn_aggr(ln_mv[:, t, :], ln_stat[:, t, :]).then_inc(ln_var_ready, 1)
            e.wait_ge(ln_std_ready, n + 1)
            e.reciprocal(ln_rstd[:, :], ln_std[:, :]).then_inc(dve_step, 1)
            steps[0] += 1
            step()
            for t in range(TT):
                e.tensor_scalar(xn[:, t, :], x[:, t, :], ln_mv[:, t, 0:1], ln_rstd[:, t:t + 1],
                                ALU.subtract, ALU.mult).then_inc(xn_ready, 1)

        def layernorm_pe(e, n, xn):
            for t in range(TT):
                e.wait_ge(xn_ready, TT * n + t + 1)
                for c in range(DC):
                    last = e.transpose(ps[:, t, c * P:(c + 1) * P], xn[:, t, c * P:(c + 1) * P], ident[:, :])
                last.then_inc(xT_ps, 1)

        def layernorm_act(e, n):
            e.wait_ge(ln_var_ready, TT * (n + 1))
            e.activation(ln_std[:, :], ln_mv[:, :, 1], ACT.Sqrt, bias=eps[:, 0:1]).then_inc(ln_std_ready, 1)
            for t in range(TT):
                e.wait_ge(xT_ps, TT * n + t + 1)
                e.activation(xT_hi[:, :, t * P:(t + 1) * P], ps[:, t, :].rearrange("p (c n) -> p c n", c=DC),
                             ACT.Copy).then_inc(xT_hi_s, 1)

        def layernorm_split_dve(e, n):
            for t in range(TT):
                e.wait_ge(xT_hi_s, TT * n + t + 1)
                tk = slice(t * P, (t + 1) * P)
                e.tensor_tensor(xT_lo[:, :, tk], ps[:, t, :].rearrange("p (c n) -> p c n", c=DC),
                                xT_hi[:, :, tk], ALU.subtract).then_inc(xT_ready, 1)

        def wo_load(e, n, W):
            Wr = W.rearrange("(h p) n -> h p n", p=P)
            for k in range(2):
                if n:
                    e.wait_ge(wo_ready, H * n + k - 1)
                e.dma_start(wo_raw[:, k, :], Wr[k]).then_inc(wo_in[k], 16)
            with e.Fori(1, HP) as i:
                for k in range(2):
                    e.wait_ge(wo_ready, i * 2 + (H * n + k - 1))
                    e.dma_start(wo_raw[:, k:k + 1, :], Wr[bass.ds(i * 2 + k, 1)].rearrange("h p n -> p h n"))\
                        .then_inc(wo_in[k], 16)

        def wo_act(e, n, prefetch):
            def head(i, k, slot_waits=True):
                e.wait_ge(wo_in[k], i * 16 + (HP * n + 1) * 16)
                if slot_waits:
                    e.wait_ge(wo_mm, i * 2 + (H * n + k - 1))
                e.activation(wo_h[:, k, :], wo_raw[:, k, :], ACT.Copy)
                e.activation(ao_h[:, k:k + 1, :], aoT[:, bass.ds(i * 2 + k, 1), :], ACT.Copy).then_inc(wo_hi_s, 1)
            e.wait_ge(ao_ready, H * (n + 1))
            prefetch(e)
            head(0, 0, n > 0)
            head(0, 1, n > 0)
            with e.Fori(1, HP) as i:
                head(i, 0)
                head(i, 1)

        def wo_dve(e, n):
            with e.Fori(0, HP) as i:
                for k in range(2):
                    e.wait_ge(wo_hi_s, i * 2 + (H * n + k + 1))
                    e.tensor_tensor(ao_l[:, k:k + 1, :], aoT[:, bass.ds(i * 2 + k, 1), :], ao_h[:, k:k + 1, :],
                                    ALU.subtract).then_inc(ao_split, 1)

        def wo_pool(e, n):
            with e.Fori(0, HP) as i:
                for k in range(2):
                    e.wait_ge(wo_hi_s, i * 2 + (H * n + k + 1))
                    e.tensor_tensor(wo_l[:, k, :], wo_raw[:, k, :], wo_h[:, k, :], ALU.subtract).then_inc(wo_ready, 1)

        def wo_pe(e, n):
            def pair(i, first=False, last=False):
                for k in range(2):
                    e.wait_ge(ao_split, i * 2 + (H * n + k + 1))
                    e.wait_ge(wo_ready, i * 2 + (H * n + k + 1))
                    for t in range(TT):
                        tk = slice(t * P, (t + 1) * P)
                        m = mm3(ps[:, t, :], ao_h[:, k, tk], ao_l[:, k, tk], wo_h[:, k, :], wo_l[:, k, :],
                                first and k == 0, last and k == 1)
                        if last and k == 1:
                            m.then_inc(y_ps, 1)
                    if not (last and k == 1):
                        m.then_inc(wo_mm, 1)
            pair(0, first=True)
            with e.Fori(1, HP - 1) as i:
                pair(i)
            pair(HP - 1, last=True)
            e.wait_ge(y_ps, TT * (n + 1))
            e.sem_inc(wo_mm, 1)

        kvb = lambda b: slice(b * SKV, (b + 1) * SKV)
        hcol = lambda k: slice(k * P, (k + 1) * P)

        def xa_act_weights(e, p):
            e.wait_ge(wq_in, p * 16 + 16)
            e.activation(wq_h[:, :, :], wq_raw[:, :, :], ACT.Copy).then_inc(wq_hi_s, 1)
            e.wait_ge(wkT_in, p * 16 + 16)
            e.activation(wkT_h[:, :, :], wkT_raw[:, :, :], ACT.Copy).then_inc(wkT_hi_s, 1)

        def xa_act_wv(e, i):
            e.wait_ge(wv_in, i * 16 + 16)
            e.activation(wv_h[:, :, :], wv_raw[:, :, :], ACT.Copy).then_inc(wv_hi_s, 1)

        def xa_act_q(e, p):
            for k in range(2):
                e.wait_ge(q_ps, p * 2 + (k + 1))
                e.activation(sq[:, k, :], ps[:, k, :], ACT.Square, scale=RSD).then_inc(sq_ready, 1)
                e.activation(qg[:, k, :], ps[:, k, :], ACT.Copy, scale=gqk[:, 2:3]).then_inc(qg_ready, 1)

        def xa_act_qn(e, p, k):
            e.wait_ge(qn_ready, p * 2 + (k + 1))
            e.activation(qn_h[:, k, :], qg[:, k, :], ACT.Copy).then_inc(qn_hi_s, 1)

        def xa_act_qp(e, p):
            for k in range(2):
                for c in range(CC):
                    e.wait_ge(qp_ps, p * 4 + (2 * k + c + 1))
                    e.activation(qpT[:, c, :, k, :], ps[:, 2 * k + c, :].rearrange("p (b q) -> p b q", b=B),
                                 ACT.Copy).then_inc(qp_ready, 1)

        def xa_act_exp(e, i, j):
            e.wait_ge(nmx_ready, i * 4 + (j + 1))
            for b in (2 * j, 2 * j + 1):
                last = e.activation(sc[:, b, :], sc[:, b, :], ACT.Exp, bias=nmx[:, b:b + 1],
                                    accum_out=sm[:, b:b + 1])
            last.then_inc(p_ready, 1)

        def xa_act_pT(e, i, j):
            e.wait_ge(pT_ps, i * 4 + (j + 1))
            e.activation(pT[:, 2 * j:2 * j + 2, :, :].rearrange("p b k n -> p (b k n)"), ps[:, 6 + j % 2, :],
                         ACT.Copy).then_inc(pT_ready, 1)

        def xa_act_u(e, i, j):
            e.wait_ge(u_ps, i * 4 + (j + 1))
            e.activation(u_h[:, :, 2 * j:2 * j + 2, :, :].rearrange("p c b k q -> p c (b k q)"),
                         ps[:, 4 + j % 2, :].rearrange("p (c n) -> p c n", c=CC), ACT.Copy).then_inc(u_hi_s, 1)

        def xa_pool_weights(e, p):
            e.wait_ge(wq_hi_s, p + 1)
            e.tensor_tensor(wq_l[:, :, :], wq_raw[:, :, :], wq_h[:, :, :], ALU.subtract).then_inc(wq_ready, 1)
            e.wait_ge(wkT_hi_s, p + 1)
            e.tensor_tensor(wkT_l[:, :, :], wkT_raw[:, :, :], wkT_h[:, :, :], ALU.subtract).then_inc(wkT_ready, 1)

        def xa_pool_wv(e, i):
            e.wait_ge(wv_hi_s, i + 1)
            e.tensor_tensor(wv_l[:, :, :], wv_raw[:, :, :], wv_h[:, :, :], ALU.subtract).then_inc(wv_ready, 1)

        def xa_dve_scores(e, i, j):
            bb = slice(2 * j, 2 * j + 2)
            e.wait_ge(s_ps, i * 4 + (j + 1))
            e.wait_ge(rkB_in[j], i * 32 + 32)
            e.tensor_tensor(sc[:, bb, :], ps[:, 4 + j % 2, :].rearrange("p (b n) -> p b n", b=2), rkB[:, bb, :],
                            ALU.mult).then_inc(s_ready, 1)
            e.wait_ge(s_ready, i * 4 + (j + 1))
            e.tensor_reduce(nmx[:, bb], sc[:, bb, :], AX.X, ALU.max, negate=True).then_inc(nmx_ready, 1)

        def xa_dve_norm(e, i, j):
            bb = slice(2 * j, 2 * j + 2)
            e.wait_ge(p_ready, i * 4 + (j + 1))
            e.reciprocal(rsm[:, bb], sm[:, bb]).then_inc(rsm_ready, 1)
            e.wait_ge(rsm_ready, i * 4 + (j + 1))
            e.tensor_tensor(sc[:, bb, :], sc[:, bb, :], rsm[:, bb].unsqueeze(2).to_broadcast([P, 2, SKV]),
                            ALU.mult).then_inc(pn_ready, 1)

        def xa_act_rms(e, p, k):
            e.wait_ge(ss_ps, p * 2 + (k + 1))
            e.activation(rB[:, k, :], ps[:, 2 + k, :], ACT.Sqrt, bias=eps[:, 0:1]).then_inc(rms_ready, 1)

        def xa_dve_qn(e, p, k):
            e.wait_ge(rms_ready, p * 2 + (k + 1))
            e.reciprocal(rB[:, k, :], rB[:, k, :]).then_inc(rB_ready, 1)
            e.wait_ge(rB_ready, p * 2 + (k + 1))
            e.wait_ge(qg_ready, p * 2 + (k + 1))
            e.tensor_tensor(qg[:, k, :], qg[:, k, :], rB[:, k, :], ALU.mult).then_inc(qn_ready, 1)

        def xa_dve_qsplit(e, p, k):
            e.wait_ge(qn_hi_s, p * 2 + (k + 1))
            e.tensor_tensor(qn_l[:, k, :], qg[:, k, :], qn_h[:, k, :], ALU.subtract).then_inc(qn_split, 1)

        def xa_dve_u(e, i, j):
            e.wait_ge(u_hi_s, i * 4 + (j + 1))
            r = lambda a: a[:, :, 2 * j:2 * j + 2, :, :].rearrange("p c b k q -> p c (b k q)")
            e.tensor_tensor(r(u_l), ps[:, 4 + j % 2, :].rearrange("p (c n) -> p c n", c=CC), r(u_h),
                            ALU.subtract).then_inc(u_ready, 1)

        def xa_dve_ao(e, i):
            for k in range(2):
                e.wait_ge(ao_ps, i * 2 + (k + 1))
                e.tensor_copy(aoT[:, bass.ds(i * 2 + k, 1), :], ps[:, 6 + k:7 + k, :]).then_inc(ao_ready, 1)

        def xa_pe_q(e, p, k):
            e.wait_ge(wq_ready, p + 1)
            for c in range(DC):
                m = mm3(ps[:, k, :], wq_h[:, c, hcol(k)], wq_l[:, c, hcol(k)], xT_hi[:, c, :], xT_lo[:, c, :],
                        c == 0, c == DC - 1)
            m.then_inc(q_ps, 1)

        def xa_pe_ss(e, p, k):
            e.wait_ge(sq_ready, p * 2 + (k + 1))
            e.matmul(ps[:, 2 + k, :], ones[:, :], sq[:, k, :], start=True, stop=True).then_inc(ss_ps, 1)

        def xa_pe_qp(e, p):
            e.wait_ge(wkT_ready, p + 1)
            e.wait_ge(qg_ready, p * 2 + 2)
            for k in range(2):
                e.wait_ge(qn_split, p * 2 + (k + 1))
                for c in range(CC):
                    mm3(ps[:, 2 * k + c, :], wkT_h[:, k, hcol(c)], wkT_l[:, k, hcol(c)], qn_h[:, k, :],
                        qn_l[:, k, :]).then_inc(qp_ps, 1)

        def xa_pe_scores(e, i, j):
            if j == 0:
                e.wait_ge(qp_ready, i * 4 + 4)
            if j >= 2:
                e.wait_ge(s_ready, i * 4 + (j - 1))
            for n, b in enumerate((2 * j, 2 * j + 1)):
                for c in range(CC):
                    m = e.matmul(ps[:, 4 + j % 2, n * SKV:(n + 1) * SKV],
                                 qpT[:, c, b, :, :].rearrange("p k q -> p (k q)"), ctxT[:, c, kvb(b)],
                                 start=c == 0, stop=c == CC - 1)
            m.then_inc(s_ps, 1)

        def xa_pe_pT(e, i, j):
            e.wait_ge(pn_ready, i * 4 + (j + 1))
            if j >= 2:
                e.wait_ge(pT_ready, i * 4 + (j - 1))
            for n, b in enumerate((2 * j, 2 * j + 1)):
                for t in range(KPB):
                    at = (n * KPB + t) * P
                    m = e.transpose(ps[:, 6 + j % 2, at:at + P], sc[:, b, t * P:(t + 1) * P], ident[:, :])
            m.then_inc(pT_ps, 1)

        def xa_pe_u(e, i, j):
            e.wait_ge(pT_ready, i * 4 + (j + 1))
            if j < 2:
                e.wait_ge(s_ready, i * 4 + (j + 3))
            else:
                e.wait_ge(u_ready, i * 4 + (j - 1))
            for c in range(CC):
                for n, b in enumerate((2 * j, 2 * j + 1)):
                    at = (c * 2 + n) * P
                    for t in range(KPB):
                        m = e.matmul(ps[:, 4 + j % 2, at:at + P], ctx[:, b * KPB + t, hcol(c)], pT[:, b, t, :],
                                     start=t == 0, stop=t == KPB - 1)
            m.then_inc(u_ps, 1)

        def xa_pe_ao(e, i):
            e.wait_ge(wv_ready, i + 1)
            e.wait_ge(u_ready, i * 4 + 4)
            for k in range(2):
                for c in range(CC):
                    m = mm3(ps[:, 6 + k, :], wv_h[:, c, hcol(k)], wv_l[:, c, hcol(k)],
                            u_h[:, c, :, k, :], u_l[:, c, :, k, :], c == 0, c == CC - 1)
                m.then_inc(ao_ps, 1)

        K_, Q_, V_, G_ = range(4)

        def la_act_split(e, n, p):
            e.wait_ge(lw_in[n], p * 16 + 16)
            e.activation(lw_h[n][:, :, :], lw_raw[n][:, :, :], ACT.Copy).then_inc(lw_hi_s[n], 1)

        def la_pool_split(e, n, p):
            e.wait_ge(lw_hi_s[n], p + 1)
            e.tensor_tensor(lw_l[n][:, :, :], lw_raw[n][:, :, :], lw_h[n][:, :, :], ALU.subtract).then_inc(lw_ready[n], 1)

        def la_proj(e, n, k, bank):
            for c in range(DC):
                m = mm3(ps[:, bank, :], lw_h[n][:, c, hcol(k)], lw_l[n][:, c, hcol(k)], xT_hi[:, c, :], xT_lo[:, c, :],
                        c == 0, c == DC - 1)
            return m

        def la_pe(e, i):
            for n in (K_, Q_):
                e.wait_ge(lw_ready[n], i + 1)
                for k in range(2):
                    la_proj(e, n, k, 2 * n + k).then_inc(kq_ps, 1)
            e.wait_ge(ao_ready, i * 2 + H)
            for n in range(4):
                e.wait_ge(kq_sq_ready, i * 4 + (n + 1))
                e.matmul(ps[:, 4 + n, :], ones[:, :], kq_sq[:, n, :], start=True, stop=True).then_inc(kq_ss_ps, 1)
            e.wait_ge(lw_ready[V_], i + 1)
            for t in range(TT):
                tk = slice(t * P, (t + 1) * P)
                for c in range(DC):
                    m = mm3(ps[:, t // 2, (t % 2) * 2 * P:(t % 2 + 1) * 2 * P], xT_hi[:, c, tk], xT_lo[:, c, tk],
                            lw_h[V_][:, c, :], lw_l[V_][:, c, :], c == 0, c == DC - 1)
                if t % 2:
                    m.then_inc(v_ps, 1)
            e.wait_ge(lw_ready[G_], i + 1)
            la_proj(e, G_, 0, 2).then_inc(og_ps, 1)
            e.wait_ge(kq_n, i * 4 + 4)
            for k in range(2):
                for t in range(TT):
                    tk = slice(t * P, (t + 1) * P)
                    m = e.matmul(ps[:, 3 + k, tk], kq[:, k, tk], kq[:, 2 + k, tk], start=True, stop=True)
                m.then_inc(at_ps, 1)
            la_proj(e, G_, 1, 5).then_inc(og_ps, 1)
            e.wait_ge(v_ready, i * 2 + 2)
            for k in range(2):
                e.wait_ge(at_ready, i * 2 + (k + 1))
                for t in range(TT):
                    tk = slice(t * P, (t + 1) * P)
                    m = e.matmul(ps[:, 6 + k, tk], vt[:, t, hcol(k)], at[:, k, tk], start=True, stop=True)
                m.then_inc(o_ps, 1)
            e.wait_ge(sg_ready, i * 2 + 2)

        def la_act(e, i, more):
            for n in range(4):
                e.wait_ge(kq_ps, i * 4 + (n + 1))
                bias = kq_b[:, n // 2, bass.ds(i * 2 + n % 2, 1)]
                e.activation(kq[:, n, :], ps[:, n, :], ACT.Identity, bias=bias, scale=RSD).then_inc(kq_ready, 1)
                e.activation(kq_sq[:, n, :], ps[:, n, :], ACT.Square, bias=bias, scale=RSD).then_inc(kq_sq_ready, 1)
            for n in range(4):
                e.wait_ge(kq_ss_ps, i * 4 + (n + 1))
                e.activation(kq_r[:, n, :], ps[:, 4 + n, :], ACT.Sqrt).then_inc(kq_norm, 1)
            if more:
                la_act_split(e, K_, i + 1)
                la_act_split(e, Q_, i + 1)
            e.wait_ge(og_ps, i * 2 + 1)
            e.activation(sg[:, 0, :], ps[:, 2, :], ACT.Silu).then_inc(sg_ready, 1)
            if more:
                e.wait_ge(v_ps, i * 2 + 2)
                la_act_split(e, V_, i + 1)
            e.wait_ge(og_ps, i * 2 + 2)
            e.activation(sg[:, 1, :], ps[:, 5, :], ACT.Silu).then_inc(sg_ready, 1)
            if more:
                la_act_split(e, G_, i + 1)

        def la_dve(e, i):
            for n in range(4):
                e.wait_ge(kq_norm, i * 4 + (n + 1))
                e.reciprocal(kq_r[:, n, :], kq_r[:, n, :]).then_inc(kq_recip, 1)
                e.wait_ge(kq_recip, i * 4 + (n + 1))
                e.scalar_tensor_tensor(kq[:, n, :], kq_r[:, n, :], 1.0 / L2_EPS, kq[:, n, :], ALU.min, ALU.mult)\
                    .then_inc(kq_n, 1)
            for g in range(2):
                tt = slice(2 * g, 2 * g + 2)
                e.wait_ge(v_ps, i * 2 + (g + 1))
                e.tensor_tensor(vt[:, tt, :], ps[:, g, :].rearrange("p (t n) -> p t n", t=2),
                                v_bias[:, bass.ds(i * 2 * P, 2 * P)].unsqueeze(1).to_broadcast([P, 2, 2 * P]),
                                ALU.add).then_inc(v_biased, 1)
                e.wait_ge(v_biased, i * 2 + (g + 1))
                for t in (2 * g, 2 * g + 1):
                    v = vt[:, t, :].rearrange("p (h n) -> p h n", h=2)
                    m = e.tensor_tensor(v, v, beta[:, t, bass.ds(i * 2, 2)].unsqueeze(2).to_broadcast([P, 2, P]), ALU.mult)
                m.then_inc(v_ready, 1)
            for k in range(2):
                e.wait_ge(at_ps, i * 2 + (k + 1))
                e.tensor_tensor(at[:, k, :].rearrange("p (t n) -> p t n", t=TT),
                                ps[:, 3 + k, :].rearrange("p (t n) -> p t n", t=TT),
                                mask[:, :].unsqueeze(1).to_broadcast([P, TT, P]), ALU.mult).then_inc(at_ready, 1)
            for k in range(2):
                e.wait_ge(o_ps, i * 2 + (k + 1))
                e.wait_ge(sg_ready, i * 2 + (k + 1))
                e.tensor_tensor(aoT[:, bass.ds(i * 2 + k, 1), :], ps[:, 6 + k:7 + k, :], sg[:, k:k + 1, :],
                                ALU.mult).then_inc(ao_ready, 1)

        NSH = 2 * TT

        def fcs(c):
            return slice(c * P, c * P + FW[c])

        def ex_up(lh, ll, k):
            for n, s in ((0, h1_ps), (1, h3_ps)):
                f = slice(n * FF, (n + 1) * FF)
                for c in range(DC):
                    m = mm3(ps[:, 2 * n + k, 0:FF], lh(c), ll(c), w13_h[:, k, c, f], w13_l[:, k, c, f],
                            c == 0, c == DC - 1)
                m.then_inc(s, 1)

        def ex_hT(e, k, u):
            e.wait_ge(h_ready, u + 1)
            e.wait_ge(hT_ready, u)
            for c in range(FC):
                m = e.transpose(ps[0:FW[c], 5, c * P:(c + 1) * P], h[:, k, fcs(c)], ident[:, :])
            m.then_inc(hT_ps, 1)

        def ex_down(k, bank, first=True, last=True):
            for c in range(FC):
                r = slice(0, FW[c])
                m = mm3(ps[:, bank, :], hT_h[r, k, c, :], hT_l[r, k, c, :], w2_h[r, k, c, :], w2_l[r, k, c, :],
                        first and c == 0, last and c == FC - 1)
            return m

        def ex_act_w13(e, k, n):
            e.wait_ge(w13_in[k], n * 32)
            e.activation(w13_h[:, k, :, :], w13_raw[:, k, :, :], ACT.Copy).then_inc(w13_hi_s, 1)

        def ex_act_w2(e, k, n):
            e.wait_ge(w2_in[k], n * 32)
            e.activation(w2_h[:, k, :, :], w2_raw[:, k, :, :], ACT.Copy).then_inc(w2_hi_s, 1)

        def ex_dve_w13(e, k, n):
            e.wait_ge(w13_hi_s, n)
            e.tensor_tensor(w13_l[:, k, :, :], w13_raw[:, k, :, :], w13_h[:, k, :, :], ALU.subtract).then_inc(w13_ready, 1)

        def ex_pool_w2(e, k, n):
            e.wait_ge(w2_hi_s, n)
            e.tensor_tensor(w2_l[:, k, :, :], w2_raw[:, k, :, :], w2_h[:, k, :, :], ALU.subtract).then_inc(w2_ready, 1)

        def ex_act_silu(e, k, u):
            e.wait_ge(h1_ps, u + 1)
            e.activation(h1[:, k, :], ps[:, k, 0:FF], ACT.Silu).then_inc(h1_ready, 1)

        def ex_dve_h(e, k, u):
            e.wait_ge(h1_ready, u + 1)
            e.wait_ge(h3_ps, u + 1)
            e.tensor_tensor(h[:, k, :], h1[:, k, :], ps[:, 2 + k, 0:FF], ALU.mult).then_inc(h_ready, 1)

        def ex_act_hT(e, k, u):
            e.wait_ge(hT_ps, u + 1)
            for c in range(FC):
                r = slice(0, FW[c])
                last = e.activation(hT_h[r, k, c, :], ps[r, 5, c * P:(c + 1) * P], ACT.Copy)
            last.then_inc(hT_hi_s, 1)

        def ex_dve_hT(e, k, u):
            e.wait_ge(hT_hi_s, u + 1)
            for c in range(FC):
                r = slice(0, FW[c])
                last = e.tensor_tensor(hT_l[r, k, c, :], ps[r, 5, c * P:(c + 1) * P], hT_h[r, k, c, :], ALU.subtract)
            last.then_inc(hT_ready, 1)

        def ex_act_xT(e, m, k):
            e.wait_ge(xeT_ps, m + 1)
            e.activation(xeT_h[:, k, :, :].rearrange("p c n -> p (c n)"), ps[:, 4, :], ACT.Copy).then_inc(xeT_hi_s, 1)

        def ex_dve_xT(e, m, k):
            e.wait_ge(xeT_hi_s, m + 1)
            e.tensor_tensor(xeT_l[:, k, :, :].rearrange("p c n -> p (c n)"), ps[:, 4, :],
                            xeT_h[:, k, :, :].rearrange("p c n -> p (c n)"), ALU.subtract).then_inc(xeT_ready, 1)

        def ex_pe_xT(e, k, n):
            e.wait_ge(xe_in[k], n * 16)
            for c in range(DC):
                last = e.transpose(ps[:, 4, c * P:(c + 1) * P], xe[:, k, c * P:(c + 1) * P], ident[:, :])
            last.then_inc(xeT_ps, 1)

        def ex_pe_down(e, m, k):
            e.wait_ge(hT_ready, m + (NSH + 1))
            e.wait_ge(w2_ready, m + 3)
            ex_down(k, 6 + k).then_inc(d_ps, 1)

        def ex_pe(e, i, k, peeled=False):
            m = i * 2 + k
            e.wait_ge(w13_ready, m + 3)
            e.wait_ge(xeT_ready, m + 1)
            e.wait_ge(h_ready, m + (NSH - 1))
            ex_up(lambda c: xeT_h[:, k, c, :], lambda c: xeT_l[:, k, c, :], k)
            ex_pe_xT(e, 1 - k, i + (k + 1))
            if not (peeled and k == 0):
                ex_pe_down(e, m - 1, 1 - k)
            ex_hT(e, k, m + NSH)

        def ex_act(e, i, k, peeled=False):
            m = i * 2 + k
            e.wait_ge(h3_ps, m + NSH)
            ex_act_w13(e, 1 - k, i + (k + 2))
            if not peeled:
                e.wait_ge(d_ps, m - 1)
            ex_act_w2(e, k, i + 2)
            ex_act_silu(e, k, m + NSH)
            ex_act_xT(e, m + 1, 1 - k)
            ex_act_hT(e, k, m + NSH)

        def ex_dve_ob(e, m, k, n):
            e.wait_ge(d_ps, m + 1)
            if n is not None:
                e.wait_ge(ob_out[k], n * 16)
            e.tensor_copy(ob[:, k, :], ps[:, 6 + k, :]).then_inc(ob_ready, 1)

        def ex_dve(e, i, k, peeled=False, slot_free=False):
            m = i * 2 + k
            ex_dve_w13(e, 1 - k, m + 4)
            ex_dve_h(e, k, m + NSH)
            ex_dve_xT(e, m + 1, 1 - k)
            if not (peeled and k == 0):
                ex_dve_ob(e, m - 1, 1 - k, None if peeled or slot_free else i + (k - 1))
            ex_dve_hT(e, k, m + NSH)

        def ex_gather_rows(e, m, k):
            e.tensor_copy(idx_col[:, k:k + 1], tl[:, bass.ds(m, 1)]).then_inc(idx_ready, 1)
            e.wait_ge(idx_ready, m + 1)

        def ex_gather(e, k):
            e.indirect_dma_start(xe[:, k, :], None, xn_dram.ap(), bass.IndirectOffsetOnAxis(ap=idx_col[:, k:k + 1], axis=0))\
                .then_inc(xe_in[k], 16)

        def ex_pool(e, i, k):
            m = i * 2 + k
            e.wait_ge(xeT_ps, m + 1)
            ex_gather_rows(e, m + 2, k)
            ex_pool_w2(e, k, m + 3)
            ex_gather(e, k)

        def load_w13(e, k, w1_ap, w3_ap):
            e.dma_start(w13_raw[:, k, :, 0:FF], w1_ap).then_inc(w13_in[k], 16)
            e.dma_start(w13_raw[:, k, :, FF:2 * FF], w3_ap).then_inc(w13_in[k], 16)

        def load_w2(e, k, whole_ap, rest_ap):
            e.dma_start(w2_raw[:, k, 0:FC - 1, :], whole_ap).then_inc(w2_in[k], 16)
            e.dma_start(w2_raw[0:FW[-1], k, FC - 1, :], rest_ap).then_inc(w2_in[k], 16)

        w1_r = w1.rearrange("e (c p) f -> e p c f", p=P)
        w3_r = w3.rearrange("e (c p) f -> e p c f", p=P)
        w2_r = w2[:, 0:(FC - 1) * P, :].rearrange("e (c p) d -> e p c d", p=P)
        w2_t = w2[:, (FC - 1) * P:FF, :]

        def ex_load(e, m, k):
            ex = e.value_load(lst[0:1, bass.ds(m, 1)], min_val=0, max_val=E - 1)
            e.wait_ge(w13_ready, m + 1)
            load_w13(e, k, w1_r[bass.ds(ex, 1)].rearrange("e p c f -> p (e c) f"),
                     w3_r[bass.ds(ex, 1)].rearrange("e p c f -> p (e c) f"))
            e.wait_ge(w2_ready, m + 1)
            load_w2(e, k, w2_r[bass.ds(ex, 1)].rearrange("e p c d -> p (e c) d"),
                    w2_t[bass.ds(ex, 1)].rearrange("e p d -> p (e d)"))

        def ex_store(e, m, k):
            e.wait_ge(ob_ready, m + 1)
            e.dma_start(ob_dram.ap().rearrange("(n p) d -> n p d", p=P)[bass.ds(m, 1)].rearrange("n p d -> p (n d)"),
                        ob[:, k, :]).then_inc(ob_out[k], 16)

        def ex_sp(e, i, k, peeled=False):
            m = i * 2 + k
            ex_load(e, m + 2, k)
            if not (peeled and k == 0):
                ex_store(e, m - 1, 1 - k)

        def last_turn(e):
            e.wait_ge(small_dve, DV_LISTS)
            return e.value_load(lst[0:1, ML:ML + 1], min_val=T * TOP_K // P // 2 - 1, max_val=MI // 2 - 1)

        rsm_ready, rB_ready, rms_ready = sem("rsm_ready"), sem("rB_ready"), sem("rms_ready")
        ln_var_ready, ln_std_ready, rk_sqrt = sem("ln_var_ready"), sem("ln_std_ready"), sem("rk_sqrt")

        ob_cleared, ob_stored = sem("ob_cleared"), sem("ob_stored")
        OZ = MI // (HP - 1)
        ob_rows = ob_dram.ap().rearrange("(n p) d -> p n d", p=P)
        lw_r = [w.rearrange("(c p) (h n) -> h p c n", p=P, n=2 * P) for w in (kwT, qwT, vwT, ogwT)]

        block = stack.enter_context(nc.Block())

        @block.sync
        def _(e):
            e.dma_start(x[:, :, :], x_in.rearrange("(t p) d -> p t d", p=P)).then_inc(x_in_s, 16)
            for g in range(4):
                kv = slice(g * G4, (g + 1) * G4)
                e.dma_start(ctxT[:, :, kv], ctxT_in.rearrange("(c p) n -> p c n", p=P)[:, :, kv]).then_inc(ctxT_in_s, 16)
                e.wait_ge(ctxT_in_s, 16 * (g + 1))
                e.dma_start(wk_raw[:, :, kv], Wk.rearrange("(c p) n -> p c n", p=P)[:, :, kv]).then_inc(wk_in, 16)
                e.wait_ge(wk_in, 16 * (g + 1))
            e.dma_start(gqk[:, 0:1], gq.rearrange("(p a) -> p a", a=1)).then_inc(g_in_s, 16)
            e.dma_start(gqk[:, 1:2], gk.rearrange("(p a) -> p a", a=1)).then_inc(g_in_s, 16)
            e.dma_start(ctx[:, :, :], ctx_in.rearrange("(t p) c -> p t c", p=P)).then_inc(ctx_in_s, 16)
            e.wait_ge(rkT_ready, 2)
            for n in range(2):
                e.dma_start(rk_dram.ap().rearrange("h (n t p) -> n t h p", n=2, p=P)[n], rkT[:, n, :]).then_inc(scratch_io, 16)
            e.wait_ge(scratch_io, IO_RK)

            wq_r = Wq.rearrange("(c p) (h n) -> h p c n", p=P, n=2 * P)
            wkT_r = WkT.rearrange("(h k p) c -> h p k c", k=2, p=P)
            wv_r = Wv.rearrange("(c p) (h n) -> h p c n", p=P, n=2 * P)
            rk_r = rk_dram.ap().rearrange("(h k) (j n) -> h k j n", k=2, j=JB)

            def rk_load(p, j):
                for k in range(2):
                    src = rk_r[bass.ds(p, 1), k, j, :]
                    e.dma_start(rkB[k * SQ:(k + 1) * SQ, 2 * j:2 * j + 2, :].rearrange("p b n -> p (b n)"),
                                src.to_broadcast([SQ, 2 * SKV])).then_inc(rkB_in[j], 16)

            def load(p):
                e.dma_start(wq_raw[:, :, :], wq_r[bass.ds(p, 1)].rearrange("h p c n -> p (h c) n")).then_inc(wq_in, 16)

            e.dma_start(wq_raw[:, :, :], wq_r[0]).then_inc(wq_in, 16)
            e.dma_start(wkT_raw[:, :, :], wkT_r[0]).then_inc(wkT_in, 16)
            e.dma_start(wv_raw[:, :, :], wv_r[0]).then_inc(wv_in, 16)
            for j in range(JB):
                rk_load(0, j)
            with e.Fori(1, HP) as p:
                e.wait_ge(wq_ready, p)
                load(p)
                e.wait_ge(wkT_ready, p)
                e.dma_start(wkT_raw[:, :, :], wkT_r[bass.ds(p, 1)].rearrange("h p k c -> p (h k) c")).then_inc(wkT_in, 16)
                e.wait_ge(wv_ready, p)
                e.dma_start(wv_raw[:, :, :], wv_r[bass.ds(p, 1)].rearrange("h p c n -> p (h c) n")).then_inc(wv_in, 16)
                e.dma_start(ob_rows[:, bass.ds(p * OZ - OZ, OZ), :], zeros[:, :].unsqueeze(1).to_broadcast([P, OZ, D]))\
                    .then_inc(ob_cleared, 16)
                for j in range(JB):
                    e.wait_ge(s_ready, p * 4 + (j - 3))
                    rk_load(p, j)
            wo_load(e, 0, Wo)
            with e.Fori(1, HP) as p:
                for n in range(4):
                    e.wait_ge(lw_ready[n], p)
                    e.dma_start(lw_raw[n][:, :, :], lw_r[n][bass.ds(p, 1)].rearrange("h p c n -> p (h c) n"))\
                        .then_inc(lw_in[n], 16)
            wo_load(e, 1, owT)
            e.wait_ge(xn_ready, 3 * TT)
            e.dma_start(xn_dram.ap().rearrange("(t p) d -> p t d", p=P), xn_c[:, :, :]).then_inc(scratch_io, 16)
            e.dma_start(tl_dram.ap().rearrange("(n s) a -> n (s a)", s=P), zeros[0:ML, 0:P]).then_inc(scratch_io, 16)
            e.wait_ge(tl_scattered, 16 * TT * TOP_K)
            e.dma_start(tl_rows[0:ML, :], tl_dram.ap().rearrange("(n s) a -> n (s a)", s=P)).then_inc(scratch_io, 16)
            last_i = last_turn(e)
            ex_load(e, 0, 0)
            ex_load(e, 1, 1)
            e.wait_ge(ob_cleared, 16 * (HP - 1))
            ex_sp(e, 0, 0, True)
            ex_sp(e, 0, 1, True)
            with e.Fori(1, last_i + 1) as i:
                ex_sp(e, i, 0)
                ex_sp(e, i, 1)
            ex_store(e, last_i * 2 + 1, 1)
            e.wait_ge(ob_out[0], last_i * 16 + 16)
            e.wait_ge(ob_out[1], last_i * 16 + 16)
            e.sem_inc(ob_stored, 1)
            for t in range(TT):
                e.wait_ge(gb_used, TOP_K * (t + 1))
                e.dma_start(out[t * P:(t + 1) * P, :], x[:, t, :]).then_inc(out_done, 16)
            e.wait_ge(out_done, 16 * TT)

        @block.gpsimd
        def _(e):
            e.memset(ident[:, :], 0.0).then_inc(consts, 1)
            e.memset(ones[:, :], 1.0).then_inc(consts, 1)
            e.memset(zeros[:, :], 0.0).then_inc(consts, 1)
            e.memset(eps[:, :], LN_EPS).then_inc(consts, 1)
            e.wait_ge(consts, 4)
            e.affine_select(out=ident[:, :], in_=ident[:, :], compare_op=ALU.not_equal, fill=1.0, base=0,
                            pattern=[[-1, P]], channel_multiplier=1).then_inc(consts, 1)
            for g in range(4):
                kv = slice(g * G4, (g + 1) * G4)
                e.wait_ge(wk_hi_s, g + 1)
                e.tensor_tensor(wk_l[:, :, kv], wk_raw[:, :, kv], wk_h[:, :, kv], ALU.subtract).then_inc(wk_ready, 1)
            xa_pool_weights(e, 0)
            with e.Fori(0, HP - 1) as i:
                xa_pool_weights(e, i + 1)
                xa_pool_wv(e, i)
            xa_pool_wv(e, HP - 1)
            wo_pool(e, 0)

            e.wait_ge(ao_ready, H)
            e.memset(mask[:, :], 1.0).then_inc(consts, 1)
            e.wait_ge(consts, 6)
            e.affine_select(out=mask[:, :], in_=mask[:, :], compare_op=ALU.is_ge, fill=0.0, base=0,
                            pattern=[[1, P]], channel_multiplier=-1).then_inc(consts, 1)
            e.wait_ge(consts, 7)
            e.affine_select(out=mask[:, SQ:P], in_=mask[:, SQ:P], compare_op=ALU.is_ge, fill=0.0, base=-SQ,
                            pattern=[[0, P - SQ]], channel_multiplier=1).then_inc(mask_ready, 1)
            e.wait_ge(small_hi, SP_BETA)
            e.tensor_tensor(bw_l[:, :, :], bw_raw[:, :, :], bw_h[:, :, :], ALU.subtract).then_inc(small_lo, 1)
            for n in range(4):
                la_pool_split(e, n, 0)
            with e.Fori(0, HP - 1) as i:
                for n in range(4):
                    la_pool_split(e, n, i + 1)
            e.wait_ge(ao_ready, 2 * H)
            e.memset(w2_raw[FW[-1]:P, :, FC - 1, :], 0.0).then_inc(consts, 1)
            e.wait_ge(consts, 8)
            wo_pool(e, 1)

            e.wait_ge(x_ready, 2 * TT)
            e.memset(below[:, :], 1.0).then_inc(pool_consts, 1)
            e.iota(iota_e[:, :], [[1, ML]], base=0, channel_multiplier=0, allow_small_or_imprecise_dtypes=True).then_inc(pool_consts, 1)
            e.iota(part_i[:, 0:1], [[0, 1]], base=0, channel_multiplier=1).then_inc(pool_consts, 1)
            e.iota(tok_id[:, :], [[P, TT]], base=0, channel_multiplier=1, allow_small_or_imprecise_dtypes=True).then_inc(pool_consts, 1)
            e.memset(strict[:, :], 1.0).then_inc(pool_consts, 1)
            e.wait_ge(pool_consts, 5)
            e.affine_select(out=below[:, :], in_=below[:, :], compare_op=ALU.is_gt, fill=0.0, base=0,
                            pattern=[[CT, E]], channel_multiplier=-1).then_inc(pool_consts, 1)
            e.affine_select(out=strict[:, :], in_=strict[:, :], compare_op=ALU.is_gt, fill=0.0, base=0,
                            pattern=[[1, P]], channel_multiplier=-1).then_inc(pool_consts, 1)
            e.wait_ge(small_hi, SP_ROUTER)
            e.tensor_tensor(gw_l[:, :, :], gw_raw[:, :, :], gw_h[:, :, :], ALU.subtract).then_inc(small_lo, 1)
            ex_pool_w2(e, 0, 1)
            ex_pool_w2(e, 1, 2)
            e.wait_ge(scratch_io, IO_CLEARED)
            e.wait_ge(small_dve, DV_SLOTS)
            for t in range(TT):
                for k in range(TOP_K):
                    e.indirect_dma_start(tl_dram.ap(), bass.IndirectOffsetOnAxis(ap=slot_i[:, t, k:k + 1], axis=0),
                                         tok_id[:, t:t + 1], None).then_inc(tl_scattered, 16)
            last_i = last_turn(e)
            e.wait_ge(scratch_io, IO_CLEARED)
            e.wait_ge(small_dve, DV_TOKENS)
            for k in range(2):
                ex_gather_rows(e, k, k)
                ex_gather(e, k)
            ex_pool(e, 0, 0)
            ex_pool(e, 0, 1)
            with e.Fori(1, last_i + 1) as i:
                ex_pool(e, i, 0)
                ex_pool(e, i, 1)
            e.wait_ge(ob_stored, 1)
            for t in range(TT):
                for k in range(TOP_K):
                    n = t * TOP_K + k
                    if n >= GB:
                        e.wait_ge(gb_used, n - GB + 1)
                    e.indirect_dma_start(gb[:, n % GB, :], None, ob_dram.ap(),
                                         bass.IndirectOffsetOnAxis(ap=slot_i[:, t, k:k + 1], axis=0)).then_inc(gb_in[n % GB], 16)

        @block.scalar
        def _(e):
            e.wait_ge(consts, 5)
            for g in range(4):
                kv = slice(g * G4, (g + 1) * G4)
                e.wait_ge(ctxT_in_s, 16 * (g + 1))
                e.activation(cT_h[:, :, kv], ctxT[:, :, kv], ACT.Copy).then_inc(cT_hi_s, 1)
                e.wait_ge(wk_in, 16 * (g + 1))
                e.activation(wk_h[:, :, kv], wk_raw[:, :, kv], ACT.Copy).then_inc(wk_hi_s, 1)
                if g == 0:
                    layernorm_act(e, 0)
            with e.Fori(0, 4) as g:
                for t in range(KT):
                    e.wait_ge(k_ps, g * KT + (t + 1))
                    e.wait_ge(sqk_free, g * KT + (t + 3))
                    e.activation(sqk[:, t % 2, :], ps[:, 4 + t % 4, :], ACT.Square, scale=RSD).then_inc(sqk_ready, 1)
            e.wait_ge(small_dve, DV_SSK)
            e.activation(rk_ln[:, :, :], ssk[:, :, :], ACT.Sqrt, bias=eps[:, 0:1]).then_inc(rk_sqrt, 1)
            e.wait_ge(small_ps, PS_RKT)
            for n in range(2):
                e.activation(rkT[:, n, :], ps[:, n, 0:P], ACT.Copy).then_inc(rkT_ready, 1)
            xa_act_weights(e, 0)
            xa_act_q(e, 0)
            xa_act_rms(e, 0, 0)
            xa_act_rms(e, 0, 1)
            xa_act_qn(e, 0, 0)
            xa_act_qn(e, 0, 1)
            xa_act_qp(e, 0)

            def pair(i, more):
                if more:
                    xa_act_weights(e, i + 1)
                xa_act_exp(e, i, 0)
                xa_act_wv(e, i)
                for j in range(1, JB):
                    xa_act_exp(e, i, j)
                if more:
                    xa_act_q(e, i + 1)
                    xa_act_rms(e, i + 1, 0)
                    xa_act_rms(e, i + 1, 1)
                xa_act_pT(e, i, 0)
                xa_act_pT(e, i, 1)
                if more:
                    xa_act_qn(e, i + 1, 0)
                xa_act_u(e, i, 0)
                xa_act_pT(e, i, 2)
                if more:
                    xa_act_qn(e, i + 1, 1)
                xa_act_u(e, i, 1)
                xa_act_pT(e, i, 3)
                xa_act_u(e, i, 2)
                xa_act_u(e, i, 3)
                if more:
                    xa_act_qp(e, i + 1)
            with e.Fori(0, HP - 1) as i:
                pair(i, True)
            pair(HP - 1, False)

            def lin_prefetch(e):
                for n in range(4):
                    e.dma_start(lw_raw[n][:, :, :], lw_r[n][0]).then_inc(lw_in[n], 16)
                e.dma_start(kq_b[:, 0, :], k_b.rearrange("(h p) -> p h", p=P), allow_slow_non_contiguous=True).then_inc(lin_in, 16)
                e.dma_start(kq_b[:, 1, :], q_b.rearrange("(h p) -> p h", p=P), allow_slow_non_contiguous=True).then_inc(lin_in, 16)
                e.dma_start(v_bias[:, :], v_b.rearrange("(a n) -> a n", a=1).to_broadcast([P, INNER])).then_inc(lin_in, 16)
                e.dma_start(ob_B[:, :], o_b.rearrange("(a n) -> a n", a=1).to_broadcast([P, D])).then_inc(lin_in, 16)
                e.dma_start(bb_B[:, :], b_b.rearrange("(a n) -> a n", a=1).to_broadcast([P, H])).then_inc(lin_in, 16)
                e.dma_start(bw_raw[:, :, :], bwT.rearrange("(c p) h -> p c h", p=P)).then_inc(lin_in, 16)

            wo_act(e, 0, lin_prefetch)
            e.wait_ge(lin_in, 96)
            e.activation(bw_h[:, :, :], bw_raw[:, :, :], ACT.Copy).then_inc(small_hi, 1)
            for n in range(4):
                la_act_split(e, n, 0)
            layernorm_act(e, 1)
            e.wait_ge(sp_dve, 1)
            e.activation(sp[:, 1, :], sp[:, 1, :], ACT.Exp).then_inc(sp_act, 1)
            e.wait_ge(sp_dve, 2)
            e.activation(sp[:, 3, :], sp[:, 2, :], ACT.Ln).then_inc(sp_act, 1)
            e.wait_ge(small_dve, DV_KQB)
            with e.Fori(0, HP - 1) as i:
                la_act(e, i, True)
            la_act(e, HP - 1, False)

            def moe_prefetch(e):
                for k in range(2):
                    load_w13(e, k, w1_r[E + k], w3_r[E + k])
                    load_w2(e, k, w2_r[E + k], w2_t[E + k])

            wo_act(e, 1, moe_prefetch)
            e.wait_ge(x_ready, 2 * TT)
            e.dma_start(gw_raw[:, :, :], gwT.rearrange("(c p) e -> p c e", p=P)).then_inc(moe_in, 16)
            layernorm_act(e, 2)
            e.wait_ge(moe_in, 16)
            e.activation(gw_h[:, :, :], gw_raw[:, :, :], ACT.Copy).then_inc(small_hi, 1)
            ex_act_w13(e, 0, 1)
            e.wait_ge(rt_dve, 1)
            for t in range(TT):
                last = e.activation(gate[:, t, :], ps[:, 4, t * E:(t + 1) * E], ACT.Exp, bias=r_small[:, 0, t:t + 1],
                                    accum_out=r_small[:, 1, t:t + 1])
            last.then_inc(rt_act, 1)
            ex_act_w13(e, 1, 1)
            e.wait_ge(consts, 8)
            ex_act_w2(e, 0, 1)
            ex_act_w2(e, 1, 1)
            for u in range(NSH):
                ex_act_silu(e, u % 2, u)
                if u >= 1:
                    ex_act_hT(e, (u - 1) % 2, u - 1)
                if u == NSH - 1:
                    last_act = last_turn(e)
                    ex_act_w13(e, 0, 2)
            ex_act_hT(e, 1, NSH - 1)
            e.wait_ge(shd_ps, TT)
            ex_act_xT(e, 0, 0)
            ex_act(e, 0, 0, True)
            ex_act(e, 0, 1, True)
            with e.Fori(1, last_act + 1) as i:
                ex_act(e, i, 0)
                ex_act(e, i, 1)

        @block.vector
        def _(e):
            e.wait_ge(x_in_s, 16)
            layernorm_dve(e, 0, xn_a)
            for g in range(4):
                kv = slice(g * G4, (g + 1) * G4)
                e.wait_ge(cT_hi_s, g + 1)
                e.tensor_tensor(cT_l[:, :, kv], ctxT[:, :, kv], cT_h[:, :, kv], ALU.subtract).then_inc(cT_ready, 1)
                if g == 0:
                    layernorm_split_dve(e, 0)
            e.sem_inc(sqk_free, 4)
            with e.Fori(0, 4) as g:
                for t in range(KT):
                    e.wait_ge(sqk_ready, g * KT + (t + 1))
                    e.tensor_reduce(ssk[:, t, bass.ds(g * 4, 4)], sqk[:, t % 2, :].rearrange("p (h n) -> p h n", n=P),
                                    AX.X, ALU.add).then_inc(sqk_free, 1)
            e.wait_ge(sqk_free, 4 * KT + 4)
            e.wait_ge(g_in_s, 32)
            e.sem_inc(small_dve, 1)
            e.wait_ge(rk_sqrt, 1)
            e.reciprocal(ssk[:, :, :], rk_ln[:, :, :]).then_inc(dve_step, 1)
            steps[0] += 1
            e.wait_ge(dve_step, steps[0])
            e.tensor_scalar(ssk[:, :, :], ssk[:, :, :], RSD, None, ALU.mult).then_inc(small_dve, 1)
            e.tensor_tensor(gqk[:, 2:3], gqk[:, 0:1], gqk[:, 1:2], ALU.mult).then_inc(small_dve, 1)
            for k in range(2):
                xa_dve_qn(e, 0, k)
            for k in range(2):
                xa_dve_qsplit(e, 0, k)

            def pair(i, more):
                xa_dve_scores(e, i, 0)
                xa_dve_scores(e, i, 1)
                xa_dve_norm(e, i, 0)
                xa_dve_scores(e, i, 2)
                xa_dve_norm(e, i, 1)
                xa_dve_scores(e, i, 3)
                xa_dve_norm(e, i, 2)
                xa_dve_norm(e, i, 3)
                if more:
                    xa_dve_qn(e, i + 1, 0)
                    xa_dve_qn(e, i + 1, 1)
                    xa_dve_qsplit(e, i + 1, 0)
                xa_dve_u(e, i, 0)
                if more:
                    xa_dve_qsplit(e, i + 1, 1)
                for j in range(1, JB):
                    xa_dve_u(e, i, j)
                xa_dve_ao(e, i)
            with e.Fori(0, HP - 1) as i:
                pair(i, True)
            pair(HP - 1, False)
            wo_dve(e, 0)

            def add_y(n):
                for t in range(TT):
                    e.wait_ge(y_ps, TT * n + t + 1)
                    e.tensor_tensor(x[:, t, :], x[:, t, :], ps[:, t, :], ALU.add).then_inc(x_ready, 1)
                e.wait_ge(x_ready, TT * (n + 1))

            def step(ins):
                steps[0] += 1
                ins.then_inc(dve_step, 1)
                e.wait_ge(dve_step, steps[0])

            add_y(0)
            layernorm_dve(e, 1, xn_b)
            layernorm_split_dve(e, 1)
            e.wait_ge(lin_in, 96)
            e.tensor_scalar(kq_b[:, :, :], kq_b[:, :, :], RSD, None, ALU.mult).then_inc(small_dve, 1)
            e.wait_ge(small_ps, PS_BETA)
            step(e.tensor_tensor(sp[:, 0, :].rearrange("p (t h) -> p t h", h=H), ps[:, 4, 0:TT * H].rearrange("p (t h) -> p t h", h=H),
                                 bb_B[:, :].unsqueeze(1).to_broadcast([P, TT, H]), ALU.add))
            e.scalar_tensor_tensor(sp[:, 1, :], sp[:, 0, :], -1.0, sp[:, 0, :], ALU.mult, ALU.min).then_inc(sp_dve, 1)
            e.wait_ge(sp_act, 1)
            e.tensor_scalar(sp[:, 2, :], sp[:, 1, :], 1.0, None, ALU.add).then_inc(sp_dve, 1)
            e.wait_ge(sp_dve, 2)
            step(e.tensor_scalar(sp[:, 4, :], sp[:, 2, :], 1.0, None, ALU.subtract))
            step(e.scalar_tensor_tensor(sp[:, 5, :], sp[:, 4, :], 0.0, sp[:, 1, :], ALU.is_equal, ALU.mult))
            step(e.tensor_scalar(sp[:, 4, :], sp[:, 4, :], 1e-30, None, ALU.max))
            step(e.reciprocal(sp[:, 4, :], sp[:, 4, :]))
            step(e.tensor_tensor(sp[:, 4, :], sp[:, 4, :], sp[:, 1, :], ALU.mult))
            e.wait_ge(sp_act, 2)
            step(e.tensor_tensor(sp[:, 4, :], sp[:, 4, :], sp[:, 3, :], ALU.mult))
            step(e.tensor_tensor(sp[:, 4, :], sp[:, 4, :], sp[:, 5, :], ALU.add))
            step(e.scalar_tensor_tensor(beta[:, :, :].rearrange("p t h -> p (t h)"), sp[:, 0, :], 0.0, sp[:, 4, :], ALU.max, ALU.add))
            e.wait_ge(mask_ready, 1)
            with e.Fori(0, HP) as i:
                la_dve(e, i)
            for t in range(TT):
                step(e.tensor_tensor(x[:, t, :], x[:, t, :], ob_B[:, :], ALU.add))
            wo_dve(e, 1)
            add_y(1)

            layernorm_dve(e, 2, xn_c)
            layernorm_split_dve(e, 2)
            lg = ps[:, 4, 0:TT * E].rearrange("p (t n) -> p t n", n=E)
            e.wait_ge(small_ps, PS_LOGITS)
            e.tensor_reduce(r_small[:, 0, :], lg, AX.X, ALU.max, negate=True).then_inc(rt_dve, 1)
            ex_dve_w13(e, 0, 1)
            e.wait_ge(rt_act, 1)
            step(e.reciprocal(r_small[:, 2, :], r_small[:, 1, :]))
            step(e.tensor_tensor(gate[:, :, :], gate[:, :, :], r_small[:, 2, :].unsqueeze(2).to_broadcast([P, TT, E]), ALU.mult))
            for t in range(TT):
                e.max(top_w[:, t, :], gate[:, t, :]).then_inc(dve_step, 1)
            steps[0] += TT
            e.wait_ge(dve_step, steps[0])
            for t in range(TT):
                e.max_index(top_i[:, t, :], top_w[:, t, :], gate[:, t, :]).then_inc(dve_step, 1)
            steps[0] += TT
            e.wait_ge(dve_step, steps[0])
            step(e.tensor_copy(top_f[:, :, :], top_i[:, :, :]))
            e.wait_ge(pool_consts, 7)
            for t in range(TT):
                e.tensor_tensor(hot[:, t, :, :], iota_e[:, 0:E].unsqueeze(1).to_broadcast([P, TOP_K, E]),
                                top_f[:, t, 0:TOP_K].unsqueeze(2).to_broadcast([P, TOP_K, E]), ALU.is_equal).then_inc(dve_step, 1)
            steps[0] += TT
            e.wait_ge(dve_step, steps[0])
            for t in range(TT):
                e.tensor_reduce(chosen[:, t, :], hot[:, t, :, :].rearrange("p k n -> p n k"), AX.X, ALU.add).then_inc(dve_step, 1)
            steps[0] += TT
            e.wait_ge(dve_step, steps[0])
            for t in range(TT):
                e.tensor_copy(chosen4[:, t, :, :], chosen[:, t, :].unsqueeze(2).to_broadcast([P, E, CT])).then_inc(rt_dve, 1)
            ex_dve_w13(e, 1, 2)

            def counts():
                e.wait_ge(small_ps, PS_POS)
                step(e.tensor_copy(pos[:, :, :], ps[:, 4, P:P + TT * E].rearrange("p (t n) -> p t n", n=E)))
                step(e.tensor_copy(cnt[:, 0:1], ps[:, 4, 2 * P:2 * P + 1]))
                step(e.tensor_scalar(part_i[:, 1:2], part_i[:, 0:1], 2, None, ALU.arith_shift_right))
                step(e.tensor_scalar(part_i[:, 2:3], part_i[:, 0:1], CT - 1, 7, ALU.bitwise_and, ALU.arith_shift_left))
                step(e.tensor_copy(part[:, 0:2], part_i[:, 1:3]))
                step(e.tensor_tensor(cnt[:, 1:2], cnt[:, 0:1], part[:, 1:2], ALU.is_gt))
                e.tensor_scalar(valid_B[:, :], ones[:, :], cnt[:, 1:2], None, ALU.mult).then_inc(small_dve, 1)

            def places():
                e.wait_ge(small_ps, PS_PREFIX)
                step(e.tensor_copy(cnt[:, 2:4], ps[:, 7, 0:2]))
                e.tensor_scalar(m_hot[:, :], iota_e[:, :], cnt[:, 2:3], cnt[:, 1:2], ALU.is_equal, ALU.mult).then_inc(small_dve, 1)
                step(e.tensor_copy(start[:, :], ps[:, 7, 2:2 + E]))
                step(e.scalar_tensor_tensor(pos[:, :, :], start[:, :].unsqueeze(1).to_broadcast([P, TT, E]), float(P),
                                            pos[:, :, :], ALU.mult, ALU.add))
                for t in range(TT):
                    e.tensor_tensor(hotp[:, t, :, :], hot[:, t, :, :], pos[:, t, :].unsqueeze(1).to_broadcast([P, TOP_K, E]),
                                    ALU.mult).then_inc(dve_step, 1)
                steps[0] += TT
                e.wait_ge(dve_step, steps[0])
                step(e.tensor_reduce(slot_f[:, :, :].rearrange("p t k -> p (t k)"), hotp[:, :, :, :].rearrange("p t k n -> p (t k) n"),
                                     AX.X, ALU.add))
                e.tensor_copy(slot_i[:, :, :], slot_f[:, :, :]).then_inc(small_dve, 1)

            def lists():
                e.wait_ge(small_ps, PS_LIST)
                step(e.tensor_copy(lst_f[0:1, 0:ML], ps[0:1, 7, 0:ML]))
                step(e.tensor_scalar(lst_f[0:1, ML:ML + 1], cnt[0:1, 3:4], 1.0, None, ALU.subtract))
                step(e.tensor_copy(lst[0:1, :], lst_f[0:1, :]))
                e.tensor_scalar(lst[0:1, ML:ML + 1], lst[0:1, ML:ML + 1], 1, None, ALU.arith_shift_right).then_inc(small_dve, 1)

            def sh_x_add(t):
                e.wait_ge(shd_ps, t + 1)
                e.tensor_tensor(x[:, t, :], x[:, t, :], ps[:, 6, :], ALU.add).then_inc(sh_x, 1)

            for u in range(NSH):
                ex_dve_h(e, u % 2, u)
                if u >= 1:
                    ex_dve_hT(e, (u - 1) % 2, u - 1)
                if u == 1:
                    counts()
                if u == 2:
                    places()
                if u == 3:
                    lists()
                if u % 2 and u >= 3:
                    sh_x_add((u - 3) // 2)
            ex_dve_hT(e, 1, NSH - 1)
            ex_dve_w13(e, 0, 3)
            e.wait_ge(small_ps, PS_TOKENS)
            e.tensor_copy(tl[:, :], ps[:, 7, 0:ML]).then_inc(small_dve, 1)
            sh_x_add(TT - 1)
            last_i = last_turn(e)
            ex_dve_xT(e, 0, 0)
            ex_dve(e, 0, 0, True)
            ex_dve(e, 0, 1, True)
            ex_dve(e, 1, 0, slot_free=True)
            ex_dve(e, 1, 1)
            with e.Fori(2, last_i + 1) as i:
                ex_dve(e, i, 0)
                ex_dve(e, i, 1)
            ex_dve_ob(e, last_i * 2 + 1, 1, last_i)
            e.wait_ge(sh_x, TT)
            for t in range(TT):
                for k in range(TOP_K):
                    n = t * TOP_K + k
                    e.wait_ge(gb_in[n % GB], 16 * (n // GB + 1))
                    if n % TOP_K:
                        e.wait_ge(gb_used, n)
                    e.scalar_tensor_tensor(x[:, t, :], gb[:, n % GB, :], top_w[:, t, k:k + 1], x[:, t, :],
                                           ALU.mult, ALU.add).then_inc(gb_used, 1)

        @block.tensor
        def _(e):
            e.wait_ge(consts, 5)
            layernorm_pe(e, 0, xn_a)
            with e.Fori(0, 4) as g:
                for t in range(KT):
                    if t % 4 == 0:
                        e.wait_ge(cT_ready, t // 4 + 1)
                    if t == 0:
                        e.wait_ge(wk_ready, g + 1)
                    e.wait_ge(sqk_free, g * KT + (t + 1))
                    tk = slice(t * P, (t + 1) * P)
                    for c in range(CC):
                        m = mm3(ps[:, 4 + t % 4, :], cT_h[:, c, tk], cT_l[:, c, tk],
                                wk_h[:, c, bass.ds(g * G4, G4)], wk_l[:, c, bass.ds(g * G4, G4)],
                                c == 0, c == CC - 1)
                    m.then_inc(k_ps, 1)
            e.wait_ge(small_dve, DV_RK)
            e.wait_ge(xT_ready, TT)
            for n in range(2):
                e.transpose(ps[:, n, 0:P], ssk[:, n * KT // 2:(n + 1) * KT // 2, :].rearrange("p t h -> p (t h)"),
                            ident[:, :]).then_inc(small_ps, 1)
            e.wait_ge(rkT_ready, 2)
            xa_pe_q(e, 0, 0)
            xa_pe_q(e, 0, 1)
            xa_pe_ss(e, 0, 0)
            xa_pe_ss(e, 0, 1)
            xa_pe_qp(e, 0)
            e.wait_ge(ctx_in_s, 16)

            def pair(i, more):
                for j in range(JB):
                    xa_pe_scores(e, i, j)
                if more:
                    xa_pe_q(e, i + 1, 0)
                    xa_pe_q(e, i + 1, 1)
                    xa_pe_ss(e, i + 1, 0)
                    xa_pe_ss(e, i + 1, 1)
                xa_pe_pT(e, i, 0)
                xa_pe_pT(e, i, 1)
                xa_pe_u(e, i, 0)
                xa_pe_pT(e, i, 2)
                xa_pe_u(e, i, 1)
                xa_pe_pT(e, i, 3)
                xa_pe_u(e, i, 2)
                xa_pe_u(e, i, 3)
                if more:
                    xa_pe_qp(e, i + 1)
                xa_pe_ao(e, i)
            with e.Fori(0, HP - 1) as i:
                pair(i, True)
            pair(HP - 1, False)
            wo_pe(e, 0)

            layernorm_pe(e, 1, xn_b)
            e.wait_ge(small_lo, SP_BETA)
            e.wait_ge(xT_ready, 2 * TT)
            for t in range(TT):
                tk = slice(t * P, (t + 1) * P)
                for c in range(DC):
                    m = mm3(ps[:, 4, t * H:(t + 1) * H], xT_hi[:, c, tk], xT_lo[:, c, tk], bw_h[:, c, :], bw_l[:, c, :],
                            c == 0, c == DC - 1)
            m.then_inc(small_ps, 1)
            e.wait_ge(sp_dve, 1)
            with e.Fori(0, HP) as i:
                la_pe(e, i)
            wo_pe(e, 1)

            layernorm_pe(e, 2, xn_c)
            e.wait_ge(small_lo, SP_ROUTER)
            e.wait_ge(xT_ready, 3 * TT)
            for t in range(TT):
                tk = slice(t * P, (t + 1) * P)
                for c in range(DC):
                    m = mm3(ps[:, 4, t * E:(t + 1) * E], xT_hi[:, c, tk], xT_lo[:, c, tk], gw_h[:, c, :], gw_l[:, c, :],
                            c == 0, c == DC - 1)
            m.then_inc(small_ps, 1)

            def shared_down(t):
                e.wait_ge(hT_ready, 2 * t + 2)
                e.wait_ge(w2_ready, 2)
                if t:
                    e.wait_ge(sh_x, t)
                ex_down(0, 6, True, False)
                ex_down(1, 6, False, True).then_inc(shd_ps, 1)

            for u in range(NSH):
                t, k = u // 2, u % 2
                tk = slice(t * P, (t + 1) * P)
                e.wait_ge(w13_ready, k + 1)
                if u >= 2:
                    e.wait_ge(h_ready, u - 1)
                ex_up(lambda c: xT_hi[:, c, tk], lambda c: xT_lo[:, c, tk], k)
                if u % 2 and u >= 3:
                    shared_down(t - 1)
                if u >= 1:
                    ex_hT(e, 1 - k, u - 1)
                if u == 1:
                    e.wait_ge(rt_dve, 1 + TT)
                    e.wait_ge(pool_consts, 7)
                    for n in range(TT):
                        for q in range(n + 1):
                            e.matmul(ps[:, 4, P + n * E:P + (n + 1) * E], (strict if q == n else ones)[:, :],
                                     chosen[:, q, :], start=q == 0, stop=q == n)
                    for n in range(TT):
                        m = e.matmul(ps[:, 4, 2 * P:2 * P + 1], chosen4[:, n, :, :].rearrange("p n j -> p (n j)"),
                                     ones[:, 0:1], start=n == 0, stop=n == TT - 1)
                    m.then_inc(small_ps, 1)
                if u == 2:
                    e.wait_ge(small_dve, DV_VALID)
                    e.matmul(ps[:, 7, 0:1], strict[:, :], cnt[:, 1:2], start=True, stop=True)
                    e.matmul(ps[:, 7, 1:2], ones[:, :], cnt[:, 1:2], start=True, stop=True)
                    e.matmul(ps[:, 7, 2:2 + E], valid_B[:, :], below[:, :], start=True, stop=True).then_inc(small_ps, 1)
                if u == 3:
                    e.wait_ge(small_dve, DV_SLOTS)
                    e.matmul(ps[0:1, 7, 0:ML], part[:, 0:1], m_hot[:, :], start=True, stop=True).then_inc(small_ps, 1)
            ex_hT(e, 1, NSH - 1)
            shared_down(TT - 1)
            e.wait_ge(small_dve, DV_LISTS)
            e.wait_ge(scratch_io, IO_LISTS)
            e.transpose(ps[:, 7, 0:ML], tl_rows[0:ML, :], ident[0:ML, 0:ML]).then_inc(small_ps, 1)
            last_i = last_turn(e)
            ex_pe_xT(e, 0, 1)
            e.wait_ge(small_dve, DV_TOKENS)
            e.wait_ge(sh_x, TT)
            ex_pe(e, 0, 0, True)
            ex_pe(e, 0, 1, True)
            with e.Fori(1, last_i + 1) as i:
                ex_pe(e, i, 0)
                ex_pe(e, i, 1)
            ex_pe_down(e, last_i * 2 + 1, 1)


def kernel(x, ctx_1024, L0_xattn_Wq, L0_xattn_Wk, L0_xattn_Wv, L0_xattn_Wo, L0_xattn_gq, L0_xattn_gk,
           L0_attn_q_w, L0_attn_q_b, L0_attn_k_w, L0_attn_k_b, L0_attn_v_w, L0_attn_v_b, L0_attn_a_w, L0_attn_a_b,
           L0_attn_b_w, L0_attn_b_b, L0_attn_og_w, L0_attn_o_w, L0_attn_o_b, L0_ffn_gate_w, L0_ffn_w1, L0_ffn_w2,
           L0_ffn_w3, L0_ffn_sw1, L0_ffn_sw2, L0_ffn_sw3):
    import numpy as np
    import concourse.bacc as bacc
    from concourse import mybir
    from concourse.bass_utils import run_bass_kernel_spmd

    x, ctx = np.asarray(x), np.asarray(ctx_1024)
    tokens, ctx = x.reshape(-1, x.shape[-1]), ctx.reshape(-1, ctx.shape[-1])
    w1, w2, w3 = (np.asarray(w) for w in (L0_ffn_w1, L0_ffn_w2, L0_ffn_w3))
    dim, inter = w1.shape[1:]
    halves = np.asarray(L0_ffn_sw1).shape[1] // inter

    def halved(w):
        return np.asarray(w).reshape(dim, halves, inter).transpose(1, 0, 2)

    host = {
        "x_in": tokens, "ctx_in": ctx, "ctxT_in": ctx.T,
        "Wq": L0_xattn_Wq, "Wk": L0_xattn_Wk, "WkT": np.asarray(L0_xattn_Wk).T, "Wv": L0_xattn_Wv, "Wo": L0_xattn_Wo,
        "gq": L0_xattn_gq, "gk": L0_xattn_gk,
        "qwT": np.asarray(L0_attn_q_w).T, "q_b": L0_attn_q_b, "kwT": np.asarray(L0_attn_k_w).T, "k_b": L0_attn_k_b,
        "vwT": np.asarray(L0_attn_v_w).T, "v_b": L0_attn_v_b, "bwT": np.asarray(L0_attn_b_w).T, "b_b": L0_attn_b_b,
        "ogwT": np.asarray(L0_attn_og_w).T, "owT": np.asarray(L0_attn_o_w).T, "o_b": L0_attn_o_b,
        "gwT": np.asarray(L0_ffn_gate_w).T,
        "w1": np.concatenate([w1, halved(L0_ffn_sw1)]),
        "w2": np.concatenate([w2, np.asarray(L0_ffn_sw2).reshape(halves, inter, dim)]),
        "w3": np.concatenate([w3, halved(L0_ffn_sw3)]),
    }
    nc = bacc.Bacc("TRN2", target_bir_lowering=False, num_devices=1)
    arrays, args = {}, {}
    for name, a in host.items():
        a = np.ascontiguousarray(a)
        arrays[f"in_{name}"] = a
        args[name] = nc.dram_tensor(f"in_{name}", a.shape, mybir.dt.from_np(a.dtype), kind="ExternalInput").ap()
    out = nc.dram_tensor("out_0", tokens.shape, mybir.dt.from_np(tokens.dtype), kind="ExternalOutput").ap()
    perceiver_block(nc, **args, out=out)
    result = run_bass_kernel_spmd(nc, [arrays], core_ids=[0])
    return result.results[0]["out_0"].reshape(x.shape)
```

```python
from contextlib import ExitStack

import concourse.bass as bass
from concourse import mybir

ALU = mybir.AluOpType
ACT = mybir.ActivationFunctionType
AX = mybir.AxisListType
F32 = mybir.dt.float32
F32R = mybir.dt.float32r
I32 = mybir.dt.int32

P = 128
LN_EPS = 1e-5
RMS_EPS = 1e-5
L2_EPS = 1e-12
TOP_K = 6


def perceiver_block(nc, x_in, ctx_in, ctxT_in_, Wq, Wk, WkT, Wv, Wo, gq, gk,
                    qwT, q_b, kwT, k_b, vwT, v_b, bwT, b_b, ogwT, owT, o_b,
                    gwT, w1, w2, w3, out):
    T, D = x_in.shape
    NKV, C = ctx_in.shape
    INNER = Wq.shape[1]
    H = INNER // P
    B = 8
    SQ = T // B
    SKV = NKV // B
    TT, DC, CC, KT = T // P, D // P, C // P, NKV // P
    KPB = SKV // P
    HP = H // 2
    JB = 4
    G4 = 512
    RSD = float(P) ** -0.5

    stack = ExitStack()
    with stack:
        def sem(name):
            return stack.enter_context(nc.semaphore(name))

        def sbuf(where, name, shape, dt=F32):
            return where.enter_context(nc.sbuf_tensor(name, shape, dt))

        ps = stack.enter_context(nc.psum_tensor("ps", [P, 8, 512], F32))

        x = sbuf(stack, "x", [P, TT, D])
        xT_hi = sbuf(stack, "xT_hi", [P, DC, T], F32R)
        xT_lo = sbuf(stack, "xT_lo", [P, DC, T], F32R)
        ident = sbuf(stack, "ident", [P, P])
        zeros = sbuf(stack, "zeros", [P, D])
        ones = sbuf(stack, "ones", [P, P])
        eps = sbuf(stack, "eps", [P, 1])
        ln_std = sbuf(stack, "ln_std", [P, TT])
        ln_stat = sbuf(stack, "ln_stat", [P, TT, 6])
        ln_mv = sbuf(stack, "ln_mv", [P, TT, 2])
        ln_rstd = sbuf(stack, "ln_rstd", [P, TT])

        kn = ExitStack()
        ssk = sbuf(kn, "ssk", [P, KT, H])
        rk_ln = sbuf(kn, "rk_ln", [P, KT, H])
        rkT = sbuf(kn, "rkT", [P, 2, P])
        wk_raw = sbuf(kn, "wk_raw", [P, CC, INNER])
        wk_h = sbuf(kn, "wk_h", [P, CC, INNER], F32R)
        wk_l = sbuf(kn, "wk_l", [P, CC, INNER], F32R)
        cT_h = sbuf(kn, "cT_h", [P, CC, NKV], F32R)
        cT_l = sbuf(kn, "cT_l", [P, CC, NKV], F32R)
        sqk = sbuf(kn, "sqk", [P, 2, G4])
        kn.close()

        attn = ExitStack()
        aoT = sbuf(attn, "aoT", [P, H, T])
        wo_raw = sbuf(attn, "wo_raw", [P, 2, D])
        wo_h = sbuf(attn, "wo_h", [P, 2, D], F32R)
        wo_l = sbuf(attn, "wo_l", [P, 2, D], F32R)
        ao_h = sbuf(attn, "ao_h", [P, 2, T], F32R)
        ao_l = sbuf(attn, "ao_l", [P, 2, T], F32R)

        xat = ExitStack()
        rkB = sbuf(xat, "rkB", [P, B, SKV])
        sc = sbuf(xat, "sc", [P, B, SKV])
        pT = sbuf(xat, "pT", [P, B, KPB, P])
        u_h = sbuf(xat, "u_h", [P, CC, B, 2, SQ], F32R)
        u_l = sbuf(xat, "u_l", [P, CC, B, 2, SQ], F32R)
        ctxT = sbuf(xat, "ctxT", [P, CC, NKV])
        ctx = sbuf(xat, "ctx", [P, KT, C])
        gqk = sbuf(xat, "gqk", [P, 3])
        wq_raw = sbuf(xat, "wq_raw", [P, DC, 2 * P])
        wq_h = sbuf(xat, "wq_h", [P, DC, 2 * P], F32R)
        wq_l = sbuf(xat, "wq_l", [P, DC, 2 * P], F32R)
        wkT_raw = sbuf(xat, "wkT_raw", [P, 2, C])
        wkT_h = sbuf(xat, "wkT_h", [P, 2, C], F32R)
        wkT_l = sbuf(xat, "wkT_l", [P, 2, C], F32R)
        wv_raw = sbuf(xat, "wv_raw", [P, CC, 2 * P])
        wv_h = sbuf(xat, "wv_h", [P, CC, 2 * P], F32R)
        wv_l = sbuf(xat, "wv_l", [P, CC, 2 * P], F32R)
        sq = sbuf(xat, "sq", [P, B, 2, SQ])
        qn_h = sbuf(xat, "qn_h", [P, 2, T], F32R)
        qn_l = sbuf(xat, "qn_l", [P, 2, T], F32R)
        qpT = sbuf(xat, "qpT", [P, CC, B, 2, SQ])
        xn_a = qpT[:, :, :, :, :].rearrange("p c b k q -> p (c b k q)").rearrange("p (t d) -> p t d", t=TT)
        rms = sbuf(xat, "rms", [P, B])
        rq = sbuf(xat, "rq", [P, B])
        nmx = sbuf(xat, "nmx", [P, 2, B])
        sm = sbuf(xat, "sm", [P, B])
        rsm = sbuf(xat, "rsm", [P, B])
        xat.close()

        lin = ExitStack()
        xn_b = sbuf(lin, "xn_b", [P, TT, D])
        lw_raw = [sbuf(lin, f"lw_raw{n}", [P, DC, 2 * P]) for n in range(4)]
        lw_h = [sbuf(lin, f"lw_h{n}", [P, DC, 2 * P], F32R) for n in range(4)]
        lw_l = [sbuf(lin, f"lw_l{n}", [P, DC, 2 * P], F32R) for n in range(4)]
        kq = sbuf(lin, "kq", [P, 4, T])
        kq_sq = sbuf(lin, "kq_sq", [P, 4, T])
        kq_std = sbuf(lin, "kq_std", [P, 4, TT])
        kq_r = sbuf(lin, "kq_r", [P, 4, TT])
        v_scale = sbuf(lin, "v_scale", [P, 2, TT])
        rq_diag = sbuf(lin, "rq_diag", [P, 2, TT, P])
        kq_b = sbuf(lin, "kq_b", [P, 2, H])
        vt = sbuf(lin, "vt", [P, TT, 2 * P])
        v_bias = sbuf(lin, "v_bias", [P, INNER])
        at = sbuf(lin, "at", [P, 2, T])
        sg = sbuf(lin, "sg", [P, 2, T])
        mask = sbuf(lin, "mask", [P, P])
        ob_B = sbuf(lin, "ob_B", [P, D])
        bw_raw = sbuf(lin, "bw_raw", [P, DC, H])
        bw_h = sbuf(lin, "bw_h", [P, DC, H], F32R)
        bw_l = sbuf(lin, "bw_l", [P, DC, H], F32R)
        bb_B = sbuf(lin, "bb_B", [P, H])
        beta = sbuf(lin, "beta", [P, TT, H])
        sp = sbuf(lin, "sp", [P, 6, TT * H])
        lin.close()
        attn.close()

        E = gwT.shape[1]
        FF = w1.shape[2]
        FC = -(-FF // P)
        FW = [min(P, FF - c * P) for c in range(FC)]
        CAP = T
        CT = CAP // P
        MI = E + T * TOP_K // P
        ML = MI + 2
        moe = ExitStack()
        xn_c = sbuf(moe, "xn_c", [P, TT, D])
        GB = 8
        gb = sbuf(moe, "gb", [P, GB, D])
        xe = sbuf(moe, "xe", [P, 2, D])
        xeT_h = sbuf(moe, "xeT_h", [P, 2, DC, P], F32R)
        xeT_l = sbuf(moe, "xeT_l", [P, 2, DC, P], F32R)
        h1 = sbuf(moe, "h1", [P, 2, FF])
        h = sbuf(moe, "h", [P, 2, FF])
        hT_h = sbuf(moe, "hT_h", [P, 2, FC, P], F32R)
        hT_l = sbuf(moe, "hT_l", [P, 2, FC, P], F32R)
        ob = sbuf(moe, "ob", [P, 2, D])
        idx_col = sbuf(moe, "idx_col", [P, 2], I32)
        gw_raw = sbuf(moe, "gw_raw", [P, DC, E])
        gw_h = sbuf(moe, "gw_h", [P, DC, E], F32R)
        gw_l = sbuf(moe, "gw_l", [P, DC, E], F32R)
        gate = sbuf(moe, "gate", [P, TT, E])
        r_small = sbuf(moe, "r_small", [P, 3, TT])
        top_w = sbuf(moe, "top_w", [P, TT, 8])
        top_i = sbuf(moe, "top_i", [P, TT, 8], mybir.dt.uint32)
        top_f = sbuf(moe, "top_f", [P, TT, 8])
        hot = sbuf(moe, "hot", [P, TT, TOP_K, E])
        hotp = sbuf(moe, "hotp", [P, TT, TOP_K, E])
        chosen = sbuf(moe, "chosen", [P, TT, E])
        chosen4 = sbuf(moe, "chosen4", [P, TT, E, CT])
        pos = sbuf(moe, "pos", [P, TT, E])
        slot_f = sbuf(moe, "slot_f", [P, TT, TOP_K])
        slot_i = sbuf(moe, "slot_i", [P, TT, TOP_K], I32)
        iota_e = sbuf(moe, "iota_e", [P, ML])
        strict = sbuf(moe, "strict", [P, P])
        part = sbuf(moe, "part", [P, 2])
        part_i = sbuf(moe, "part_i", [P, 3], I32)
        tok_id = sbuf(moe, "tok_id", [P, TT])
        tl_rows = sbuf(moe, "tl_rows", [P, P])
        tl = sbuf(moe, "tl", [P, ML], I32)
        valid_B = sbuf(moe, "valid_B", [P, P])
        below = sbuf(moe, "below", [P, E])
        start = sbuf(moe, "start", [P, E])
        cnt = sbuf(moe, "cnt", [P, 4])
        m_hot = sbuf(moe, "m_hot", [P, ML])
        lst_f = sbuf(moe, "lst_f", [1, ML + 1])
        lst = sbuf(moe, "lst", [1, ML + 1], I32)
        w13_raw = sbuf(moe, "w13_raw", [P, 2, DC, 2 * FF])
        w13_h = sbuf(moe, "w13_h", [P, 2, DC, 2 * FF], F32R)
        w13_l = sbuf(moe, "w13_l", [P, 2, DC, 2 * FF], F32R)
        w2_raw = sbuf(moe, "w2_raw", [P, 2, FC, D])
        w2_h = sbuf(moe, "w2_h", [P, 2, FC, D], F32R)
        w2_l = sbuf(moe, "w2_l", [P, 2, FC, D], F32R)
        moe.close()

        xn_dram = nc.dram_tensor("xn_scratch", [T, D], F32)
        tl_dram = nc.dram_tensor("token_list_scratch", [ML * P, 1], F32)
        ob_dram = nc.dram_tensor("expert_out_scratch", [MI * P, D], F32)
        rk_dram = nc.dram_tensor("rk_scratch", [H, NKV], F32)

        consts = sem("consts")
        x_in_s, ctx_in_s, g_in_s = sem("x_in"), sem("ctx_in_s"), sem("g_in")
        ctxT_in = [sem(f"ctxT_in{g}") for g in range(4)]
        wk_in = [sem(f"wk_in{g}") for g in range(4)]
        dve_step = sem("dve_step")
        xn_ready, xT_ps, xT_hi_s, xT_ready = sem("xn_ready"), sem("xT_ps"), sem("xT_hi_s"), sem("xT_ready")
        cT_hi_s, cT_ready, wk_hi_s, wk_ready = sem("cT_hi_s"), sem("cT_ready"), sem("wk_hi_s"), sem("wk_ready")
        k_ps, sqk_ready, sqk_free = sem("k_ps"), sem("sqk_ready"), sem("sqk_free")
        rkT_ready, scratch_io = sem("rkT_ready"), sem("scratch_io")
        small_ps, small_dve, small_hi, small_lo = sem("small_ps"), sem("small_dve"), sem("small_hi"), sem("small_lo")
        PS_RKT, PS_BETA, PS_LOGITS, PS_POS, PS_PREFIX, PS_LIST, PS_TOKENS = 2, 3, 4, 5, 6, 7, 8
        DV_SSK, DV_RK, DV_KQB, DV_VALID, DV_ORDER, DV_SLOTS, DV_LISTS, DV_TOKENS = 2, 3, 4, 5, 6, 7, 8, 9
        SP_BETA, SP_ROUTER = 1, 2
        IO_RK, IO_CLEARED, IO_LISTS = 32, 64, 80
        wq_in, wq_hi_s, wq_ready = sem("wq_in"), sem("wq_hi_s"), sem("wq_ready")
        wkT_in, wkT_hi_s, wkT_ready = sem("wkT_in"), sem("wkT_hi_s"), sem("wkT_ready")
        wv_in, wv_hi_s, wv_ready = sem("wv_in"), sem("wv_hi_s"), sem("wv_ready")
        rkB_in = [sem(f"rkB_in{j}") for j in range(JB)]
        q_ps, sq_ready, ss_ps, qn_hi_s, qn_split = sem("q_ps"), sem("sq_ready"), sem("ss_ps"), sem("qn_hi_s"), sem("qn_split")
        qp_ps, qp_ready = sem("qp_ps"), sem("qp_ready")
        s_ps, s_ready, nmx_ready, p_ready, pn_ready = sem("s_ps"), sem("s_ready"), sem("nmx_ready"), sem("p_ready"), sem("pn_ready")
        pT_ps, pT_ready, u_ps, u_hi_s, u_ready = sem("pT_ps"), sem("pT_ready"), sem("u_ps"), sem("u_hi_s"), sem("u_ready")
        ao_ps, ao_ready = sem("ao_ps"), sem("ao_ready")
        wo_in = [sem("wo_in0"), sem("wo_in1")]
        wo_hi_s, wo_ready, ao_split, wo_mm, y_ps = sem("wo_hi_s"), sem("wo_ready"), sem("ao_split"), sem("wo_mm"), sem("y_ps")
        x_ready = sem("x_ready")
        out_done = sem("out_done")
        lw_in = [sem(f"lw_in{n}") for n in range(4)]
        lw_hi_s = [sem(f"lw_hi_s{n}") for n in range(4)]
        lw_ready = [sem(f"lw_ready{n}") for n in range(4)]
        lin_in = sem("lin_in")
        mask_ready = sem("mask_ready")
        sp_dve, sp_act, beta_ready = sem("sp_dve"), sem("sp_act"), sem("beta_ready")
        kq_ps, kq_sq_ready, kq_ss_ps, kq_norm, kq_guard, kq_recip, q_n = (
            sem("kq_ps"), sem("kq_sq_ready"), sem("kq_ss_ps"), sem("kq_norm"), sem("kq_guard"),
            sem("kq_recip"), sem("q_n"))
        v_scale_ready, rq_diag_ready, rqB_ps = sem("v_scale_ready"), sem("rq_diag_ready"), sem("rqB_ps")
        v_ps, v_biased, v_ready = sem("v_ps"), sem("v_biased"), sem("v_ready")
        og_ps, sg_ready, at_ps, at_ready, o_ps = sem("og_ps"), sem("sg_ready"), sem("at_ps"), sem("at_ready"), sem("o_ps")
        moe_in, pool_consts, rt_dve, rt_act, tl_scattered = (
            sem("moe_in"), sem("pool_consts"), sem("rt_dve"), sem("rt_act"), sem("tl_scattered"))
        shd_ps, sh_x = sem("shd_ps"), sem("sh_x")
        w13_in, w2_in = [sem("w13_in0"), sem("w13_in1")], [sem("w2_in0"), sem("w2_in1")]
        w13_hi_s, w13_ready, w2_hi_s, w2_ready = sem("w13_hi_s"), sem("w13_ready"), sem("w2_hi_s"), sem("w2_ready")
        idx_ready, xe_in = sem("idx_ready"), [sem("xe_in0"), sem("xe_in1")]
        xeT_ps, xeT_hi_s, xeT_ready, h1_ps, h3_ps, h1_ready, h_ready = (
            sem("xeT_ps"), sem("xeT_hi_s"), sem("xeT_ready"), sem("h1_ps"), sem("h3_ps"), sem("h1_ready"), sem("h_ready"))
        hT_ps, hT_hi_s, hT_ready, d_ps, ob_ready = sem("hT_ps"), sem("hT_hi_s"), sem("hT_ready"), sem("d_ps"), sem("ob_ready")
        ob_out = [sem("ob_out0"), sem("ob_out1")]
        gb_in, gb_used = [sem(f"gb_in{n}") for n in range(GB)], sem("gb_used")

        steps = [0]

        def mm3(out_ap, lh, ll, rh, rl, first=True, last=True):
            nc.tensor.matmul(out_ap, lh, rh, start=first, stop=False)
            nc.tensor.matmul(out_ap, lh, rl, start=False, stop=False)
            return nc.tensor.matmul(out_ap, ll, rh, start=False, stop=last)

        def layernorm_dve(e, n, xn):
            def step():
                e.wait_ge(dve_step, steps[0])
            for t in range(TT):
                e.bn_stats(ln_stat[:, t, :], x[:, t, :]).then_inc(dve_step, 1)
            steps[0] += TT
            step()
            for t in range(TT):
                e.bn_aggr(ln_mv[:, t, :], ln_stat[:, t, :]).then_inc(ln_var_ready, 1)
            e.wait_ge(ln_std_ready, n + 1)
            e.reciprocal(ln_rstd[:, :], ln_std[:, :]).then_inc(dve_step, 1)
            steps[0] += 1
            step()
            for t in range(TT):
                e.tensor_scalar(xn[:, t, :], x[:, t, :], ln_mv[:, t, 0:1], ln_rstd[:, t:t + 1],
                                ALU.subtract, ALU.mult).then_inc(xn_ready, 1)

        def layernorm_pe(e, n, xn):
            for t in range(TT):
                e.wait_ge(xn_ready, TT * n + t + 1)
                for c in range(DC):
                    last = e.transpose(ps[:, t, c * P:(c + 1) * P], xn[:, t, c * P:(c + 1) * P], ident[:, :])
                last.then_inc(xT_ps, 1)

        def layernorm_act(e, n):
            e.wait_ge(ln_var_ready, TT * (n + 1))
            e.activation(ln_std[:, :], ln_mv[:, :, 1], ACT.Sqrt, bias=eps[:, 0:1]).then_inc(ln_std_ready, 1)
            for t in range(TT):
                e.wait_ge(xT_ps, TT * n + t + 1)
                e.activation(xT_hi[:, :, t * P:(t + 1) * P], ps[:, t, :].rearrange("p (c n) -> p c n", c=DC),
                             ACT.Copy).then_inc(xT_hi_s, 1)

        def layernorm_split_dve(e, n):
            for t in range(TT):
                e.wait_ge(xT_hi_s, TT * n + t + 1)
                tk = slice(t * P, (t + 1) * P)
                e.tensor_tensor(xT_lo[:, :, tk], ps[:, t, :].rearrange("p (c n) -> p c n", c=DC),
                                xT_hi[:, :, tk], ALU.subtract).then_inc(xT_ready, 1)

        def wo_load(e, n, W):
            Wr = W.rearrange("(h p) n -> h p n", p=P)
            for k in range(2):
                if n:
                    e.wait_ge(wo_ready, H * n + k - 1)
                e.dma_start(wo_raw[:, k, :], Wr[k]).then_inc(wo_in[k], 16)
            with e.Fori(1, HP) as i:
                for k in range(2):
                    e.wait_ge(wo_ready, i * 2 + (H * n + k - 1))
                    e.dma_start(wo_raw[:, k:k + 1, :], Wr[bass.ds(i * 2 + k, 1)].rearrange("h p n -> p h n"))\
                        .then_inc(wo_in[k], 16)

        def wo_act(e, n, prefetch):
            def head(i, k, slot_waits=True):
                e.wait_ge(wo_in[k], i * 16 + (HP * n + 1) * 16)
                if slot_waits:
                    e.wait_ge(wo_mm, i * 2 + (H * n + k - 1))
                e.activation(wo_h[:, k, :], wo_raw[:, k, :], ACT.Copy)
                e.activation(ao_h[:, k:k + 1, :], aoT[:, bass.ds(i * 2 + k, 1), :], ACT.Copy).then_inc(wo_hi_s, 1)
            e.wait_ge(ao_ready, H * (n + 1))
            prefetch(e)
            head(0, 0, n > 0)
            head(0, 1, n > 0)
            with e.Fori(1, HP) as i:
                head(i, 0)
                head(i, 1)

        def wo_dve(e, n):
            with e.Fori(0, HP) as i:
                for k in range(2):
                    e.wait_ge(wo_hi_s, i * 2 + (H * n + k + 1))
                    e.tensor_tensor(ao_l[:, k:k + 1, :], aoT[:, bass.ds(i * 2 + k, 1), :], ao_h[:, k:k + 1, :],
                                    ALU.subtract).then_inc(ao_split, 1)

        def wo_pool(e, n):
            with e.Fori(0, HP) as i:
                for k in range(2):
                    e.wait_ge(wo_hi_s, i * 2 + (H * n + k + 1))
                    e.tensor_tensor(wo_l[:, k, :], wo_raw[:, k, :], wo_h[:, k, :], ALU.subtract).then_inc(wo_ready, 1)

        def wo_pe(e, n):
            def pair(i, first=False, last=False):
                for k in range(2):
                    e.wait_ge(ao_split, i * 2 + (H * n + k + 1))
                    e.wait_ge(wo_ready, i * 2 + (H * n + k + 1))
                    for t in range(TT):
                        tk = slice(t * P, (t + 1) * P)
                        m = mm3(ps[:, t, :], ao_h[:, k, tk], ao_l[:, k, tk], wo_h[:, k, :], wo_l[:, k, :],
                                first and k == 0, last and k == 1)
                        if last and k == 1:
                            m.then_inc(y_ps, 1)
                    if not (last and k == 1):
                        m.then_inc(wo_mm, 1)
            pair(0, first=True)
            with e.Fori(1, HP - 1) as i:
                pair(i)
            pair(HP - 1, last=True)
            e.wait_ge(y_ps, TT * (n + 1))
            e.sem_inc(wo_mm, 1)

        kvb = lambda b: slice(b * SKV, (b + 1) * SKV)
        hcol = lambda k: slice(k * P, (k + 1) * P)

        def xa_act_weights(e, p):
            e.wait_ge(wq_in, p * 16 + 16)
            e.activation(wq_h[:, :, :], wq_raw[:, :, :], ACT.Copy).then_inc(wq_hi_s, 1)
            e.wait_ge(wkT_in, p * 16 + 16)
            e.activation(wkT_h[:, :, :], wkT_raw[:, :, :], ACT.Copy).then_inc(wkT_hi_s, 1)

        def xa_act_wv(e, i):
            e.wait_ge(wv_in, i * 16 + 16)
            e.activation(wv_h[:, :, :], wv_raw[:, :, :], ACT.Copy).then_inc(wv_hi_s, 1)

        def xa_act_q(e, p, k):
            e.wait_ge(q_ps, p * 2 + (k + 1))
            e.activation(sq[:, :, k, :], ps[:, k, :].rearrange("p (b q) -> p b q", b=B), ACT.Square,
                         scale=RSD).then_inc(sq_ready, 1)
            e.activation(qn_h[:, k, :], ps[:, k, :], ACT.Copy, scale=gqk[:, 2:3]).then_inc(qn_hi_s, 1)

        def xa_act_qp(e, p):
            for k in range(2):
                for c in range(CC):
                    e.wait_ge(qp_ps, p * 4 + (2 * k + c + 1))
                    e.activation(qpT[:, c, :, k, :], ps[:, 2 * k + c, :].rearrange("p (b q) -> p b q", b=B),
                                 ACT.Copy).then_inc(qp_ready, 1)

        def xa_act_exp(e, i, j):
            e.wait_ge(nmx_ready, i * 4 + (j + 1))
            for b in (2 * j, 2 * j + 1):
                last = e.activation(sc[:, b, :], sc[:, b, :], ACT.Exp, bias=nmx[:, 1, b:b + 1], scale=rq[:, b:b + 1],
                                    accum_out=sm[:, b:b + 1])
            last.then_inc(p_ready, 1)

        def xa_act_pT(e, i, j):
            e.wait_ge(pT_ps, i * 4 + (j + 1))
            e.activation(pT[:, 2 * j:2 * j + 2, :, :].rearrange("p b k n -> p (b k n)"), ps[:, 6 + j % 2, :],
                         ACT.Copy).then_inc(pT_ready, 1)

        def xa_act_u(e, i, j):
            e.wait_ge(u_ps, i * 4 + (j + 1))
            e.activation(u_h[:, :, 2 * j:2 * j + 2, :, :].rearrange("p c b k q -> p c (b k q)"),
                         ps[:, 4 + j % 2, :].rearrange("p (c n) -> p c n", c=CC), ACT.Copy).then_inc(u_hi_s, 1)

        def xa_pool_weights(e, p):
            e.wait_ge(wq_hi_s, p + 1)
            e.tensor_tensor(wq_l[:, :, :], wq_raw[:, :, :], wq_h[:, :, :], ALU.subtract).then_inc(wq_ready, 1)
            e.wait_ge(wkT_hi_s, p + 1)
            e.tensor_tensor(wkT_l[:, :, :], wkT_raw[:, :, :], wkT_h[:, :, :], ALU.subtract).then_inc(wkT_ready, 1)

        def xa_pool_wv(e, i):
            e.wait_ge(wv_hi_s, i + 1)
            e.tensor_tensor(wv_l[:, :, :], wv_raw[:, :, :], wv_h[:, :, :], ALU.subtract).then_inc(wv_ready, 1)

        def xa_dve_scores(e, i, j):
            bb = slice(2 * j, 2 * j + 2)
            e.wait_ge(s_ps, i * 4 + (j + 1))
            e.wait_ge(rkB_in[j], i * 32 + 32)
            e.tensor_tensor(sc[:, bb, :], ps[:, 4 + j % 2, :].rearrange("p (b n) -> p b n", b=2), rkB[:, bb, :],
                            ALU.mult).then_inc(s_ready, 1)
            e.wait_ge(s_ready, i * 4 + (j + 1))
            e.tensor_reduce(nmx[:, 0, bb], sc[:, bb, :], AX.X, ALU.max, negate=True).then_inc(mx_ready, 1)
            e.wait_ge(mx_ready, i * 4 + (j + 1))
            e.tensor_tensor(nmx[:, 1, bb], nmx[:, 0, bb], rq[:, bb], ALU.mult).then_inc(nmx_ready, 1)

        def xa_dve_norm(e, i, j):
            bb = slice(2 * j, 2 * j + 2)
            e.wait_ge(p_ready, i * 4 + (j + 1))
            e.reciprocal(rsm[:, bb], sm[:, bb]).then_inc(rsm_ready, 1)
            e.wait_ge(rsm_ready, i * 4 + (j + 1))
            e.tensor_tensor(sc[:, bb, :], sc[:, bb, :], rsm[:, bb].unsqueeze(2).to_broadcast([P, 2, SKV]),
                            ALU.mult).then_inc(pn_ready, 1)

        def xa_act_rms(e, p):
            e.wait_ge(ss_ps, p + 1)
            e.activation(rms[:, :], ps[:, 2, 0:B], ACT.Sqrt, bias=eps[:, 0:1]).then_inc(rms_ready, 1)

        def xa_dve_rq(e, p):
            e.wait_ge(rms_ready, p + 1)
            e.reciprocal(rq[:, :], rms[:, :]).then_inc(rq_ready, 1)

        def xa_dve_qsplit(e, p, k):
            e.wait_ge(qn_hi_s, p * 2 + (k + 1))
            e.scalar_tensor_tensor(qn_l[:, k, :], ps[:, k, :], gqk[:, 2:3], qn_h[:, k, :], ALU.mult, ALU.subtract)\
                .then_inc(qn_split, 1)

        def xa_dve_u(e, i, j):
            e.wait_ge(u_hi_s, i * 4 + (j + 1))
            r = lambda a: a[:, :, 2 * j:2 * j + 2, :, :].rearrange("p c b k q -> p c (b k q)")
            e.tensor_tensor(r(u_l), ps[:, 4 + j % 2, :].rearrange("p (c n) -> p c n", c=CC), r(u_h),
                            ALU.subtract).then_inc(u_ready, 1)

        def xa_dve_ao(e, i):
            for k in range(2):
                e.wait_ge(ao_ps, i * 2 + (k + 1))
                e.tensor_copy(aoT[:, bass.ds(i * 2 + k, 1), :], ps[:, 6 + k:7 + k, :]).then_inc(ao_ready, 1)

        def xa_pe_q(e, p, k):
            e.wait_ge(wq_ready, p + 1)
            for c in range(DC):
                m = mm3(ps[:, k, :], wq_h[:, c, hcol(k)], wq_l[:, c, hcol(k)], xT_hi[:, c, :], xT_lo[:, c, :],
                        c == 0, c == DC - 1)
            m.then_inc(q_ps, 1)

        def xa_pe_ss(e, p):
            e.wait_ge(sq_ready, p * 2 + 2)
            for b in range(B):
                m = e.matmul(ps[:, 2, b:b + 1], sq[:, b, :, :].rearrange("p k q -> p (k q)"), ones[:, 0:1],
                             start=True, stop=True)
            m.then_inc(ss_ps, 1)

        def xa_pe_qp(e, p):
            e.wait_ge(wkT_ready, p + 1)
            e.wait_ge(qn_split, p * 2 + 2)
            for k in range(2):
                if k == 1:
                    e.wait_ge(rms_ready, p + 1)
                for c in range(CC):
                    mm3(ps[:, 2 * k + c, :], wkT_h[:, k, hcol(c)], wkT_l[:, k, hcol(c)], qn_h[:, k, :],
                        qn_l[:, k, :]).then_inc(qp_ps, 1)

        def xa_pe_scores(e, i, j):
            if j == 0:
                e.wait_ge(qp_ready, i * 4 + 4)
            if j >= 2:
                e.wait_ge(s_ready, i * 4 + (j - 1))
            for n, b in enumerate((2 * j, 2 * j + 1)):
                for c in range(CC):
                    m = e.matmul(ps[:, 4 + j % 2, n * SKV:(n + 1) * SKV],
                                 qpT[:, c, b, :, :].rearrange("p k q -> p (k q)"), ctxT[:, c, kvb(b)],
                                 start=c == 0, stop=c == CC - 1)
            m.then_inc(s_ps, 1)

        def xa_pe_pT(e, i, j):
            e.wait_ge(pn_ready, i * 4 + (j + 1))
            if j >= 2:
                e.wait_ge(pT_ready, i * 4 + (j - 1))
            for n, b in enumerate((2 * j, 2 * j + 1)):
                for t in range(KPB):
                    at = (n * KPB + t) * P
                    m = e.transpose(ps[:, 6 + j % 2, at:at + P], sc[:, b, t * P:(t + 1) * P], ident[:, :])
            m.then_inc(pT_ps, 1)

        def xa_pe_u(e, i, j):
            e.wait_ge(pT_ready, i * 4 + (j + 1))
            if j < 2:
                e.wait_ge(s_ready, i * 4 + (j + 3))
            else:
                e.wait_ge(u_ready, i * 4 + (j - 1))
            for c in range(CC):
                for n, b in enumerate((2 * j, 2 * j + 1)):
                    at = (c * 2 + n) * P
                    for t in range(KPB):
                        m = e.matmul(ps[:, 4 + j % 2, at:at + P], ctx[:, b * KPB + t, hcol(c)], pT[:, b, t, :],
                                     start=t == 0, stop=t == KPB - 1)
            m.then_inc(u_ps, 1)

        def xa_pe_ao(e, i):
            e.wait_ge(wv_ready, i + 1)
            e.wait_ge(u_ready, i * 4 + 4)
            for k in range(2):
                for c in range(CC):
                    m = mm3(ps[:, 6 + k, :], wv_h[:, c, hcol(k)], wv_l[:, c, hcol(k)],
                            u_h[:, c, :, k, :], u_l[:, c, :, k, :], c == 0, c == CC - 1)
                m.then_inc(ao_ps, 1)

        K_, Q_, V_, G_ = range(4)

        def la_act_split(e, n, p):
            e.wait_ge(lw_in[n], p * 16 + 16)
            e.activation(lw_h[n][:, :, :], lw_raw[n][:, :, :], ACT.Copy).then_inc(lw_hi_s[n], 1)

        def la_pool_split(e, n, p):
            e.wait_ge(lw_hi_s[n], p + 1)
            e.tensor_tensor(lw_l[n][:, :, :], lw_raw[n][:, :, :], lw_h[n][:, :, :], ALU.subtract).then_inc(lw_ready[n], 1)

        def la_proj(e, n, k, bank):
            for c in range(DC):
                m = mm3(ps[:, bank, :], lw_h[n][:, c, hcol(k)], lw_l[n][:, c, hcol(k)], xT_hi[:, c, :], xT_lo[:, c, :],
                        c == 0, c == DC - 1)
            return m

        def la_pe(e, i):
            for n in (K_, Q_):
                e.wait_ge(lw_ready[n], i + 1)
                for k in range(2):
                    la_proj(e, n, k, 2 * n + k).then_inc(kq_ps, 1)
            e.wait_ge(lw_ready[V_], i + 1)
            e.wait_ge(ao_ready, i * 2 + H)
            for t in range(TT):
                tk = slice(t * P, (t + 1) * P)
                for c in range(DC):
                    m = mm3(ps[:, 4 + t // 2, (t % 2) * 2 * P:(t % 2 + 1) * 2 * P], xT_hi[:, c, tk], xT_lo[:, c, tk],
                            lw_h[V_][:, c, :], lw_l[V_][:, c, :], c == 0, c == DC - 1)
                if t % 2:
                    m.then_inc(v_ps, 1)
                if t == 1:
                    e.wait_ge(kq_sq_ready, i * 4 + 4)
                    for n in range(4):
                        for s in range(TT):
                            m = e.matmul(ps[:, 0, n * TT + s:n * TT + s + 1], kq_sq[:, n, s * P:(s + 1) * P], ones[:, 0:1],
                                         start=True, stop=True)
                    m.then_inc(kq_ss_ps, 1)
            e.wait_ge(lw_ready[G_], i + 1)
            la_proj(e, G_, 0, 6).then_inc(og_ps, 1)
            for k in range(2):
                e.wait_ge(rq_diag_ready, i * 2 + (k + 1))
                e.matmul(ps[:, 2 + k, :], ones[:, :], rq_diag[:, k, :, :].rearrange("p t n -> p (t n)"),
                         start=True, stop=True).then_inc(rqB_ps, 1)
            la_proj(e, G_, 1, 7).then_inc(og_ps, 1)
            for k in range(2):
                e.wait_ge(q_n, i * 2 + (k + 1))
                for t in range(TT):
                    tk = slice(t * P, (t + 1) * P)
                    m = e.matmul(ps[:, k, tk], kq[:, k, tk], kq[:, 2 + k, tk], start=True, stop=True)
                m.then_inc(at_ps, 1)
            e.wait_ge(v_ready, i * 2 + 2)
            for k in range(2):
                e.wait_ge(at_ready, i * 2 + (k + 1))
                for t in range(TT):
                    tk = slice(t * P, (t + 1) * P)
                    m = e.matmul(ps[:, 4 + k, tk], vt[:, t, hcol(k)], at[:, k, tk], start=True, stop=True)
                m.then_inc(o_ps, 1)
            e.wait_ge(sg_ready, i * 2 + 2)

        def la_act(e, i, more):
            for n in range(4):
                e.wait_ge(kq_ps, i * 4 + (n + 1))
                bias = kq_b[:, n // 2, bass.ds(i * 2 + n % 2, 1)]
                e.activation(kq_sq[:, n, :], ps[:, n, :], ACT.Square, bias=bias, scale=RSD)
                e.activation(kq[:, n, :], ps[:, n, :], ACT.Identity, bias=bias, scale=RSD).then_inc(kq_sq_ready, 1)
            if more:
                la_act_split(e, K_, i + 1)
            e.wait_ge(kq_ss_ps, i + 1)
            e.activation(kq_std[:, :, :].rearrange("p n t -> p (n t)"), ps[:, 0, 0:4 * TT], ACT.Sqrt).then_inc(kq_norm, 1)
            if more:
                la_act_split(e, Q_, i + 1)
                e.wait_ge(v_ps, i * 2 + 2)
                la_act_split(e, V_, i + 1)
            for k in range(2):
                e.wait_ge(og_ps, i * 2 + (k + 1))
                e.activation(sg[:, k, :], ps[:, 6 + k, :], ACT.Silu).then_inc(sg_ready, 1)
            if more:
                la_act_split(e, G_, i + 1)

        def la_dve(e, i):
            for g in range(2):
                e.wait_ge(v_ps, i * 2 + (g + 1))
                e.tensor_tensor(vt[:, 2 * g:2 * g + 2, :], ps[:, 4 + g, :].rearrange("p (t n) -> p t n", t=2),
                                v_bias[:, bass.ds(i * 2 * P, 2 * P)].unsqueeze(1).to_broadcast([P, 2, 2 * P]),
                                ALU.add).then_inc(v_biased, 1)
                if g == 0:
                    e.wait_ge(kq_norm, i + 1)
                    e.tensor_scalar(kq_std[:, :, :], kq_std[:, :, :], L2_EPS, None, ALU.max).then_inc(kq_guard, 1)
                    e.wait_ge(kq_guard, i + 1)
                    e.reciprocal(kq_r[:, :, :], kq_std[:, :, :]).then_inc(kq_recip, 1)
                    e.wait_ge(kq_recip, i + 1)
                    for k in range(2):
                        e.tensor_tensor(rq_diag[:, k, :, :], ident[:, :].unsqueeze(1).to_broadcast([P, TT, P]),
                                        kq_r[:, 2 + k, :].unsqueeze(2).to_broadcast([P, TT, P]), ALU.mult)\
                            .then_inc(rq_diag_ready, 1)
                    e.tensor_tensor(v_scale[:, :, :], kq_r[:, 0:2, :],
                                    beta[:, :, bass.ds(i * 2, 2)].rearrange("p t h -> p h t"), ALU.mult).then_inc(v_scale_ready, 1)
                    e.wait_ge(v_scale_ready, i + 1)
                e.wait_ge(v_biased, i * 2 + (g + 1))
                for t in (2 * g, 2 * g + 1):
                    v = vt[:, t, :].rearrange("p (h n) -> p h n", h=2)
                    m = e.tensor_tensor(v, v, v_scale[:, :, t].unsqueeze(2).to_broadcast([P, 2, P]), ALU.mult)
                m.then_inc(v_ready, 1)
            for k in range(2):
                e.wait_ge(rqB_ps, i * 2 + (k + 1))
                e.tensor_tensor(kq[:, 2 + k, :], kq[:, 2 + k, :], ps[:, 2 + k, :], ALU.mult).then_inc(q_n, 1)
            for k in range(2):
                e.wait_ge(at_ps, i * 2 + (k + 1))
                e.tensor_tensor(at[:, k, :].rearrange("p (t n) -> p t n", t=TT),
                                ps[:, k, :].rearrange("p (t n) -> p t n", t=TT),
                                mask[:, :].unsqueeze(1).to_broadcast([P, TT, P]), ALU.mult).then_inc(at_ready, 1)
            for k in range(2):
                e.wait_ge(o_ps, i * 2 + (k + 1))
                e.wait_ge(sg_ready, i * 2 + (k + 1))
                e.tensor_tensor(aoT[:, bass.ds(i * 2 + k, 1), :], ps[:, 4 + k:5 + k, :], sg[:, k:k + 1, :],
                                ALU.mult).then_inc(ao_ready, 1)

        NSH = 2 * TT

        def fcs(c):
            return slice(c * P, c * P + FW[c])

        def ex_up(lh, ll, k):
            for n, s in ((0, h1_ps), (1, h3_ps)):
                f = slice(n * FF, (n + 1) * FF)
                for c in range(DC):
                    m = mm3(ps[:, 2 * n + k, 0:FF], lh(c), ll(c), w13_h[:, k, c, f], w13_l[:, k, c, f],
                            c == 0, c == DC - 1)
                m.then_inc(s, 1)

        def ex_hT(e, k, u):
            e.wait_ge(h_ready, u + 1)
            e.wait_ge(hT_ready, u)
            for c in range(FC):
                m = e.transpose(ps[0:FW[c], 5, c * P:(c + 1) * P], h[:, k, fcs(c)], ident[:, :])
            m.then_inc(hT_ps, 1)

        def ex_down(k, bank, first=True, last=True):
            for c in range(FC):
                r = slice(0, FW[c])
                m = mm3(ps[:, bank, :], hT_h[r, k, c, :], hT_l[r, k, c, :], w2_h[r, k, c, :], w2_l[r, k, c, :],
                        first and c == 0, last and c == FC - 1)
            return m

        def ex_act_w13(e, k, n):
            e.wait_ge(w13_in[k], n * 32)
            e.activation(w13_h[:, k, :, :], w13_raw[:, k, :, :], ACT.Copy).then_inc(w13_hi_s, 1)

        def ex_act_w2(e, k, n):
            e.wait_ge(w2_in[k], n * 32)
            e.activation(w2_h[:, k, :, :], w2_raw[:, k, :, :], ACT.Copy).then_inc(w2_hi_s, 1)

        def ex_dve_w13(e, k, n):
            e.wait_ge(w13_hi_s, n)
            e.tensor_tensor(w13_l[:, k, :, :], w13_raw[:, k, :, :], w13_h[:, k, :, :], ALU.subtract).then_inc(w13_ready, 1)

        def ex_pool_w2(e, k, n):
            e.wait_ge(w2_hi_s, n)
            e.tensor_tensor(w2_l[:, k, :, :], w2_raw[:, k, :, :], w2_h[:, k, :, :], ALU.subtract).then_inc(w2_ready, 1)

        def ex_act_silu(e, k, u):
            e.wait_ge(h1_ps, u + 1)
            e.activation(h1[:, k, :], ps[:, k, 0:FF], ACT.Silu).then_inc(h1_ready, 1)

        def ex_dve_h(e, k, u):
            e.wait_ge(h1_ready, u + 1)
            e.wait_ge(h3_ps, u + 1)
            e.tensor_tensor(h[:, k, :], h1[:, k, :], ps[:, 2 + k, 0:FF], ALU.mult).then_inc(h_ready, 1)

        def ex_act_hT(e, k, u):
            e.wait_ge(hT_ps, u + 1)
            for c in range(FC):
                r = slice(0, FW[c])
                last = e.activation(hT_h[r, k, c, :], ps[r, 5, c * P:(c + 1) * P], ACT.Copy)
            last.then_inc(hT_hi_s, 1)

        def ex_dve_hT(e, k, u):
            e.wait_ge(hT_hi_s, u + 1)
            for c in range(FC):
                r = slice(0, FW[c])
                last = e.tensor_tensor(hT_l[r, k, c, :], ps[r, 5, c * P:(c + 1) * P], hT_h[r, k, c, :], ALU.subtract)
            last.then_inc(hT_ready, 1)

        def ex_act_xT(e, m, k):
            e.wait_ge(xeT_ps, m + 1)
            e.activation(xeT_h[:, k, :, :].rearrange("p c n -> p (c n)"), ps[:, 4, :], ACT.Copy).then_inc(xeT_hi_s, 1)

        def ex_dve_xT(e, m, k):
            e.wait_ge(xeT_hi_s, m + 1)
            e.tensor_tensor(xeT_l[:, k, :, :].rearrange("p c n -> p (c n)"), ps[:, 4, :],
                            xeT_h[:, k, :, :].rearrange("p c n -> p (c n)"), ALU.subtract).then_inc(xeT_ready, 1)

        def ex_pe_xT(e, k, n):
            e.wait_ge(xe_in[k], n * 16)
            for c in range(DC):
                last = e.transpose(ps[:, 4, c * P:(c + 1) * P], xe[:, k, c * P:(c + 1) * P], ident[:, :])
            last.then_inc(xeT_ps, 1)

        def ex_pe_down(e, m, k):
            e.wait_ge(hT_ready, m + (NSH + 1))
            e.wait_ge(w2_ready, m + 3)
            ex_down(k, 6 + k).then_inc(d_ps, 1)

        def ex_pe(e, i, k, peeled=False):
            m = i * 2 + k
            e.wait_ge(w13_ready, m + 3)
            e.wait_ge(xeT_ready, m + 1)
            e.wait_ge(h_ready, m + (NSH - 1))
            ex_up(lambda c: xeT_h[:, k, c, :], lambda c: xeT_l[:, k, c, :], k)
            ex_pe_xT(e, 1 - k, i + (k + 1))
            if not (peeled and k == 0):
                ex_pe_down(e, m - 1, 1 - k)
            ex_hT(e, k, m + NSH)

        def ex_act(e, i, k, peeled=False):
            m = i * 2 + k
            e.wait_ge(h3_ps, m + NSH)
            ex_act_w13(e, 1 - k, i + (k + 2))
            if not peeled:
                e.wait_ge(d_ps, m - 1)
            ex_act_w2(e, k, i + 2)
            ex_act_silu(e, k, m + NSH)
            ex_act_xT(e, m + 1, 1 - k)
            ex_act_hT(e, k, m + NSH)

        def ex_dve_ob(e, m, k, n):
            e.wait_ge(d_ps, m + 1)
            if n is not None:
                e.wait_ge(ob_out[k], n * 16)
            e.tensor_copy(ob[:, k, :], ps[:, 6 + k, :]).then_inc(ob_ready, 1)

        def ex_dve(e, i, k, peeled=False, slot_free=False):
            m = i * 2 + k
            ex_dve_w13(e, 1 - k, m + 4)
            ex_dve_h(e, k, m + NSH)
            ex_dve_xT(e, m + 1, 1 - k)
            if not (peeled and k == 0):
                ex_dve_ob(e, m - 1, 1 - k, None if peeled or slot_free else i + (k - 1))
            ex_dve_hT(e, k, m + NSH)

        def ex_gather_rows(e, m, k):
            e.tensor_copy(idx_col[:, k:k + 1], tl[:, bass.ds(m, 1)]).then_inc(idx_ready, 1)
            e.wait_ge(idx_ready, m + 1)

        def ex_gather(e, k):
            e.indirect_dma_start(xe[:, k, :], None, xn_dram.ap(), bass.IndirectOffsetOnAxis(ap=idx_col[:, k:k + 1], axis=0))\
                .then_inc(xe_in[k], 16)

        def ex_pool(e, i, k):
            m = i * 2 + k
            e.wait_ge(xeT_ps, m + 1)
            ex_gather_rows(e, m + 2, k)
            ex_pool_w2(e, k, m + 3)
            ex_gather(e, k)

        def load_w13(e, k, w1_ap, w3_ap):
            e.dma_start(w13_raw[:, k, :, 0:FF], w1_ap).then_inc(w13_in[k], 16)
            e.dma_start(w13_raw[:, k, :, FF:2 * FF], w3_ap).then_inc(w13_in[k], 16)

        def load_w2(e, k, whole_ap, rest_ap):
            e.dma_start(w2_raw[:, k, 0:FC - 1, :], whole_ap).then_inc(w2_in[k], 16)
            e.dma_start(w2_raw[0:FW[-1], k, FC - 1, :], rest_ap).then_inc(w2_in[k], 16)

        w1_r = w1.rearrange("e (c p) f -> e p c f", p=P)
        w3_r = w3.rearrange("e (c p) f -> e p c f", p=P)
        w2_r = w2[:, 0:(FC - 1) * P, :].rearrange("e (c p) d -> e p c d", p=P)
        w2_t = w2[:, (FC - 1) * P:FF, :]

        def ex_load(e, m, k):
            ex = e.value_load(lst[0:1, bass.ds(m, 1)], min_val=0, max_val=E - 1)
            e.wait_ge(w13_ready, m + 1)
            load_w13(e, k, w1_r[bass.ds(ex, 1)].rearrange("e p c f -> p (e c) f"),
                     w3_r[bass.ds(ex, 1)].rearrange("e p c f -> p (e c) f"))
            e.wait_ge(w2_ready, m + 1)
            load_w2(e, k, w2_r[bass.ds(ex, 1)].rearrange("e p c d -> p (e c) d"),
                    w2_t[bass.ds(ex, 1)].rearrange("e p d -> p (e d)"))

        def ex_store(e, m, k):
            e.wait_ge(ob_ready, m + 1)
            e.dma_start(ob_dram.ap().rearrange("(n p) d -> n p d", p=P)[bass.ds(m, 1)].rearrange("n p d -> p (n d)"),
                        ob[:, k, :]).then_inc(ob_out[k], 16)

        def ex_sp(e, i, k, peeled=False):
            m = i * 2 + k
            ex_load(e, m + 2, k)
            if not (peeled and k == 0):
                ex_store(e, m - 1, 1 - k)

        def last_turn(e):
            e.wait_ge(small_dve, DV_LISTS)
            return e.value_load(lst[0:1, ML:ML + 1], min_val=T * TOP_K // P // 2 - 1, max_val=MI // 2 - 1)

        rsm_ready, rq_ready, rms_ready, mx_ready = sem("rsm_ready"), sem("rq_ready"), sem("rms_ready"), sem("mx_ready")
        ln_var_ready, ln_std_ready, rk_sqrt = sem("ln_var_ready"), sem("ln_std_ready"), sem("rk_sqrt")

        ob_cleared, ob_stored = sem("ob_cleared"), sem("ob_stored")
        OZ = MI // (HP - 1)
        ob_rows = ob_dram.ap().rearrange("(n p) d -> p n d", p=P)
        lw_r = [w.rearrange("(c p) (h n) -> h p c n", p=P, n=2 * P) for w in (kwT, qwT, vwT, ogwT)]

        block = stack.enter_context(nc.Block())

        @block.sync
        def _(e):
            def load_ctxT(g):
                kv = slice(g * G4, (g + 1) * G4)
                e.dma_start(ctxT[:, :, kv], ctxT_in_.rearrange("(c p) n -> p c n", p=P)[:, :, kv]).then_inc(ctxT_in[g], 16)

            def load_wk(g):
                kv = slice(g * G4, (g + 1) * G4)
                e.dma_start(wk_raw[:, :, kv], Wk.rearrange("(c p) n -> p c n", p=P)[:, :, kv]).then_inc(wk_in[g], 16)

            load_wk(0)
            load_ctxT(0)
            load_ctxT(1)
            e.dma_start(x[:, :, :], x_in.rearrange("(t p) d -> p t d", p=P)).then_inc(x_in_s, 16)
            load_ctxT(2)
            load_ctxT(3)
            e.dma_start(gqk[:, 0:1], gq.rearrange("(p a) -> p a", a=1)).then_inc(g_in_s, 16)
            e.dma_start(gqk[:, 1:2], gk.rearrange("(p a) -> p a", a=1)).then_inc(g_in_s, 16)
            for g in range(1, 4):
                load_wk(g)
            wq_r = Wq.rearrange("(c p) (h n) -> h p c n", p=P, n=2 * P)
            wkT_r = WkT.rearrange("(h k p) c -> h p k c", k=2, p=P)
            wv_r = Wv.rearrange("(c p) (h n) -> h p c n", p=P, n=2 * P)
            e.dma_start(wq_raw[:, :, :], wq_r[0]).then_inc(wq_in, 16)
            e.dma_start(wkT_raw[:, :, :], wkT_r[0]).then_inc(wkT_in, 16)
            e.dma_start(wv_raw[:, :, :], wv_r[0]).then_inc(wv_in, 16)
            e.dma_start(ctx[:, :, :], ctx_in.rearrange("(t p) c -> p t c", p=P)).then_inc(ctx_in_s, 16)
            e.wait_ge(rkT_ready, 2)
            for n in range(2):
                e.dma_start(rk_dram.ap().rearrange("h (n t p) -> n t h p", n=2, p=P)[n], rkT[:, n, :]).then_inc(scratch_io, 16)
            e.wait_ge(scratch_io, IO_RK)

            rk_r = rk_dram.ap().rearrange("(h k) (j n) -> h k j n", k=2, j=JB)

            def rk_load(p, j):
                for k in range(2):
                    src = rk_r[bass.ds(p, 1), k, j, :]
                    e.dma_start(rkB[k * SQ:(k + 1) * SQ, 2 * j:2 * j + 2, :].rearrange("p b n -> p (b n)"),
                                src.to_broadcast([SQ, 2 * SKV])).then_inc(rkB_in[j], 16)

            for j in range(JB):
                rk_load(0, j)
            with e.Fori(1, HP) as p:
                e.wait_ge(wq_ready, p)
                e.dma_start(wq_raw[:, :, :], wq_r[bass.ds(p, 1)].rearrange("h p c n -> p (h c) n")).then_inc(wq_in, 16)
                e.wait_ge(wkT_ready, p)
                e.dma_start(wkT_raw[:, :, :], wkT_r[bass.ds(p, 1)].rearrange("h p k c -> p (h k) c")).then_inc(wkT_in, 16)
                e.wait_ge(wv_ready, p)
                e.dma_start(wv_raw[:, :, :], wv_r[bass.ds(p, 1)].rearrange("h p c n -> p (h c) n")).then_inc(wv_in, 16)
                e.dma_start(ob_rows[:, bass.ds(p * OZ - OZ, OZ), :], zeros[:, :].unsqueeze(1).to_broadcast([P, OZ, D]))\
                    .then_inc(ob_cleared, 16)
                for j in range(JB):
                    e.wait_ge(s_ready, p * 4 + (j - 3))
                    rk_load(p, j)
            wo_load(e, 0, Wo)
            with e.Fori(1, HP) as p:
                for n in range(4):
                    e.wait_ge(lw_ready[n], p)
                    e.dma_start(lw_raw[n][:, :, :], lw_r[n][bass.ds(p, 1)].rearrange("h p c n -> p (h c) n"))\
                        .then_inc(lw_in[n], 16)
            wo_load(e, 1, owT)
            e.wait_ge(xn_ready, 3 * TT)
            e.dma_start(xn_dram.ap().rearrange("(t p) d -> p t d", p=P), xn_c[:, :, :]).then_inc(scratch_io, 16)
            e.dma_start(tl_dram.ap().rearrange("(n s) a -> n (s a)", s=P), zeros[0:ML, 0:P]).then_inc(scratch_io, 16)
            e.wait_ge(tl_scattered, 16 * TT * TOP_K)
            e.dma_start(tl_rows[0:ML, :], tl_dram.ap().rearrange("(n s) a -> n (s a)", s=P)).then_inc(scratch_io, 16)
            last_i = last_turn(e)
            ex_load(e, 0, 0)
            ex_load(e, 1, 1)
            e.wait_ge(ob_cleared, 16 * (HP - 1))
            ex_sp(e, 0, 0, True)
            ex_sp(e, 0, 1, True)
            with e.Fori(1, last_i + 1) as i:
                ex_sp(e, i, 0)
                ex_sp(e, i, 1)
            ex_store(e, last_i * 2 + 1, 1)
            e.wait_ge(ob_out[0], last_i * 16 + 16)
            e.wait_ge(ob_out[1], last_i * 16 + 16)
            e.sem_inc(ob_stored, 1)
            for t in range(TT):
                e.wait_ge(gb_used, TOP_K * (t + 1))
                e.dma_start(out[t * P:(t + 1) * P, :], x[:, t, :]).then_inc(out_done, 16)
            e.wait_ge(out_done, 16 * TT)

        @block.gpsimd
        def _(e):
            e.memset(ident[:, :], 0.0).then_inc(consts, 1)
            e.memset(ones[:, :], 1.0).then_inc(consts, 1)
            e.memset(zeros[:, :], 0.0).then_inc(consts, 1)
            e.memset(eps[:, :], LN_EPS).then_inc(consts, 1)
            e.wait_ge(consts, 4)
            e.affine_select(out=ident[:, :], in_=ident[:, :], compare_op=ALU.not_equal, fill=1.0, base=0,
                            pattern=[[-1, P]], channel_multiplier=1).then_inc(consts, 1)
            for g in range(4):
                kv = slice(g * G4, (g + 1) * G4)
                e.wait_ge(wk_hi_s, g + 1)
                e.tensor_tensor(wk_l[:, :, kv], wk_raw[:, :, kv], wk_h[:, :, kv], ALU.subtract).then_inc(wk_ready, 1)
            xa_pool_weights(e, 0)
            with e.Fori(0, HP - 1) as i:
                xa_pool_weights(e, i + 1)
                xa_pool_wv(e, i)
            xa_pool_wv(e, HP - 1)
            wo_pool(e, 0)

            e.wait_ge(ao_ready, H)
            e.memset(mask[:, :], 1.0).then_inc(consts, 1)
            e.wait_ge(consts, 6)
            e.affine_select(out=mask[:, :], in_=mask[:, :], compare_op=ALU.is_ge, fill=0.0, base=0,
                            pattern=[[1, P]], channel_multiplier=-1).then_inc(consts, 1)
            e.wait_ge(consts, 7)
            e.affine_select(out=mask[:, SQ:P], in_=mask[:, SQ:P], compare_op=ALU.is_ge, fill=0.0, base=-SQ,
                            pattern=[[0, P - SQ]], channel_multiplier=1).then_inc(mask_ready, 1)
            e.wait_ge(small_hi, SP_BETA)
            e.tensor_tensor(bw_l[:, :, :], bw_raw[:, :, :], bw_h[:, :, :], ALU.subtract).then_inc(small_lo, 1)
            for n in range(4):
                la_pool_split(e, n, 0)
            with e.Fori(0, HP - 1) as i:
                for n in range(4):
                    la_pool_split(e, n, i + 1)
            e.wait_ge(ao_ready, 2 * H)
            e.memset(w2_raw[FW[-1]:P, :, FC - 1, :], 0.0).then_inc(consts, 1)
            e.wait_ge(consts, 8)
            wo_pool(e, 1)

            e.wait_ge(x_ready, 2 * TT)
            e.memset(below[:, :], 1.0).then_inc(pool_consts, 1)
            e.iota(iota_e[:, :], [[1, ML]], base=0, channel_multiplier=0, allow_small_or_imprecise_dtypes=True).then_inc(pool_consts, 1)
            e.iota(part_i[:, 0:1], [[0, 1]], base=0, channel_multiplier=1).then_inc(pool_consts, 1)
            e.iota(tok_id[:, :], [[P, TT]], base=0, channel_multiplier=1, allow_small_or_imprecise_dtypes=True).then_inc(pool_consts, 1)
            e.memset(strict[:, :], 1.0).then_inc(pool_consts, 1)
            e.wait_ge(pool_consts, 5)
            e.affine_select(out=below[:, :], in_=below[:, :], compare_op=ALU.is_gt, fill=0.0, base=0,
                            pattern=[[CT, E]], channel_multiplier=-1).then_inc(pool_consts, 1)
            e.affine_select(out=strict[:, :], in_=strict[:, :], compare_op=ALU.is_gt, fill=0.0, base=0,
                            pattern=[[1, P]], channel_multiplier=-1).then_inc(pool_consts, 1)
            e.wait_ge(small_hi, SP_ROUTER)
            e.tensor_tensor(gw_l[:, :, :], gw_raw[:, :, :], gw_h[:, :, :], ALU.subtract).then_inc(small_lo, 1)
            ex_pool_w2(e, 0, 1)
            ex_pool_w2(e, 1, 2)
            e.wait_ge(scratch_io, IO_CLEARED)
            e.wait_ge(small_dve, DV_SLOTS)
            for t in range(TT):
                for k in range(TOP_K):
                    e.indirect_dma_start(tl_dram.ap(), bass.IndirectOffsetOnAxis(ap=slot_i[:, t, k:k + 1], axis=0),
                                         tok_id[:, t:t + 1], None).then_inc(tl_scattered, 16)
            last_i = last_turn(e)
            e.wait_ge(scratch_io, IO_CLEARED)
            e.wait_ge(small_dve, DV_TOKENS)
            for k in range(2):
                ex_gather_rows(e, k, k)
                ex_gather(e, k)
            ex_pool(e, 0, 0)
            ex_pool(e, 0, 1)
            with e.Fori(1, last_i + 1) as i:
                ex_pool(e, i, 0)
                ex_pool(e, i, 1)
            e.wait_ge(ob_stored, 1)
            for t in range(TT):
                for k in range(TOP_K):
                    n = t * TOP_K + k
                    if n >= GB:
                        e.wait_ge(gb_used, n - GB + 1)
                    e.indirect_dma_start(gb[:, n % GB, :], None, ob_dram.ap(),
                                         bass.IndirectOffsetOnAxis(ap=slot_i[:, t, k:k + 1], axis=0)).then_inc(gb_in[n % GB], 16)

        @block.scalar
        def _(e):
            e.wait_ge(consts, 5)
            def ctxT_hi(g):
                kv = slice(g * G4, (g + 1) * G4)
                e.wait_ge(ctxT_in[g], 16)
                e.activation(cT_h[:, :, kv], ctxT[:, :, kv], ACT.Copy).then_inc(cT_hi_s, 1)

            def wk_hi(g):
                kv = slice(g * G4, (g + 1) * G4)
                e.wait_ge(wk_in[g], 16)
                e.activation(wk_h[:, :, kv], wk_raw[:, :, kv], ACT.Copy).then_inc(wk_hi_s, 1)

            def squares(g, t):
                e.wait_ge(k_ps, g * KT + (t + 1))
                e.wait_ge(sqk_free, g * KT + (t + 3))
                e.activation(sqk[:, t % 2, :], ps[:, 4 + t % 4, :], ACT.Square, scale=RSD).then_inc(sqk_ready, 1)

            wk_hi(0)
            ctxT_hi(0)
            ctxT_hi(1)
            for t in range(KT):
                squares(0, t)
                if t in (1, 4):
                    ctxT_hi(2 + t // 4)
                if t in (6, 8, 10):
                    wk_hi(t // 2 - 2)
            layernorm_act(e, 0)
            xa_act_weights(e, 0)
            with e.Fori(1, 4) as g:
                for t in range(KT):
                    squares(g, t)
            e.wait_ge(small_dve, DV_SSK)
            e.activation(rk_ln[:, :, :], ssk[:, :, :], ACT.Sqrt, bias=eps[:, 0:1]).then_inc(rk_sqrt, 1)
            xa_act_q(e, 0, 0)
            e.wait_ge(small_ps, PS_RKT)
            for n in range(2):
                e.activation(rkT[:, n, :], ps[:, 6 + n, 0:P], ACT.Copy).then_inc(rkT_ready, 1)
            xa_act_q(e, 0, 1)
            xa_act_rms(e, 0)
            xa_act_qp(e, 0)

            def pair(i, more):
                if more:
                    xa_act_weights(e, i + 1)
                xa_act_exp(e, i, 0)
                xa_act_wv(e, i)
                for j in range(1, JB):
                    xa_act_exp(e, i, j)
                if more:
                    xa_act_q(e, i + 1, 0)
                    xa_act_q(e, i + 1, 1)
                    xa_act_rms(e, i + 1)
                xa_act_pT(e, i, 0)
                xa_act_pT(e, i, 1)
                xa_act_u(e, i, 0)
                xa_act_pT(e, i, 2)
                xa_act_u(e, i, 1)
                xa_act_pT(e, i, 3)
                xa_act_u(e, i, 2)
                xa_act_u(e, i, 3)
                if more:
                    xa_act_qp(e, i + 1)
            with e.Fori(0, HP - 1) as i:
                pair(i, True)
            pair(HP - 1, False)

            def lin_prefetch(e):
                for n in range(4):
                    e.dma_start(lw_raw[n][:, :, :], lw_r[n][0]).then_inc(lw_in[n], 16)
                e.dma_start(kq_b[:, 0, :], k_b.rearrange("(h p) -> p h", p=P), allow_slow_non_contiguous=True).then_inc(lin_in, 16)
                e.dma_start(kq_b[:, 1, :], q_b.rearrange("(h p) -> p h", p=P), allow_slow_non_contiguous=True).then_inc(lin_in, 16)
                e.dma_start(v_bias[:, :], v_b.rearrange("(a n) -> a n", a=1).to_broadcast([P, INNER])).then_inc(lin_in, 16)
                e.dma_start(ob_B[:, :], o_b.rearrange("(a n) -> a n", a=1).to_broadcast([P, D])).then_inc(lin_in, 16)
                e.dma_start(bb_B[:, :], b_b.rearrange("(a n) -> a n", a=1).to_broadcast([P, H])).then_inc(lin_in, 16)
                e.dma_start(bw_raw[:, :, :], bwT.rearrange("(c p) h -> p c h", p=P)).then_inc(lin_in, 16)

            wo_act(e, 0, lin_prefetch)
            e.wait_ge(lin_in, 96)
            e.activation(bw_h[:, :, :], bw_raw[:, :, :], ACT.Copy).then_inc(small_hi, 1)
            for n in range(4):
                la_act_split(e, n, 0)
            layernorm_act(e, 1)
            e.wait_ge(sp_dve, 1)
            e.activation(sp[:, 1, :], sp[:, 1, :], ACT.Exp).then_inc(sp_act, 1)
            e.wait_ge(sp_dve, 2)
            e.activation(sp[:, 3, :], sp[:, 2, :], ACT.Ln).then_inc(sp_act, 1)
            e.wait_ge(small_dve, DV_KQB)
            with e.Fori(0, HP - 1) as i:
                la_act(e, i, True)
            la_act(e, HP - 1, False)

            def moe_prefetch(e):
                for k in range(2):
                    load_w13(e, k, w1_r[E + k], w3_r[E + k])
                    load_w2(e, k, w2_r[E + k], w2_t[E + k])

            wo_act(e, 1, moe_prefetch)
            e.wait_ge(x_ready, 2 * TT)
            e.dma_start(gw_raw[:, :, :], gwT.rearrange("(c p) e -> p c e", p=P)).then_inc(moe_in, 16)
            layernorm_act(e, 2)
            e.wait_ge(moe_in, 16)
            e.activation(gw_h[:, :, :], gw_raw[:, :, :], ACT.Copy).then_inc(small_hi, 1)
            ex_act_w13(e, 0, 1)
            e.wait_ge(rt_dve, 1)
            for t in range(TT):
                last = e.activation(gate[:, t, :], ps[:, 4, t * E:(t + 1) * E], ACT.Exp, bias=r_small[:, 0, t:t + 1],
                                    accum_out=r_small[:, 1, t:t + 1])
            last.then_inc(rt_act, 1)
            ex_act_w13(e, 1, 1)
            e.wait_ge(consts, 8)
            ex_act_w2(e, 0, 1)
            ex_act_w2(e, 1, 1)
            for u in range(NSH):
                ex_act_silu(e, u % 2, u)
                if u >= 1:
                    ex_act_hT(e, (u - 1) % 2, u - 1)
                if u == NSH - 1:
                    last_act = last_turn(e)
                    ex_act_w13(e, 0, 2)
            ex_act_hT(e, 1, NSH - 1)
            e.wait_ge(shd_ps, TT)
            ex_act_xT(e, 0, 0)
            ex_act(e, 0, 0, True)
            ex_act(e, 0, 1, True)
            with e.Fori(1, last_act + 1) as i:
                ex_act(e, i, 0)
                ex_act(e, i, 1)

        @block.vector
        def _(e):
            def ctxT_lo(g):
                kv = slice(g * G4, (g + 1) * G4)
                e.wait_ge(cT_hi_s, g + 1)
                e.tensor_tensor(cT_l[:, :, kv], ctxT[:, :, kv], cT_h[:, :, kv], ALU.subtract).then_inc(cT_ready, 1)

            def sums(g, t):
                e.wait_ge(sqk_ready, g * KT + (t + 1))
                e.tensor_reduce(ssk[:, t, bass.ds(g * 4, 4)], sqk[:, t % 2, :].rearrange("p (h n) -> p h n", n=P),
                                AX.X, ALU.add).then_inc(sqk_free, 1)

            e.sem_inc(sqk_free, 4)
            ctxT_lo(0)
            ctxT_lo(1)
            for t in range(KT):
                sums(0, t)
                if t in (1, 4):
                    ctxT_lo(2 + t // 4)
            e.wait_ge(g_in_s, 32)
            e.tensor_tensor(gqk[:, 2:3], gqk[:, 0:1], gqk[:, 1:2], ALU.mult).then_inc(small_dve, 1)
            e.wait_ge(x_in_s, 16)
            layernorm_dve(e, 0, xn_a)
            layernorm_split_dve(e, 0)
            with e.Fori(1, 4) as g:
                for t in range(KT):
                    sums(g, t)
            e.wait_ge(sqk_free, 4 * KT + 4)
            e.sem_inc(small_dve, 1)
            e.wait_ge(rk_sqrt, 1)
            e.reciprocal(ssk[:, :, :], rk_ln[:, :, :]).then_inc(dve_step, 1)
            steps[0] += 1
            e.wait_ge(dve_step, steps[0])
            e.tensor_scalar(ssk[:, :, :], ssk[:, :, :], RSD, None, ALU.mult).then_inc(small_dve, 1)
            for k in range(2):
                xa_dve_qsplit(e, 0, k)
            xa_dve_rq(e, 0)

            def pair(i, more):
                e.wait_ge(rq_ready, i + 1)
                xa_dve_scores(e, i, 0)
                xa_dve_scores(e, i, 1)
                xa_dve_norm(e, i, 0)
                xa_dve_scores(e, i, 2)
                xa_dve_norm(e, i, 1)
                xa_dve_scores(e, i, 3)
                xa_dve_norm(e, i, 2)
                xa_dve_norm(e, i, 3)
                if more:
                    xa_dve_qsplit(e, i + 1, 0)
                    xa_dve_qsplit(e, i + 1, 1)
                    xa_dve_rq(e, i + 1)
                xa_dve_u(e, i, 0)
                for j in range(1, JB):
                    xa_dve_u(e, i, j)
                xa_dve_ao(e, i)
            with e.Fori(0, HP - 1) as i:
                pair(i, True)
            pair(HP - 1, False)
            wo_dve(e, 0)

            def add_y(n):
                for t in range(TT):
                    e.wait_ge(y_ps, TT * n + t + 1)
                    e.tensor_tensor(x[:, t, :], x[:, t, :], ps[:, t, :], ALU.add).then_inc(x_ready, 1)
                e.wait_ge(x_ready, TT * (n + 1))

            def step(ins):
                steps[0] += 1
                ins.then_inc(dve_step, 1)
                e.wait_ge(dve_step, steps[0])

            add_y(0)
            layernorm_dve(e, 1, xn_b)
            layernorm_split_dve(e, 1)
            e.wait_ge(lin_in, 96)
            e.tensor_scalar(kq_b[:, :, :], kq_b[:, :, :], RSD, None, ALU.mult).then_inc(small_dve, 1)
            e.wait_ge(small_ps, PS_BETA)
            step(e.tensor_tensor(sp[:, 0, :].rearrange("p (t h) -> p t h", h=H), ps[:, 4, 0:TT * H].rearrange("p (t h) -> p t h", h=H),
                                 bb_B[:, :].unsqueeze(1).to_broadcast([P, TT, H]), ALU.add))
            e.scalar_tensor_tensor(sp[:, 1, :], sp[:, 0, :], -1.0, sp[:, 0, :], ALU.mult, ALU.min).then_inc(sp_dve, 1)
            e.wait_ge(sp_act, 1)
            e.tensor_scalar(sp[:, 2, :], sp[:, 1, :], 1.0, None, ALU.add).then_inc(sp_dve, 1)
            e.wait_ge(sp_dve, 2)
            step(e.tensor_scalar(sp[:, 4, :], sp[:, 2, :], 1.0, None, ALU.subtract))
            step(e.scalar_tensor_tensor(sp[:, 5, :], sp[:, 4, :], 0.0, sp[:, 1, :], ALU.is_equal, ALU.mult))
            step(e.tensor_scalar(sp[:, 4, :], sp[:, 4, :], 1e-30, None, ALU.max))
            step(e.reciprocal(sp[:, 4, :], sp[:, 4, :]))
            step(e.tensor_tensor(sp[:, 4, :], sp[:, 4, :], sp[:, 1, :], ALU.mult))
            e.wait_ge(sp_act, 2)
            step(e.tensor_tensor(sp[:, 4, :], sp[:, 4, :], sp[:, 3, :], ALU.mult))
            step(e.tensor_tensor(sp[:, 4, :], sp[:, 4, :], sp[:, 5, :], ALU.add))
            step(e.scalar_tensor_tensor(beta[:, :, :].rearrange("p t h -> p (t h)"), sp[:, 0, :], 0.0, sp[:, 4, :], ALU.max, ALU.add))
            e.wait_ge(mask_ready, 1)
            with e.Fori(0, HP) as i:
                la_dve(e, i)
            for t in range(TT):
                step(e.tensor_tensor(x[:, t, :], x[:, t, :], ob_B[:, :], ALU.add))
            wo_dve(e, 1)
            add_y(1)

            layernorm_dve(e, 2, xn_c)
            layernorm_split_dve(e, 2)
            lg = ps[:, 4, 0:TT * E].rearrange("p (t n) -> p t n", n=E)
            e.wait_ge(small_ps, PS_LOGITS)
            e.tensor_reduce(r_small[:, 0, :], lg, AX.X, ALU.max, negate=True).then_inc(rt_dve, 1)
            ex_dve_w13(e, 0, 1)
            e.wait_ge(rt_act, 1)
            step(e.reciprocal(r_small[:, 2, :], r_small[:, 1, :]))
            step(e.tensor_tensor(gate[:, :, :], gate[:, :, :], r_small[:, 2, :].unsqueeze(2).to_broadcast([P, TT, E]), ALU.mult))
            for t in range(TT):
                e.max(top_w[:, t, :], gate[:, t, :]).then_inc(dve_step, 1)
            steps[0] += TT
            e.wait_ge(dve_step, steps[0])
            for t in range(TT):
                e.max_index(top_i[:, t, :], top_w[:, t, :], gate[:, t, :]).then_inc(dve_step, 1)
            steps[0] += TT
            e.wait_ge(dve_step, steps[0])
            step(e.tensor_copy(top_f[:, :, :], top_i[:, :, :]))
            e.wait_ge(pool_consts, 7)
            for t in range(TT):
                e.tensor_tensor(hot[:, t, :, :], iota_e[:, 0:E].unsqueeze(1).to_broadcast([P, TOP_K, E]),
                                top_f[:, t, 0:TOP_K].unsqueeze(2).to_broadcast([P, TOP_K, E]), ALU.is_equal).then_inc(dve_step, 1)
            steps[0] += TT
            e.wait_ge(dve_step, steps[0])
            for t in range(TT):
                e.tensor_reduce(chosen[:, t, :], hot[:, t, :, :].rearrange("p k n -> p n k"), AX.X, ALU.add).then_inc(dve_step, 1)
            steps[0] += TT
            e.wait_ge(dve_step, steps[0])
            for t in range(TT):
                e.tensor_copy(chosen4[:, t, :, :], chosen[:, t, :].unsqueeze(2).to_broadcast([P, E, CT])).then_inc(rt_dve, 1)
            ex_dve_w13(e, 1, 2)

            def counts():
                e.wait_ge(small_ps, PS_POS)
                step(e.tensor_copy(pos[:, :, :], ps[:, 4, P:P + TT * E].rearrange("p (t n) -> p t n", n=E)))
                step(e.tensor_copy(cnt[:, 0:1], ps[:, 4, 2 * P:2 * P + 1]))
                step(e.tensor_scalar(part_i[:, 1:2], part_i[:, 0:1], 2, None, ALU.arith_shift_right))
                step(e.tensor_scalar(part_i[:, 2:3], part_i[:, 0:1], CT - 1, 7, ALU.bitwise_and, ALU.arith_shift_left))
                step(e.tensor_copy(part[:, 0:2], part_i[:, 1:3]))
                step(e.tensor_tensor(cnt[:, 1:2], cnt[:, 0:1], part[:, 1:2], ALU.is_gt))
                e.tensor_scalar(valid_B[:, :], ones[:, :], cnt[:, 1:2], None, ALU.mult).then_inc(small_dve, 1)

            def places():
                e.wait_ge(small_ps, PS_PREFIX)
                step(e.tensor_copy(cnt[:, 2:4], ps[:, 7, 0:2]))
                e.tensor_scalar(m_hot[:, :], iota_e[:, :], cnt[:, 2:3], cnt[:, 1:2], ALU.is_equal, ALU.mult).then_inc(small_dve, 1)
                step(e.tensor_copy(start[:, :], ps[:, 7, 2:2 + E]))
                step(e.scalar_tensor_tensor(pos[:, :, :], start[:, :].unsqueeze(1).to_broadcast([P, TT, E]), float(P),
                                            pos[:, :, :], ALU.mult, ALU.add))
                for t in range(TT):
                    e.tensor_tensor(hotp[:, t, :, :], hot[:, t, :, :], pos[:, t, :].unsqueeze(1).to_broadcast([P, TOP_K, E]),
                                    ALU.mult).then_inc(dve_step, 1)
                steps[0] += TT
                e.wait_ge(dve_step, steps[0])
                step(e.tensor_reduce(slot_f[:, :, :].rearrange("p t k -> p (t k)"), hotp[:, :, :, :].rearrange("p t k n -> p (t k) n"),
                                     AX.X, ALU.add))
                e.tensor_copy(slot_i[:, :, :], slot_f[:, :, :]).then_inc(small_dve, 1)

            def lists():
                e.wait_ge(small_ps, PS_LIST)
                step(e.tensor_copy(lst_f[0:1, 0:ML], ps[0:1, 7, 0:ML]))
                step(e.tensor_scalar(lst_f[0:1, ML:ML + 1], cnt[0:1, 3:4], 1.0, None, ALU.subtract))
                step(e.tensor_copy(lst[0:1, :], lst_f[0:1, :]))
                e.tensor_scalar(lst[0:1, ML:ML + 1], lst[0:1, ML:ML + 1], 1, None, ALU.arith_shift_right).then_inc(small_dve, 1)

            def sh_x_add(t):
                e.wait_ge(shd_ps, t + 1)
                e.tensor_tensor(x[:, t, :], x[:, t, :], ps[:, 6, :], ALU.add).then_inc(sh_x, 1)

            for u in range(NSH):
                ex_dve_h(e, u % 2, u)
                if u >= 1:
                    ex_dve_hT(e, (u - 1) % 2, u - 1)
                if u == 1:
                    counts()
                if u == 2:
                    places()
                if u == 3:
                    lists()
                if u % 2 and u >= 3:
                    sh_x_add((u - 3) // 2)
            ex_dve_hT(e, 1, NSH - 1)
            ex_dve_w13(e, 0, 3)
            e.wait_ge(small_ps, PS_TOKENS)
            e.tensor_copy(tl[:, :], ps[:, 7, 0:ML]).then_inc(small_dve, 1)
            sh_x_add(TT - 1)
            last_i = last_turn(e)
            ex_dve_xT(e, 0, 0)
            ex_dve(e, 0, 0, True)
            ex_dve(e, 0, 1, True)
            ex_dve(e, 1, 0, slot_free=True)
            ex_dve(e, 1, 1)
            with e.Fori(2, last_i + 1) as i:
                ex_dve(e, i, 0)
                ex_dve(e, i, 1)
            ex_dve_ob(e, last_i * 2 + 1, 1, last_i)
            e.wait_ge(sh_x, TT)
            for t in range(TT):
                for k in range(TOP_K):
                    n = t * TOP_K + k
                    e.wait_ge(gb_in[n % GB], 16 * (n // GB + 1))
                    if n % TOP_K:
                        e.wait_ge(gb_used, n)
                    e.scalar_tensor_tensor(x[:, t, :], gb[:, n % GB, :], top_w[:, t, k:k + 1], x[:, t, :],
                                           ALU.mult, ALU.add).then_inc(gb_used, 1)

        @block.tensor
        def _(e):
            e.wait_ge(consts, 5)
            def keys(g, t, first=False):
                if t % 4 == 0 and first:
                    e.wait_ge(cT_ready, t // 4 + 1)
                if t == 0:
                    e.wait_ge(wk_ready, g + 1)
                e.wait_ge(sqk_free, g * KT + (t + 1))
                tk = slice(t * P, (t + 1) * P)
                for c in range(CC):
                    m = mm3(ps[:, 4 + t % 4, :], cT_h[:, c, tk], cT_l[:, c, tk],
                            wk_h[:, c, bass.ds(g * G4, G4)], wk_l[:, c, bass.ds(g * G4, G4)], c == 0, c == CC - 1)
                m.then_inc(k_ps, 1)

            for t in range(KT):
                keys(0, t, True)
            layernorm_pe(e, 0, xn_a)
            with e.Fori(1, 4) as g:
                for t in range(KT):
                    keys(g, t)
            e.wait_ge(xT_ready, TT)
            xa_pe_q(e, 0, 0)
            e.wait_ge(small_dve, DV_RK)
            for n in range(2):
                e.transpose(ps[:, 6 + n, 0:P], ssk[:, n * KT // 2:(n + 1) * KT // 2, :].rearrange("p t h -> p (t h)"),
                            ident[:, :]).then_inc(small_ps, 1)
            xa_pe_q(e, 0, 1)
            xa_pe_ss(e, 0)
            e.wait_ge(rkT_ready, 2)
            xa_pe_qp(e, 0)
            e.wait_ge(ctx_in_s, 16)

            def pair(i, more):
                for j in range(JB):
                    xa_pe_scores(e, i, j)
                if more:
                    xa_pe_q(e, i + 1, 0)
                    xa_pe_q(e, i + 1, 1)
                    xa_pe_ss(e, i + 1)
                xa_pe_pT(e, i, 0)
                xa_pe_pT(e, i, 1)
                xa_pe_u(e, i, 0)
                xa_pe_pT(e, i, 2)
                xa_pe_u(e, i, 1)
                xa_pe_pT(e, i, 3)
                xa_pe_u(e, i, 2)
                xa_pe_u(e, i, 3)
                if more:
                    xa_pe_qp(e, i + 1)
                xa_pe_ao(e, i)
            with e.Fori(0, HP - 1) as i:
                pair(i, True)
            pair(HP - 1, False)
            wo_pe(e, 0)

            layernorm_pe(e, 1, xn_b)
            e.wait_ge(small_lo, SP_BETA)
            e.wait_ge(xT_ready, 2 * TT)
            for t in range(TT):
                tk = slice(t * P, (t + 1) * P)
                for c in range(DC):
                    m = mm3(ps[:, 4, t * H:(t + 1) * H], xT_hi[:, c, tk], xT_lo[:, c, tk], bw_h[:, c, :], bw_l[:, c, :],
                            c == 0, c == DC - 1)
            m.then_inc(small_ps, 1)
            e.wait_ge(sp_dve, 1)
            with e.Fori(0, HP) as i:
                la_pe(e, i)
            wo_pe(e, 1)

            layernorm_pe(e, 2, xn_c)
            e.wait_ge(small_lo, SP_ROUTER)
            e.wait_ge(xT_ready, 3 * TT)
            for t in range(TT):
                tk = slice(t * P, (t + 1) * P)
                for c in range(DC):
                    m = mm3(ps[:, 4, t * E:(t + 1) * E], xT_hi[:, c, tk], xT_lo[:, c, tk], gw_h[:, c, :], gw_l[:, c, :],
                            c == 0, c == DC - 1)
            m.then_inc(small_ps, 1)

            def shared_down(t):
                e.wait_ge(hT_ready, 2 * t + 2)
                e.wait_ge(w2_ready, 2)
                if t:
                    e.wait_ge(sh_x, t)
                ex_down(0, 6, True, False)
                ex_down(1, 6, False, True).then_inc(shd_ps, 1)

            for u in range(NSH):
                t, k = u // 2, u % 2
                tk = slice(t * P, (t + 1) * P)
                e.wait_ge(w13_ready, k + 1)
                if u >= 2:
                    e.wait_ge(h_ready, u - 1)
                ex_up(lambda c: xT_hi[:, c, tk], lambda c: xT_lo[:, c, tk], k)
                if u % 2 and u >= 3:
                    shared_down(t - 1)
                if u >= 1:
                    ex_hT(e, 1 - k, u - 1)
                if u == 1:
                    e.wait_ge(rt_dve, 1 + TT)
                    e.wait_ge(pool_consts, 7)
                    for n in range(TT):
                        for q in range(n + 1):
                            e.matmul(ps[:, 4, P + n * E:P + (n + 1) * E], (strict if q == n else ones)[:, :],
                                     chosen[:, q, :], start=q == 0, stop=q == n)
                    for n in range(TT):
                        m = e.matmul(ps[:, 4, 2 * P:2 * P + 1], chosen4[:, n, :, :].rearrange("p n j -> p (n j)"),
                                     ones[:, 0:1], start=n == 0, stop=n == TT - 1)
                    m.then_inc(small_ps, 1)
                if u == 2:
                    e.wait_ge(small_dve, DV_VALID)
                    e.matmul(ps[:, 7, 0:1], strict[:, :], cnt[:, 1:2], start=True, stop=True)
                    e.matmul(ps[:, 7, 1:2], ones[:, :], cnt[:, 1:2], start=True, stop=True)
                    e.matmul(ps[:, 7, 2:2 + E], valid_B[:, :], below[:, :], start=True, stop=True).then_inc(small_ps, 1)
                if u == 3:
                    e.wait_ge(small_dve, DV_SLOTS)
                    e.matmul(ps[0:1, 7, 0:ML], part[:, 0:1], m_hot[:, :], start=True, stop=True).then_inc(small_ps, 1)
            ex_hT(e, 1, NSH - 1)
            shared_down(TT - 1)
            e.wait_ge(small_dve, DV_LISTS)
            e.wait_ge(scratch_io, IO_LISTS)
            e.transpose(ps[:, 7, 0:ML], tl_rows[0:ML, :], ident[0:ML, 0:ML]).then_inc(small_ps, 1)
            last_i = last_turn(e)
            ex_pe_xT(e, 0, 1)
            e.wait_ge(small_dve, DV_TOKENS)
            e.wait_ge(sh_x, TT)
            ex_pe(e, 0, 0, True)
            ex_pe(e, 0, 1, True)
            with e.Fori(1, last_i + 1) as i:
                ex_pe(e, i, 0)
                ex_pe(e, i, 1)
            ex_pe_down(e, last_i * 2 + 1, 1)


def kernel(x, ctx_1024, L0_xattn_Wq, L0_xattn_Wk, L0_xattn_Wv, L0_xattn_Wo, L0_xattn_gq, L0_xattn_gk,
           L0_attn_q_w, L0_attn_q_b, L0_attn_k_w, L0_attn_k_b, L0_attn_v_w, L0_attn_v_b, L0_attn_a_w, L0_attn_a_b,
           L0_attn_b_w, L0_attn_b_b, L0_attn_og_w, L0_attn_o_w, L0_attn_o_b, L0_ffn_gate_w, L0_ffn_w1, L0_ffn_w2,
           L0_ffn_w3, L0_ffn_sw1, L0_ffn_sw2, L0_ffn_sw3):
    import numpy as np
    import concourse.bacc as bacc
    from concourse import mybir
    from concourse.bass_utils import run_bass_kernel_spmd

    x, ctx = np.asarray(x), np.asarray(ctx_1024)
    tokens, ctx = x.reshape(-1, x.shape[-1]), ctx.reshape(-1, ctx.shape[-1])
    w1, w2, w3 = (np.asarray(w) for w in (L0_ffn_w1, L0_ffn_w2, L0_ffn_w3))
    dim, inter = w1.shape[1:]
    halves = np.asarray(L0_ffn_sw1).shape[1] // inter

    def halved(w):
        return np.asarray(w).reshape(dim, halves, inter).transpose(1, 0, 2)

    host = {
        "x_in": tokens, "ctx_in": ctx, "ctxT_in_": ctx.T,
        "Wq": L0_xattn_Wq, "Wk": L0_xattn_Wk, "WkT": np.asarray(L0_xattn_Wk).T, "Wv": L0_xattn_Wv, "Wo": L0_xattn_Wo,
        "gq": L0_xattn_gq, "gk": L0_xattn_gk,
        "qwT": np.asarray(L0_attn_q_w).T, "q_b": L0_attn_q_b, "kwT": np.asarray(L0_attn_k_w).T, "k_b": L0_attn_k_b,
        "vwT": np.asarray(L0_attn_v_w).T, "v_b": L0_attn_v_b, "bwT": np.asarray(L0_attn_b_w).T, "b_b": L0_attn_b_b,
        "ogwT": np.asarray(L0_attn_og_w).T, "owT": np.asarray(L0_attn_o_w).T, "o_b": L0_attn_o_b,
        "gwT": np.asarray(L0_ffn_gate_w).T,
        "w1": np.concatenate([w1, halved(L0_ffn_sw1)]),
        "w2": np.concatenate([w2, np.asarray(L0_ffn_sw2).reshape(halves, inter, dim)]),
        "w3": np.concatenate([w3, halved(L0_ffn_sw3)]),
    }
    nc = bacc.Bacc("TRN2", target_bir_lowering=False, num_devices=1)
    arrays, args = {}, {}
    for name, a in host.items():
        a = np.ascontiguousarray(a)
        arrays[f"in_{name}"] = a
        args[name] = nc.dram_tensor(f"in_{name}", a.shape, mybir.dt.from_np(a.dtype), kind="ExternalInput").ap()
    out = nc.dram_tensor("out_0", tokens.shape, mybir.dt.from_np(tokens.dtype), kind="ExternalOutput").ap()
    perceiver_block(nc, **args, out=out)
    result = run_bass_kernel_spmd(nc, [arrays], core_ids=[0])
    return result.results[0]["out_0"].reshape(x.shape)
```

```python
from contextlib import ExitStack

import concourse.bass as bass
from concourse import mybir

ALU = mybir.AluOpType
ACT = mybir.ActivationFunctionType
AX = mybir.AxisListType
F32 = mybir.dt.float32
F32R = mybir.dt.float32r
I32 = mybir.dt.int32

P = 128
LN_EPS = 1e-5
RMS_EPS = 1e-5
L2_EPS = 1e-12
TOP_K = 6


def perceiver_block(nc, x_in, ctx_in, ctxT_in, Wq, Wk, WkT, Wv, Wo, gq, gk,
                    qwT, q_b, kwT, k_b, vwT, v_b, bwT, b_b, ogwT, owT, o_b,
                    gwT, w1, w2, w3, out):
    T, D = x_in.shape
    NKV, C = ctx_in.shape
    INNER = Wq.shape[1]
    H = INNER // P
    B = 8
    SQ = T // B
    SKV = NKV // B
    TT, DC, CC, KT = T // P, D // P, C // P, NKV // P
    KPB = SKV // P
    HP = H // 2
    JB = 4
    G4 = 512
    RSD = float(P) ** -0.5

    stack = ExitStack()
    with stack:
        def sem(name):
            return stack.enter_context(nc.semaphore(name))

        def sbuf(where, name, shape, dt=F32):
            return where.enter_context(nc.sbuf_tensor(name, shape, dt))

        ps = stack.enter_context(nc.psum_tensor("ps", [P, 8, 512], F32))

        x = sbuf(stack, "x", [P, TT, D])
        xT_hi = sbuf(stack, "xT_hi", [P, DC, T], F32R)
        xT_lo = sbuf(stack, "xT_lo", [P, DC, T], F32R)
        ident = sbuf(stack, "ident", [P, P])
        zeros = sbuf(stack, "zeros", [P, D])
        ones = sbuf(stack, "ones", [P, P])
        eps = sbuf(stack, "eps", [P, 1])
        ln_std = sbuf(stack, "ln_std", [P, TT])
        ln_stat = sbuf(stack, "ln_stat", [P, TT, 6])
        ln_mv = sbuf(stack, "ln_mv", [P, TT, 2])
        ln_rstd = sbuf(stack, "ln_rstd", [P, TT])
        gw_raw = sbuf(stack, "gw_raw", [P, DC, gwT.shape[1]])

        kn = ExitStack()
        ssk = sbuf(kn, "ssk", [P, KT, H])
        rk_rms = sbuf(kn, "rk_rms", [P, KT, H])
        rkT = sbuf(kn, "rkT", [P, 2, P])
        wk_raw = sbuf(kn, "wk_raw", [P, CC, INNER])
        wk_h = sbuf(kn, "wk_h", [P, CC, INNER], F32R)
        wk_l = sbuf(kn, "wk_l", [P, CC, INNER], F32R)
        cT_h = sbuf(kn, "cT_h", [P, CC, NKV], F32R)
        cT_l = sbuf(kn, "cT_l", [P, CC, NKV], F32R)
        sqk = sbuf(kn, "sqk", [P, 2, G4])
        kn.close()

        attn = ExitStack()
        aoT = sbuf(attn, "aoT", [P, H, T])
        wo_raw = sbuf(attn, "wo_raw", [P, 2, D])
        wo_h = sbuf(attn, "wo_h", [P, 2, D], F32R)
        wo_l = sbuf(attn, "wo_l", [P, 2, D], F32R)
        ao_h = sbuf(attn, "ao_h", [P, 2, T], F32R)
        ao_l = sbuf(attn, "ao_l", [P, 2, T], F32R)

        xat = ExitStack()
        rkB = sbuf(xat, "rkB", [P, B, SKV])
        sc = sbuf(xat, "sc", [P, B, SKV])
        pT = sbuf(xat, "pT", [P, B, KPB, P])
        u_h = sbuf(xat, "u_h", [P, CC, B, 2, SQ], F32R)
        u_l = sbuf(xat, "u_l", [P, CC, B, 2, SQ], F32R)
        ctxT = sbuf(xat, "ctxT", [P, CC, NKV])
        ctx = sbuf(xat, "ctx", [P, KT, C])
        gqk = sbuf(xat, "gqk", [P, 3])
        wq_raw = sbuf(xat, "wq_raw", [P, DC, 2 * P])
        wq_h = sbuf(xat, "wq_h", [P, DC, 2 * P], F32R)
        wq_l = sbuf(xat, "wq_l", [P, DC, 2 * P], F32R)
        wkT_raw = sbuf(xat, "wkT_raw", [P, 2, C])
        wkT_h = sbuf(xat, "wkT_h", [P, 2, C], F32R)
        wkT_l = sbuf(xat, "wkT_l", [P, 2, C], F32R)
        wv_raw = sbuf(xat, "wv_raw", [P, CC, 2 * P])
        wv_h = sbuf(xat, "wv_h", [P, CC, 2 * P], F32R)
        wv_l = sbuf(xat, "wv_l", [P, CC, 2 * P], F32R)
        sq = sbuf(xat, "sq", [P, B, 2, SQ])
        qn_h = sbuf(xat, "qn_h", [P, 2, T], F32R)
        qn_l = sbuf(xat, "qn_l", [P, 2, T], F32R)
        qpT = sbuf(xat, "qpT", [P, CC, B, 2, SQ])
        xn_a = qpT[:, :, :, :, :].rearrange("p c b k q -> p (c b k q)").rearrange("p (t d) -> p t d", t=TT)
        rms = sbuf(xat, "rms", [P, B])
        rq = sbuf(xat, "rq", [P, B])
        nmx = sbuf(xat, "nmx", [P, 2, B])
        sm = sbuf(xat, "sm", [P, B])
        rsm = sbuf(xat, "rsm", [P, B])
        xat.close()

        lin = ExitStack()
        xn_b = sbuf(lin, "xn_b", [P, TT, D])
        lw_raw = [sbuf(lin, f"lw_raw{n}", [P, DC, 2 * P]) for n in range(4)]
        lw_h = [sbuf(lin, f"lw_h{n}", [P, DC, 2 * P], F32R) for n in range(4)]
        lw_l = [sbuf(lin, f"lw_l{n}", [P, DC, 2 * P], F32R) for n in range(4)]
        kq = sbuf(lin, "kq", [P, 4, T])
        kq_sq = sbuf(lin, "kq_sq", [P, 4, T])
        k_std = sbuf(lin, "k_std", [P, 2, TT])
        k_r = sbuf(lin, "k_r", [P, 2, TT])
        v_scale = sbuf(lin, "v_scale", [P, 2, TT])
        q_sqh = sbuf(lin, "q_sqh", [P, 2, T], F32R)
        q_sql = sbuf(lin, "q_sql", [P, 2, T], F32R)
        q_r = sbuf(lin, "q_r", [P, 2, T])
        ones_r = sbuf(lin, "ones_r", [P, P], F32R)
        kq_b = sbuf(lin, "kq_b", [P, 2, H])
        vt = sbuf(lin, "vt", [P, TT, 2 * P])
        v_bias = sbuf(lin, "v_bias", [P, INNER])
        at = sbuf(lin, "at", [P, 2, T])
        sg = sbuf(lin, "sg", [P, 2, T])
        mask = sbuf(lin, "mask", [P, P])
        ob_B = sbuf(lin, "ob_B", [P, D])
        bw_raw = sbuf(lin, "bw_raw", [P, DC, H])
        bw_h = sbuf(lin, "bw_h", [P, DC, H], F32R)
        bw_l = sbuf(lin, "bw_l", [P, DC, H], F32R)
        bb_B = sbuf(lin, "bb_B", [P, H])
        betaT = sbuf(lin, "betaT", [H, T])
        beta = sbuf(lin, "beta", [P, TT, H])
        sp = sbuf(lin, "sp", [P, 6, TT * H])
        lin.close()
        attn.close()

        E = gwT.shape[1]
        FF = w1.shape[2]
        FC = -(-FF // P)
        FW = [min(P, FF - c * P) for c in range(FC)]
        CAP = T
        CT = CAP // P
        MI = E + T * TOP_K // P
        ML = MI + 3
        moe = ExitStack()
        xn_c = sbuf(moe, "xn_c", [P, TT, D])
        xe = sbuf(moe, "xe", [P, 2, D])
        xeT_h = sbuf(moe, "xeT_h", [P, 2, DC, P], F32R)
        xeT_l = sbuf(moe, "xeT_l", [P, 2, DC, P], F32R)
        h1 = sbuf(moe, "h1", [P, 2, FF])
        h = sbuf(moe, "h", [P, 2, FF])
        hT_h = sbuf(moe, "hT_h", [P, 2, FC, P], F32R)
        hT_l = sbuf(moe, "hT_l", [P, 2, FC, P], F32R)
        ob = sbuf(moe, "ob", [P, 2, D])
        take = sbuf(moe, "take", [P, 2], I32)
        give = sbuf(moe, "give", [P, 2], I32)
        gw_h = sbuf(moe, "gw_h", [P, DC, E], F32R)
        gw_l = sbuf(moe, "gw_l", [P, DC, E], F32R)
        gateT = sbuf(moe, "gateT", [E, T])
        gate = sbuf(moe, "gate", [P, TT, E])
        r_small = sbuf(moe, "r_small", [P, 3, TT])
        top_w = sbuf(moe, "top_w", [P, TT, 8])
        top_i = sbuf(moe, "top_i", [P, TT, 8], mybir.dt.uint32)
        top_f = sbuf(moe, "top_f", [P, TT, 8])
        hot = sbuf(moe, "hot", [P, TT, TOP_K, E])
        hotp = sbuf(moe, "hotp", [P, TT, TOP_K, E])
        chosen = sbuf(moe, "chosen", [P, TT, E])
        before = sbuf(moe, "before", [P, TT + 1, E])
        chosen4 = sbuf(moe, "chosen4", [P, E, CT])
        pos = sbuf(moe, "pos", [P, TT, E])
        slot_f = sbuf(moe, "slot_f", [P, TT, TOP_K])
        slot_i = sbuf(moe, "slot_i", [P, 3, TT * TOP_K], I32)
        slot_rm = sbuf(moe, "slot_rm", [P, 2, TT * TOP_K])
        seat = sbuf(moe, "seat", [P, TT * TOP_K, P])
        item = sbuf(moe, "item", [P, TT * TOP_K, 2, ML])
        iota_e = sbuf(moe, "iota_e", [P, P])
        strict = sbuf(moe, "strict", [P, P])
        part = sbuf(moe, "part", [P, 3])
        part_i = sbuf(moe, "part_i", [P, 3], I32)
        tok_1 = sbuf(moe, "tok_1", [P, TT])
        spare = sbuf(moe, "spare", [P, 1])
        tl_f = sbuf(moe, "tl_f", [P, 2, ML])
        tl = sbuf(moe, "tl", [P, ML], I32)
        wl = sbuf(moe, "wl", [P, ML])
        valid_B = sbuf(moe, "valid_B", [P, P])
        below = sbuf(moe, "below", [P, E])
        start = sbuf(moe, "start", [P, E])
        cnt = sbuf(moe, "cnt", [P, 4])
        m_hot = sbuf(moe, "m_hot", [P, ML])
        EXPERT, LOADED, SLOT, ODD = range(4)
        lst_f = sbuf(moe, "lst_f", [1, 4, ML + 1])
        lst_j = sbuf(moe, "lst_j", [1, ML + 1])
        lst = sbuf(moe, "lst", [1, 4, ML + 1], I32)
        w13_raw = sbuf(moe, "w13_raw", [P, 2, DC, 2 * FF])
        w13_h = sbuf(moe, "w13_h", [P, 2, DC, 2 * FF], F32R)
        w13_l = sbuf(moe, "w13_l", [P, 2, DC, 2 * FF], F32R)
        w2_raw = sbuf(moe, "w2_raw", [P, 2, FC, D])
        w2_h = sbuf(moe, "w2_h", [P, 2, FC, D], F32R)
        w2_l = sbuf(moe, "w2_l", [P, 2, FC, D], F32R)
        moe.close()

        xn_dram = nc.dram_tensor("xn_scratch", [T + P, D], F32)
        y_dram = nc.dram_tensor("y_scratch", [T + P, D], F32)
        rk_dram = nc.dram_tensor("rk_scratch", [H, NKV], F32)

        consts = sem("consts")
        x_in_s, ctx_in_s, g_in_s = sem("x_in"), sem("ctx_in_s"), sem("g_in")
        ctxT_arrived = [sem(f"ctxT_arrived{g}") for g in range(4)]
        wk_arrived = [sem(f"wk_arrived{g}") for g in range(4)]
        dve_step = sem("dve_step")
        xn_ready, xT_ps, xT_hi_s, xT_ready = sem("xn_ready"), sem("xT_ps"), sem("xT_hi_s"), sem("xT_ready")
        cT_hi_s, cT_ready, wk_hi_s, wk_ready = sem("cT_hi_s"), sem("cT_ready"), sem("wk_hi_s"), sem("wk_ready")
        k_ps, sqk_ready, sqk_free = sem("k_ps"), sem("sqk_ready"), sem("sqk_free")
        rkT_ready, scratch_io = sem("rkT_ready"), sem("scratch_io")
        small_ps, small_dve, small_hi, small_lo, small_act = (
            sem("small_ps"), sem("small_dve"), sem("small_hi"), sem("small_lo"), sem("small_act"))
        PS_RKT, PS_BETAT, PS_BETA, PS_LOGITST, PS_LOGITS, PS_POS, PS_PREFIX, PS_LIST, PS_TOKENS = 2, 3, 4, 5, 6, 7, 8, 9, 10
        AC_BETA, AC_LOGITS = 1, 2
        DV_SSK, DV_RK, DV_KQB, DV_VALID, DV_ORDER, DV_LISTS, DV_SEATS, DV_TOKENS = 2, 3, 4, 5, 6, 7, 8, 9
        SP_BETA, SP_ROUTER = 1, 2
        IO_RK, IO_SPARE, IO_TOKENS = 32, 64, 80
        wq_in, wq_hi_s, wq_ready = sem("wq_in"), sem("wq_hi_s"), sem("wq_ready")
        wkT_in, wkT_hi_s, wkT_ready = sem("wkT_in"), sem("wkT_hi_s"), sem("wkT_ready")
        wv_in, wv_hi_s, wv_ready = sem("wv_in"), sem("wv_hi_s"), sem("wv_ready")
        rkB_in = [sem(f"rkB_in{j}") for j in range(JB)]
        q_ps, sq_ready, ss_ps, qn_hi_s, qn_split = sem("q_ps"), sem("sq_ready"), sem("ss_ps"), sem("qn_hi_s"), sem("qn_split")
        qp_ps, qp_ready = sem("qp_ps"), sem("qp_ready")
        s_ps, s_ready, nmx_ready, p_ready, pn_ready = sem("s_ps"), sem("s_ready"), sem("nmx_ready"), sem("p_ready"), sem("pn_ready")
        pT_ps, pT_ready, u_ps, u_hi_s, u_ready = sem("pT_ps"), sem("pT_ready"), sem("u_ps"), sem("u_hi_s"), sem("u_ready")
        ao_ps, ao_ready = sem("ao_ps"), sem("ao_ready")
        wo_in = [sem("wo_in0"), sem("wo_in1")]
        wo_hi_s, wo_ready, ao_split, wo_mm, y_ps = sem("wo_hi_s"), sem("wo_ready"), sem("ao_split"), sem("wo_mm"), sem("y_ps")
        x_ready = sem("x_ready")
        out_done = sem("out_done")
        lw_in = [sem(f"lw_in{n}") for n in range(4)]
        lw_hi_s = [sem(f"lw_hi_s{n}") for n in range(4)]
        lw_ready = [sem(f"lw_ready{n}") for n in range(4)]
        lin_in = sem("lin_in")
        mask_ready = sem("mask_ready")
        sp_dve, sp_act = sem("sp_dve"), sem("sp_act")
        kq_ps, kq_sq_ready, k_ss_ps, k_norm, k_guard, k_recip = (
            sem("kq_ps"), sem("kq_sq_ready"), sem("k_ss_ps"), sem("k_norm"), sem("k_guard"), sem("k_recip"))
        q_sqh_ready, q_sq_split, q_ss_ps, q_norm, q_recip, q_n = (
            sem("q_sqh_ready"), sem("q_sq_split"), sem("q_ss_ps"), sem("q_norm"), sem("q_recip"), sem("q_n"))
        v_scale_ready = sem("v_scale_ready")
        v_ps, v_biased, v_ready = sem("v_ps"), sem("v_biased"), sem("v_ready")
        og_ps, sg_ready, at_ps, at_ready, o_ps = sem("og_ps"), sem("sg_ready"), sem("at_ps"), sem("at_ready"), sem("o_ps")
        moe_in, pool_consts, rt_dve, rt_act = sem("moe_in"), sem("pool_consts"), sem("rt_dve"), sem("rt_act")
        sh_x, y_in, acc_done, acc_turn, past_loads = (
            sem("sh_x"), sem("y_in"), sem("acc_done"), sem("acc_turn"), sem("past_loads"))
        w13_in = [[sem(f"w{1 + 2 * n}_in{k}") for n in range(2)] for k in range(2)]
        w2_in = [sem("w2_in0"), sem("w2_in1")]
        w13_hi_s, w13_ready, w2_hi_s, w2_ready = sem("w13_hi_s"), sem("w13_ready"), sem("w2_hi_s"), sem("w2_ready")
        idx_ready, xe_in = sem("idx_ready"), [sem("xe_in0"), sem("xe_in1")]
        xeT_ps, xeT_hi_s, xeT_ready, h1_ps, h3_ps, h1_ready, h_ready = (
            sem("xeT_ps"), sem("xeT_hi_s"), sem("xeT_ready"), sem("h1_ps"), sem("h3_ps"), sem("h1_ready"), sem("h_ready"))
        hT_ps, hT_hi_s, hT_ready, d_ps, ob_ready = sem("hT_ps"), sem("hT_hi_s"), sem("hT_ready"), sem("d_ps"), sem("ob_ready")

        steps = [0]

        def mm3(out_ap, lh, ll, rh, rl, first=True, last=True):
            nc.tensor.matmul(out_ap, lh, rh, start=first, stop=False)
            nc.tensor.matmul(out_ap, lh, rl, start=False, stop=False)
            return nc.tensor.matmul(out_ap, ll, rh, start=False, stop=last)

        def ln_stats(e, t):
            e.bn_stats(ln_stat[:, t, :], x[:, t, :]).then_inc(dve_step, 1)
            steps[0] += 1

        def ln_mean_var(e):
            e.wait_ge(dve_step, steps[0])
            for t in range(TT):
                e.bn_aggr(ln_mv[:, t, :], ln_stat[:, t, :]).then_inc(ln_var_ready, 1)

        def ln_scale(e, n, xn):
            e.wait_ge(ln_std_ready, n + 1)
            e.reciprocal(ln_rstd[:, :], ln_std[:, :]).then_inc(dve_step, 1)
            steps[0] += 1
            e.wait_ge(dve_step, steps[0])
            for t in range(TT):
                e.tensor_scalar(xn[:, t, :], x[:, t, :], ln_mv[:, t, 0:1], ln_rstd[:, t:t + 1],
                                ALU.subtract, ALU.mult).then_inc(xn_ready, 1)

        def layernorm_dve(e, n, xn):
            for t in range(TT):
                ln_stats(e, t)
            ln_mean_var(e)
            ln_scale(e, n, xn)

        def layernorm_pe(e, n, xn):
            for t in range(TT):
                e.wait_ge(xn_ready, TT * n + t + 1)
                for c in range(DC):
                    last = e.transpose(ps[:, t, c * P:(c + 1) * P], xn[:, t, c * P:(c + 1) * P], ident[:, :])
                last.then_inc(xT_ps, 1)

        def wk_lo(e, g):
            kv = slice(g * G4, (g + 1) * G4)
            e.wait_ge(wk_hi_s, g + 1)
            e.tensor_tensor(wk_l[:, :, kv], wk_raw[:, :, kv], wk_h[:, :, kv], ALU.subtract).then_inc(wk_ready, 1)

        def layernorm_act_std(e, n):
            e.wait_ge(ln_var_ready, TT * (n + 1))
            e.activation(ln_std[:, :], ln_mv[:, :, 1], ACT.Sqrt, bias=eps[:, 0:1]).then_inc(ln_std_ready, 1)

        def layernorm_act_hi(e, n):
            for t in range(TT):
                e.wait_ge(xT_ps, TT * n + t + 1)
                e.activation(xT_hi[:, :, t * P:(t + 1) * P], ps[:, t, :].rearrange("p (c n) -> p c n", c=DC),
                             ACT.Copy).then_inc(xT_hi_s, 1)

        def layernorm_split_dve(e, n):
            for t in range(TT):
                e.wait_ge(xT_hi_s, TT * n + t + 1)
                tk = slice(t * P, (t + 1) * P)
                e.tensor_tensor(xT_lo[:, :, tk], ps[:, t, :].rearrange("p (c n) -> p c n", c=DC),
                                xT_hi[:, :, tk], ALU.subtract).then_inc(xT_ready, 1)

        def spans(n):
            return ((1, HP, None),) if n == 0 else ((1, 4, 0), (4, 5, 1), (5, 6, 2), (6, 7, 3), (7, HP, None))

        def wo_load(e, n, W, loads):
            Wr = W.rearrange("(h p) n -> h p n", p=P)
            for k in range(2):
                if n:
                    e.wait_ge(wo_ready, H * n + k - 1)
                e.dma_start(wo_raw[:, k, :], Wr[k]).then_inc(wo_in[k], 16)
            for i in range(1, len(loads) + 1):
                for k in range(2):
                    e.wait_ge(wo_ready, i * 2 + (H * n + k - 1))
                    e.dma_start(wo_raw[:, k, :], Wr[i * 2 + k]).then_inc(wo_in[k], 16)
                e.wait_ge(ao_ready, H * (n + 1))
                loads[i - 1]()
            with e.Fori(len(loads) + 1, HP) as i:
                for k in range(2):
                    e.wait_ge(wo_ready, i * 2 + (H * n + k - 1))
                    e.dma_start(wo_raw[:, k:k + 1, :], Wr[bass.ds(i * 2 + k, 1)].rearrange("h p n -> p h n"))\
                        .then_inc(wo_in[k], 16)

        def wo_act_head(e, n, i, k):
            e.wait_ge(wo_in[k], i * 16 + (HP * n + 1) * 16)
            e.wait_ge(ao_ready, i * 2 + (H * n + k + 1))
            if n or not isinstance(i, int):
                e.wait_ge(wo_mm, i * 2 + (H * n + k - 1))
            e.activation(wo_h[:, k, :], wo_raw[:, k, :], ACT.Copy)
            e.activation(ao_h[:, k:k + 1, :], aoT[:, bass.ds(i * 2 + k, 1), :], ACT.Copy).then_inc(wo_hi_s, 1)

        def wo_dve_head(e, n, i, k):
            e.wait_ge(wo_hi_s, i * 2 + (H * n + k + 1))
            e.tensor_tensor(ao_l[:, k:k + 1, :], aoT[:, bass.ds(i * 2 + k, 1), :], ao_h[:, k:k + 1, :],
                            ALU.subtract).then_inc(ao_split, 1)

        def wo_pool_head(e, n, i, k):
            e.wait_ge(wo_hi_s, i * 2 + (H * n + k + 1))
            e.tensor_tensor(wo_l[:, k, :], wo_raw[:, k, :], wo_h[:, k, :], ALU.subtract).then_inc(wo_ready, 1)

        def wo_first(e, n, head):
            for k in range(2):
                head(e, n, 0, k)

        def wo_act(e, n):
            for a, b, between in spans(n):
                with e.Fori(a, b) as i:
                    for k in range(2):
                        wo_act_head(e, n, i, k)
                if between is not None:
                    ex_act_w13(e, between // 2, between % 2, 1)

        def wo_dve(e, n):
            for a, b, between in spans(n):
                with e.Fori(a, b) as i:
                    for k in range(2):
                        wo_dve_head(e, n, i, k)
                if between is not None:
                    ex_dve_w13(e, between // 2, between % 2, between + 1)

        def wo_pool(e, n):
            with e.Fori(1, HP) as i:
                for k in range(2):
                    wo_pool_head(e, n, i, k)

        def wo_pe_tile(k, t, first=False, last=False):
            tk = slice(t * P, (t + 1) * P)
            return mm3(ps[:, t, :], ao_h[:, k, tk], ao_l[:, k, tk], wo_h[:, k, :], wo_l[:, k, :], first, last)

        def wo_pe_wait(e, n, i, k):
            e.wait_ge(ao_split, i * 2 + (H * n + k + 1))
            e.wait_ge(wo_ready, i * 2 + (H * n + k + 1))

        def wo_pe_head(e, n, i, k, first=False):
            wo_pe_wait(e, n, i, k)
            for t in range(TT):
                m = wo_pe_tile(k, t, first)
            m.then_inc(wo_mm, 1)

        def wo_pe_first(e, n):
            wo_pe_head(e, n, 0, 0, first=True)
            wo_pe_head(e, n, 0, 1)

        def wo_pe(e, n):
            with e.Fori(1, HP - 1) as i:
                for k in range(2):
                    wo_pe_head(e, n, i, k)
            wo_pe_head(e, n, HP - 1, 0)
            wo_pe_wait(e, n, HP - 1, 1)
            for t in range(TT):
                wo_pe_tile(1, t, last=True).then_inc(y_ps, 1)
            e.wait_ge(y_ps, TT * (n + 1))
            e.sem_inc(wo_mm, 1)

        kvb = lambda b: slice(b * SKV, (b + 1) * SKV)
        hcol = lambda k: slice(k * P, (k + 1) * P)

        def xa_act_weights(e, p):
            e.wait_ge(wq_in, p * 16 + 16)
            e.activation(wq_h[:, :, :], wq_raw[:, :, :], ACT.Copy).then_inc(wq_hi_s, 1)
            e.wait_ge(wkT_in, p * 16 + 16)
            e.activation(wkT_h[:, :, :], wkT_raw[:, :, :], ACT.Copy).then_inc(wkT_hi_s, 1)

        def xa_act_wv(e, i):
            e.wait_ge(wv_in, i * 16 + 16)
            e.activation(wv_h[:, :, :], wv_raw[:, :, :], ACT.Copy).then_inc(wv_hi_s, 1)

        def xa_act_q(e, p, k):
            e.wait_ge(q_ps, p * 2 + (k + 1))
            e.activation(sq[:, :, k, :], ps[:, k, :].rearrange("p (b q) -> p b q", b=B), ACT.Square,
                         scale=RSD).then_inc(sq_ready, 1)
            e.activation(qn_h[:, k, :], ps[:, k, :], ACT.Copy, scale=gqk[:, 2:3]).then_inc(qn_hi_s, 1)

        def xa_act_qp(e, p):
            for k in range(2):
                for c in range(CC):
                    e.wait_ge(qp_ps, p * 4 + (2 * k + c + 1))
                    e.activation(qpT[:, c, :, k, :], ps[:, 2 * k + c, :].rearrange("p (b q) -> p b q", b=B),
                                 ACT.Copy).then_inc(qp_ready, 1)

        def xa_act_exp(e, i, j):
            e.wait_ge(nmx_ready, i * 4 + (j + 1))
            for b in (2 * j, 2 * j + 1):
                last = e.activation(sc[:, b, :], sc[:, b, :], ACT.Exp, bias=nmx[:, 1, b:b + 1], scale=rq[:, b:b + 1],
                                    accum_out=sm[:, b:b + 1])
            last.then_inc(p_ready, 1)

        def xa_act_pT(e, i, j):
            e.wait_ge(pT_ps, i * 4 + (j + 1))
            e.activation(pT[:, 2 * j:2 * j + 2, :, :].rearrange("p b k n -> p (b k n)"), ps[:, 6 + j % 2, :],
                         ACT.Copy).then_inc(pT_ready, 1)

        def xa_act_u(e, i, j):
            e.wait_ge(u_ps, i * 4 + (j + 1))
            e.activation(u_h[:, :, 2 * j:2 * j + 2, :, :].rearrange("p c b k q -> p c (b k q)"),
                         ps[:, 4 + j % 2, :].rearrange("p (c n) -> p c n", c=CC), ACT.Copy).then_inc(u_hi_s, 1)

        def xa_pool_weights(e, p):
            e.wait_ge(wq_hi_s, p + 1)
            e.tensor_tensor(wq_l[:, :, :], wq_raw[:, :, :], wq_h[:, :, :], ALU.subtract).then_inc(wq_ready, 1)
            e.wait_ge(wkT_hi_s, p + 1)
            e.tensor_tensor(wkT_l[:, :, :], wkT_raw[:, :, :], wkT_h[:, :, :], ALU.subtract).then_inc(wkT_ready, 1)

        def xa_pool_wv(e, i):
            e.wait_ge(wv_hi_s, i + 1)
            e.tensor_tensor(wv_l[:, :, :], wv_raw[:, :, :], wv_h[:, :, :], ALU.subtract).then_inc(wv_ready, 1)

        def xa_dve_scores(e, i, j):
            bb = slice(2 * j, 2 * j + 2)
            e.wait_ge(s_ps, i * 4 + (j + 1))
            e.wait_ge(rkB_in[j], i * 32 + 32)
            e.tensor_tensor(sc[:, bb, :], ps[:, 4 + j % 2, :].rearrange("p (b n) -> p b n", b=2), rkB[:, bb, :],
                            ALU.mult).then_inc(s_ready, 1)
            e.wait_ge(s_ready, i * 4 + (j + 1))
            e.tensor_reduce(nmx[:, 0, bb], sc[:, bb, :], AX.X, ALU.max, negate=True).then_inc(mx_ready, 1)
            e.wait_ge(mx_ready, i * 4 + (j + 1))
            e.tensor_tensor(nmx[:, 1, bb], nmx[:, 0, bb], rq[:, bb], ALU.mult).then_inc(nmx_ready, 1)

        def xa_dve_norm(e, i, j):
            bb = slice(2 * j, 2 * j + 2)
            e.wait_ge(p_ready, i * 4 + (j + 1))
            e.reciprocal(rsm[:, bb], sm[:, bb]).then_inc(rsm_ready, 1)
            e.wait_ge(rsm_ready, i * 4 + (j + 1))
            e.tensor_tensor(sc[:, bb, :], sc[:, bb, :], rsm[:, bb].unsqueeze(2).to_broadcast([P, 2, SKV]),
                            ALU.mult).then_inc(pn_ready, 1)

        def xa_act_rms(e, p):
            e.wait_ge(ss_ps, p + 1)
            e.activation(rms[:, :].rearrange("p (a b) -> p a b", a=2),
                         ps[:, 2:4, :].rearrange("p a (b n) -> p a b n", n=P)[:, :, :, 0], ACT.Sqrt, bias=eps[:, 0:1]).then_inc(rms_ready, 1)

        def xa_dve_rq(e, p):
            e.wait_ge(rms_ready, p + 1)
            e.reciprocal(rq[:, :], rms[:, :]).then_inc(rq_ready, 1)

        def xa_dve_qsplit(e, p, k):
            e.wait_ge(qn_hi_s, p * 2 + (k + 1))
            e.scalar_tensor_tensor(qn_l[:, k, :], ps[:, k, :], gqk[:, 2:3], qn_h[:, k, :], ALU.mult, ALU.subtract)\
                .then_inc(qn_split, 1)

        def xa_dve_u(e, i, j):
            e.wait_ge(u_hi_s, i * 4 + (j + 1))
            r = lambda a: a[:, :, 2 * j:2 * j + 2, :, :].rearrange("p c b k q -> p c (b k q)")
            e.tensor_tensor(r(u_l), ps[:, 4 + j % 2, :].rearrange("p (c n) -> p c n", c=CC), r(u_h),
                            ALU.subtract).then_inc(u_ready, 1)

        def xa_dve_ao(e, i):
            for k in range(2):
                e.wait_ge(ao_ps, i * 2 + (k + 1))
                e.tensor_copy(aoT[:, bass.ds(i * 2 + k, 1), :], ps[:, 6 + k:7 + k, :]).then_inc(ao_ready, 1)

        def xa_pe_q(e, p, k):
            e.wait_ge(wq_ready, p + 1)
            for c in range(DC):
                m = mm3(ps[:, k, :], wq_h[:, c, hcol(k)], wq_l[:, c, hcol(k)], xT_hi[:, c, :], xT_lo[:, c, :],
                        c == 0, c == DC - 1)
            m.then_inc(q_ps, 1)

        def xa_pe_ss(e, p):
            e.wait_ge(sq_ready, p * 2 + 2)
            for b in range(B):
                m = e.matmul(ps[:, 2 + b // 4, b % 4 * P:(b % 4 + 1) * P], sq[:, b, :, :].rearrange("p k q -> p (k q)"),
                             ones[:, :], start=True, stop=True)
            m.then_inc(ss_ps, 1)

        def xa_pe_qp(e, p):
            e.wait_ge(wkT_ready, p + 1)
            e.wait_ge(qn_split, p * 2 + 2)
            for k in range(2):
                if k == 1:
                    e.wait_ge(rms_ready, p + 1)
                for c in range(CC):
                    mm3(ps[:, 2 * k + c, :], wkT_h[:, k, hcol(c)], wkT_l[:, k, hcol(c)], qn_h[:, k, :],
                        qn_l[:, k, :]).then_inc(qp_ps, 1)

        def xa_pe_scores(e, i, j):
            if j == 0:
                e.wait_ge(qp_ready, i * 4 + 4)
            if j >= 2:
                e.wait_ge(s_ready, i * 4 + (j - 1))
            for n, b in enumerate((2 * j, 2 * j + 1)):
                for c in range(CC):
                    m = e.matmul(ps[:, 4 + j % 2, n * SKV:(n + 1) * SKV],
                                 qpT[:, c, b, :, :].rearrange("p k q -> p (k q)"), ctxT[:, c, kvb(b)],
                                 start=c == 0, stop=c == CC - 1)
            m.then_inc(s_ps, 1)

        def xa_pe_pT(e, i, j):
            e.wait_ge(pn_ready, i * 4 + (j + 1))
            if j >= 2:
                e.wait_ge(pT_ready, i * 4 + (j - 1))
            for n, b in enumerate((2 * j, 2 * j + 1)):
                for t in range(KPB):
                    at = (n * KPB + t) * P
                    m = e.transpose(ps[:, 6 + j % 2, at:at + P], sc[:, b, t * P:(t + 1) * P], ident[:, :])
            m.then_inc(pT_ps, 1)

        def xa_pe_u(e, i, j):
            e.wait_ge(pT_ready, i * 4 + (j + 1))
            if j < 2:
                e.wait_ge(s_ready, i * 4 + (j + 3))
            else:
                e.wait_ge(u_ready, i * 4 + (j - 1))
            for c in range(CC):
                for n, b in enumerate((2 * j, 2 * j + 1)):
                    at = (c * 2 + n) * P
                    for t in range(KPB):
                        m = e.matmul(ps[:, 4 + j % 2, at:at + P], ctx[:, b * KPB + t, hcol(c)], pT[:, b, t, :],
                                     start=t == 0, stop=t == KPB - 1)
            m.then_inc(u_ps, 1)

        def xa_pe_ao(e, i):
            e.wait_ge(wv_ready, i + 1)
            e.wait_ge(u_ready, i * 4 + 4)
            for k in range(2):
                for c in range(CC):
                    m = mm3(ps[:, 6 + k, :], wv_h[:, c, hcol(k)], wv_l[:, c, hcol(k)],
                            u_h[:, c, :, k, :], u_l[:, c, :, k, :], c == 0, c == CC - 1)
                m.then_inc(ao_ps, 1)

        K_, Q_, V_, G_ = range(4)

        def la_act_split(e, n, p):
            e.wait_ge(lw_in[n], p * 16 + 16)
            e.activation(lw_h[n][:, :, :], lw_raw[n][:, :, :], ACT.Copy).then_inc(lw_hi_s[n], 1)

        def la_pool_split(e, n, p):
            e.wait_ge(lw_hi_s[n], p + 1)
            e.tensor_tensor(lw_l[n][:, :, :], lw_raw[n][:, :, :], lw_h[n][:, :, :], ALU.subtract).then_inc(lw_ready[n], 1)

        def la_proj(e, n, k, bank):
            for c in range(DC):
                m = mm3(ps[:, bank, :], lw_h[n][:, c, hcol(k)], lw_l[n][:, c, hcol(k)], xT_hi[:, c, :], xT_lo[:, c, :],
                        c == 0, c == DC - 1)
            return m

        def la_pe(e, i):
            def q_sum(k):
                e.wait_ge(q_sq_split, i * 2 + (k + 1))
                e.matmul(ps[:, 2 + k, :], ones_r[:, :], q_sqh[:, k, :], start=True, stop=False)
                e.matmul(ps[:, 2 + k, :], ones_r[:, :], q_sql[:, k, :], start=False, stop=True).then_inc(q_ss_ps, 1)

            for n in (K_, Q_):
                e.wait_ge(lw_ready[n], i + 1)
                for k in range(2):
                    la_proj(e, n, k, 2 * n + k).then_inc(kq_ps, 1)
            q_sum(0)
            e.wait_ge(lw_ready[V_], i + 1)
            e.wait_ge(ao_ready, i * 2 + H)
            e.wait_ge(sp_dve, 1)
            for t in range(TT):
                tk = slice(t * P, (t + 1) * P)
                for c in range(DC):
                    m = mm3(ps[:, 4 + t // 2, (t % 2) * 2 * P:(t % 2 + 1) * 2 * P], xT_hi[:, c, tk], xT_lo[:, c, tk],
                            lw_h[V_][:, c, :], lw_l[V_][:, c, :], c == 0, c == DC - 1)
                if t % 2:
                    m.then_inc(v_ps, 1)
                if t == 1:
                    q_sum(1)
                    for n in range(2):
                        for s in range(TT):
                            m = e.matmul(ps[:, n, s * P:(s + 1) * P], kq_sq[:, n, s * P:(s + 1) * P], ones[:, :],
                                         start=True, stop=True)
                    m.then_inc(k_ss_ps, 1)
            e.wait_ge(lw_ready[G_], i + 1)
            la_proj(e, G_, 0, 6).then_inc(og_ps, 1)
            la_proj(e, G_, 1, 7).then_inc(og_ps, 1)
            e.wait_ge(k_norm, i + 1)
            for k in range(2):
                e.wait_ge(q_n, i * 2 + (k + 1))
                for t in range(TT):
                    tk = slice(t * P, (t + 1) * P)
                    m = e.matmul(ps[:, k, tk], kq[:, k, tk], kq[:, 2 + k, tk], start=True, stop=True)
                m.then_inc(at_ps, 1)
            e.wait_ge(v_ready, i * 2 + 2)
            for k in range(2):
                e.wait_ge(at_ready, i * 2 + (k + 1))
                for t in range(TT):
                    tk = slice(t * P, (t + 1) * P)
                    m = e.matmul(ps[:, 4 + k, tk], vt[:, t, hcol(k)], at[:, k, tk], start=True, stop=True)
                m.then_inc(o_ps, 1)
            e.wait_ge(sg_ready, i * 2 + 2)

        def la_act(e, i, more):
            for n in range(4):
                e.wait_ge(kq_ps, i * 4 + (n + 1))
                bias = kq_b[:, n // 2, bass.ds(i * 2 + n % 2, 1)]
                e.activation(kq_sq[:, n, :], ps[:, n, :], ACT.Square, bias=bias, scale=RSD)
                e.activation(kq[:, n, :], ps[:, n, :], ACT.Identity, bias=bias, scale=RSD).then_inc(kq_sq_ready, 1)
            for k in range(2):
                e.wait_ge(q_ss_ps, i * 2 + (k + 1))
                e.activation(q_r[:, k, :], ps[:, 2 + k, :], ACT.Sqrt).then_inc(q_norm, 1)
                if more and k == 0:
                    la_act_split(e, K_, i + 1)
            e.wait_ge(k_ss_ps, i + 1)
            e.activation(k_std[:, :, :], ps[:, 0:2, :].rearrange("p n (t s) -> p n t s", s=P)[:, :, :, 0], ACT.Sqrt).then_inc(k_norm, 1)
            if more:
                la_act_split(e, Q_, i + 1)
                e.wait_ge(v_ps, i * 2 + 2)
                la_act_split(e, V_, i + 1)
            for k in range(2):
                e.wait_ge(og_ps, i * 2 + (k + 1))
                e.activation(sg[:, k, :], ps[:, 6 + k, :], ACT.Silu).then_inc(sg_ready, 1)
            if more:
                la_act_split(e, G_, i + 1)

        def la_dve(e, i):
            def q_split(k):
                e.wait_ge(kq_sq_ready, i * 4 + (k + 3))
                e.tensor_copy(q_sqh[:, k, :], kq_sq[:, 2 + k, :]).then_inc(q_sqh_ready, 1)
                e.wait_ge(q_sqh_ready, i * 2 + (k + 1))
                e.tensor_tensor(q_sql[:, k, :], kq_sq[:, 2 + k, :], q_sqh[:, k, :], ALU.subtract).then_inc(q_sq_split, 1)

            def q_scale(k):
                e.wait_ge(q_norm, i * 2 + (k + 1))
                e.reciprocal(q_r[:, k, :], q_r[:, k, :]).then_inc(q_recip, 1)
                e.wait_ge(q_recip, i * 2 + (k + 1))
                e.scalar_tensor_tensor(kq[:, 2 + k, :], q_r[:, k, :], 1.0 / L2_EPS, kq[:, 2 + k, :], ALU.min, ALU.mult)\
                    .then_inc(q_n, 1)

            q_split(0)
            q_split(1)
            q_scale(0)
            for g in range(2):
                e.wait_ge(v_ps, i * 2 + (g + 1))
                e.tensor_tensor(vt[:, 2 * g:2 * g + 2, :], ps[:, 4 + g, :].rearrange("p (t n) -> p t n", t=2),
                                v_bias[:, bass.ds(i * 2 * P, 2 * P)].unsqueeze(1).to_broadcast([P, 2, 2 * P]),
                                ALU.add).then_inc(v_biased, 1)
                if g == 0:
                    e.wait_ge(k_norm, i + 1)
                    e.tensor_scalar(k_std[:, :, :], k_std[:, :, :], L2_EPS, None, ALU.max).then_inc(k_guard, 1)
                    e.wait_ge(k_guard, i + 1)
                    e.reciprocal(k_r[:, :, :], k_std[:, :, :]).then_inc(k_recip, 1)
                    e.wait_ge(k_recip, i + 1)
                    e.tensor_tensor(v_scale[:, :, :], k_r[:, :, :],
                                    beta[:, :, bass.ds(i * 2, 2)].rearrange("p t h -> p h t"), ALU.mult).then_inc(v_scale_ready, 1)
                    e.wait_ge(v_scale_ready, i + 1)
                e.wait_ge(v_biased, i * 2 + (g + 1))
                for t in (2 * g, 2 * g + 1):
                    v = vt[:, t, :].rearrange("p (h n) -> p h n", h=2)
                    m = e.tensor_tensor(v, v, v_scale[:, :, t].unsqueeze(2).to_broadcast([P, 2, P]), ALU.mult)
                m.then_inc(v_ready, 1)
                if g == 0:
                    q_scale(1)
            for k in range(2):
                e.wait_ge(at_ps, i * 2 + (k + 1))
                e.tensor_tensor(at[:, k, :].rearrange("p (t n) -> p t n", t=TT),
                                ps[:, k, :].rearrange("p (t n) -> p t n", t=TT),
                                mask[:, :].unsqueeze(1).to_broadcast([P, TT, P]), ALU.mult).then_inc(at_ready, 1)
            for k in range(2):
                e.wait_ge(o_ps, i * 2 + (k + 1))
                e.wait_ge(sg_ready, i * 2 + (k + 1))
                e.tensor_tensor(aoT[:, bass.ds(i * 2 + k, 1), :], ps[:, 4 + k:5 + k, :], sg[:, k:k + 1, :],
                                ALU.mult).then_inc(ao_ready, 1)

        NSH = 2 * TT
        every = slice(None)
        LC = 3 * P

        def fcs(c):
            return slice(c * P, c * P + FW[c])

        def item_value(e, row, m, most=1):
            return e.value_load(lst[0:1, row, bass.ds(m, 1)], min_val=0, max_val=most)

        def part_of(weights, w, *rest):
            if isinstance(w, int):
                return weights[(rest[0], w) + rest[1:]]
            return weights[(rest[0], bass.ds(w, 1)) + rest[1:]]

        def ex_up(lh, ll, k, w, ready):
            for n, s in ((0, h1_ps), (1, h3_ps)):
                nc.tensor.wait_ge(w13_ready, ready + (n - 1))
                f = slice(n * FF, (n + 1) * FF)
                for c in range(DC):
                    m = mm3(ps[:, 2 * n + k, 0:FF], lh(c), ll(c), part_of(w13_h, w, every, c, f), part_of(w13_l, w, every, c, f),
                            c == 0, c == DC - 1)
                m.then_inc(s, 1)

        def ex_hT(e, k, u):
            e.wait_ge(h_ready, u + 1)
            e.wait_ge(hT_ready, u)
            for c in range(FC):
                m = e.transpose(ps[0:FW[c], 5, c * P:(c + 1) * P], h[:, k, fcs(c)], ident[:, :])
            m.then_inc(hT_ps, 1)

        def ex_down(e, k, u, w, ready):
            e.wait_ge(hT_ready, u + 1)
            e.wait_ge(w2_ready, ready)
            for c in range(FC):
                r = slice(0, FW[c])
                m = mm3(ps[:, 6 + k, :], hT_h[r, k, c, :], hT_l[r, k, c, :], part_of(w2_h, w, r, c, every), part_of(w2_l, w, r, c, every),
                        c == 0, c == FC - 1)
            m.then_inc(d_ps, 1)

        def ex_act_w13(e, k, n, use):
            e.wait_ge(w13_in[k][n], use * 16)
            f = slice(n * FF, (n + 1) * FF)
            e.activation(w13_h[:, k, :, f], w13_raw[:, k, :, f], ACT.Copy).then_inc(w13_hi_s, 1)

        def ex_dve_w13(e, k, n, count):
            e.wait_ge(w13_hi_s, count)
            f = slice(n * FF, (n + 1) * FF)
            e.tensor_tensor(w13_l[:, k, :, f], w13_raw[:, k, :, f], w13_h[:, k, :, f], ALU.subtract).then_inc(w13_ready, 1)

        def ex_act_w2(e, k, n):
            e.wait_ge(w2_in[k], n * 32)
            e.activation(w2_h[:, k, :, :], w2_raw[:, k, :, :], ACT.Copy).then_inc(w2_hi_s, 1)

        def ex_pool_w2(e, k, n):
            e.wait_ge(w2_hi_s, n)
            e.tensor_tensor(w2_l[:, k, :, :], w2_raw[:, k, :, :], w2_h[:, k, :, :], ALU.subtract).then_inc(w2_ready, 1)

        def ex_act_silu(e, k, u):
            e.wait_ge(h1_ps, u + 1)
            e.activation(h1[:, k, :], ps[:, k, 0:FF], ACT.Silu).then_inc(h1_ready, 1)

        def ex_dve_h(e, k, u):
            e.wait_ge(h1_ready, u + 1)
            e.wait_ge(h3_ps, u + 1)
            e.tensor_tensor(h[:, k, :], h1[:, k, :], ps[:, 2 + k, 0:FF], ALU.mult).then_inc(h_ready, 1)

        def ex_act_hT(e, k, u):
            e.wait_ge(hT_ps, u + 1)
            for c in range(FC):
                r = slice(0, FW[c])
                last = e.activation(hT_h[r, k, c, :], ps[r, 5, c * P:(c + 1) * P], ACT.Copy)
            last.then_inc(hT_hi_s, 1)

        def ex_dve_hT(e, k, u):
            e.wait_ge(hT_hi_s, u + 1)
            for c in range(FC):
                r = slice(0, FW[c])
                last = e.tensor_tensor(hT_l[r, k, c, :], ps[r, 5, c * P:(c + 1) * P], hT_h[r, k, c, :], ALU.subtract)
            last.then_inc(hT_ready, 1)

        def ex_act_xT(e, m, k):
            e.wait_ge(xeT_ps, m + 1)
            e.activation(xeT_h[:, k, :, :].rearrange("p c n -> p (c n)"), ps[:, 4, :], ACT.Copy).then_inc(xeT_hi_s, 1)

        def ex_dve_xT(e, m, k):
            e.wait_ge(xeT_hi_s, m + 1)
            e.tensor_tensor(xeT_l[:, k, :, :].rearrange("p c n -> p (c n)"), ps[:, 4, :],
                            xeT_h[:, k, :, :].rearrange("p c n -> p (c n)"), ALU.subtract).then_inc(xeT_ready, 1)

        def ex_pe_xT(e, k, n):
            e.wait_ge(xe_in[k], n * 16)
            for c in range(DC):
                last = e.transpose(ps[:, 4, c * P:(c + 1) * P], xe[:, k, c * P:(c + 1) * P], ident[:, :])
            last.then_inc(xeT_ps, 1)

        def ex_pe(e, i, k, first=False):
            m = i * 2 + k
            e.wait_ge(xeT_ready, m + 1)
            ex_pe_xT(e, 1 - k, i + (k + 1))
            e.wait_ge(h_ready, m + (NSH - 1))
            ex_up(lambda c: xeT_h[:, k, c, :], lambda c: xeT_l[:, k, c, :], k, item_value(e, SLOT, m), m * 2 + 6)
            ex_down(e, 1 - k, m + (NSH - 1), 1 if first else item_value(e, SLOT, m - 1), 2 if first else m + 2)
            ex_hT(e, k, m + NSH)

        def ex_act(e, i, k):
            m = i * 2 + k
            odd, last_odd = item_value(e, ODD, m + 1), item_value(e, ODD, m)
            ex_act_hT(e, 1 - k, m + (NSH - 1))
            ex_act_xT(e, m + 1, 1 - k)
            ex_act_silu(e, k, m + NSH)
            e.wait_ge(h3_ps, m + odd + NSH)
            ex_act_w13(e, 1 - k, 0, i + (k + 2))
            ex_act_w13(e, 1 - k, 1, i + (k + 2))
            e.wait_ge(d_ps, m + last_odd + (NSH - 1))
            ex_act_w2(e, k, i + 2)

        def ex_dve_ob(e, m, k, slot_used=True):
            e.wait_ge(d_ps, m + (NSH - 1))
            if slot_used:
                e.wait_ge(acc_done, m * 16 - 48)
            e.tensor_scalar(ob[:, k, :], ps[:, 6 + k, :], wl[:, bass.ds(m - 2, 1)], None, ALU.mult).then_inc(ob_ready, 1)

        def ex_dve_x(e, u):
            e.wait_ge(d_ps, u + 1)
            if u >= TT:
                e.wait_ge(sh_x, u - TT + 1)
            e.tensor_tensor(x[:, u % TT, :], x[:, u % TT, :], ps[:, 6 + u % 2, :], ALU.add).then_inc(sh_x, 1)

        def ex_dve(e, i, k):
            m = i * 2 + k
            ex_dve_hT(e, 1 - k, m + (NSH - 1))
            ex_dve_xT(e, m + 1, 1 - k)
            if isinstance(i, int) and i == 0:
                ex_dve_x(e, NSH - 2 + k)
            else:
                ex_dve_ob(e, m, k, not isinstance(i, int))
            ex_dve_h(e, k, m + NSH)
            ex_dve_w13(e, 1 - k, 0, m * 2 + 7)
            ex_dve_w13(e, 1 - k, 1, m * 2 + 8)

        def ex_rows(e, to, m, k):
            e.tensor_copy(to[:, k:k + 1], tl[:, bass.ds(m, 1)]).then_inc(idx_ready, 1)

        def ex_gather(e, k):
            e.indirect_dma_start(xe[:, k, :], None, xn_dram.ap(), bass.IndirectOffsetOnAxis(ap=take[:, k:k + 1], axis=0))\
                .then_inc(xe_in[k], 16)

        def ex_scatter(e, k):
            e.indirect_dma_start(y_dram.ap(), bass.IndirectOffsetOnAxis(ap=give[:, k:k + 1], axis=0), ob[:, k, :], None,
                                 compute_op=ALU.add).then_inc(acc_done, 16)

        def ex_pool(e, i, k):
            m = i * 2 + k
            peeled = isinstance(i, int)
            e.wait_ge(xeT_ps, m + 2)
            ex_rows(e, take, m + 3, 1 - k)
            if not peeled or i > 0:
                if not peeled or k > 0:
                    e.wait_ge(acc_done, m * 16 - 32)
                else:
                    e.wait_ge(y_in, 16 * TT)
                ex_rows(e, give, m - 2, k)
                e.wait_ge(ob_ready, m - 1)
                e.wait_ge(idx_ready, m * 2 + 3)
            else:
                e.wait_ge(idx_ready, m + 4)
            e.sem_inc(acc_turn, 1)
            ex_gather(e, 1 - k)
            if not peeled or i > 0:
                ex_scatter(e, k)
            ex_pool_w2(e, k, m + 3)

        def load_w13(e, k, n, ap, **cond):
            e.dma_start(w13_raw[:, k, :, n * FF:(n + 1) * FF], ap, **cond).then_inc(w13_in[k][n], 16)

        def load_w2(e, k, whole_ap, rest_ap, **cond):
            e.dma_start(w2_raw[:, k, 0:FC - 1, :], whole_ap, **cond).then_inc(w2_in[k], 16)
            e.dma_start(w2_raw[0:FW[-1], k, FC - 1, :], rest_ap, **cond).then_inc(w2_in[k], 16)

        w1_r = w1.rearrange("e (c p) f -> e p c f", p=P)
        w3_r = w3.rearrange("e (c p) f -> e p c f", p=P)
        w2_r = w2[:, 0:(FC - 1) * P, :].rearrange("e (c p) d -> e p c d", p=P)
        w2_t = w2[:, (FC - 1) * P:FF, :]

        def ex_load_w13(e, m, k):
            ex, new = item_value(e, EXPERT, m, E - 1), item_value(e, LOADED, m)
            for n, w in enumerate((w1_r, w3_r)):
                e.wait_ge(w13_ready, m * 2 + (n + 1))
                load_w13(e, k, n, w[bass.ds(ex, 1)].rearrange("e p c f -> p (e c) f"), cond=new)

        def ex_load_w2(e, m, k):
            ex, new = item_value(e, EXPERT, m, E - 1), item_value(e, LOADED, m)
            e.wait_ge(w2_ready, m + 1)
            load_w2(e, k, w2_r[bass.ds(ex, 1)].rearrange("e p c d -> p (e c) d"),
                    w2_t[bass.ds(ex, 1)].rearrange("e p d -> p (e d)"), cond=new)

        def last_turn(e):
            e.wait_ge(small_dve, DV_LISTS)
            return e.value_load(lst[0:1, EXPERT, ML:ML + 1], min_val=T * TOP_K // P // 2 - 1, max_val=MI // 2 - 1)

        rsm_ready, rq_ready, rms_ready, mx_ready = sem("rsm_ready"), sem("rq_ready"), sem("rms_ready"), sem("mx_ready")
        ln_var_ready, ln_std_ready, rk_sqrt = sem("ln_var_ready"), sem("ln_std_ready"), sem("rk_sqrt")

        lw_r = [w.rearrange("(c p) (h n) -> h p c n", p=P, n=2 * P) for w in (kwT, qwT, vwT, ogwT)]

        block = stack.enter_context(nc.Block())

        @block.sync
        def _(e):
            def load_ctxT(g):
                kv = slice(g * G4, (g + 1) * G4)
                e.dma_start(ctxT[:, :, kv], ctxT_in.rearrange("(c p) n -> p c n", p=P)[:, :, kv]).then_inc(ctxT_arrived[g], 16)

            def load_wk(g):
                kv = slice(g * G4, (g + 1) * G4)
                e.dma_start(wk_raw[:, :, kv], Wk.rearrange("(c p) n -> p c n", p=P)[:, :, kv]).then_inc(wk_arrived[g], 16)

            load_wk(0)
            load_ctxT(0)
            load_ctxT(1)
            e.dma_start(x[:, :, :], x_in.rearrange("(t p) d -> p t d", p=P)).then_inc(x_in_s, 16)
            load_ctxT(2)
            load_ctxT(3)
            e.dma_start(gqk[:, 0:1], gq.rearrange("(p a) -> p a", a=1)).then_inc(g_in_s, 16)
            e.dma_start(gqk[:, 1:2], gk.rearrange("(p a) -> p a", a=1)).then_inc(g_in_s, 16)
            for g in range(1, 4):
                load_wk(g)
            wq_r = Wq.rearrange("(c p) (h n) -> h p c n", p=P, n=2 * P)
            wkT_r = WkT.rearrange("(h k p) c -> h p k c", k=2, p=P)
            wv_r = Wv.rearrange("(c p) (h n) -> h p c n", p=P, n=2 * P)
            e.dma_start(wq_raw[:, :, :], wq_r[0]).then_inc(wq_in, 16)
            e.dma_start(wkT_raw[:, :, :], wkT_r[0]).then_inc(wkT_in, 16)
            e.dma_start(wv_raw[:, :, :], wv_r[0]).then_inc(wv_in, 16)
            e.dma_start(ctx[:, :, :], ctx_in.rearrange("(t p) c -> p t c", p=P)).then_inc(ctx_in_s, 16)
            e.wait_ge(rkT_ready, 2)
            for n in range(2):
                e.dma_start(rk_dram.ap().rearrange("h (n t p) -> n t h p", n=2, p=P)[n], rkT[:, n, :]).then_inc(scratch_io, 16)
            e.wait_ge(scratch_io, IO_RK)
            e.dma_start(xn_dram.ap()[T:T + P, :], zeros[:, :]).then_inc(scratch_io, 16)
            e.dma_start(y_dram.ap()[T:T + P, :], zeros[:, :]).then_inc(scratch_io, 16)

            rk_r = rk_dram.ap().rearrange("(h k) (j n) -> h k j n", k=2, j=JB)

            def rk_load(p, j):
                for k in range(2):
                    src = rk_r[bass.ds(p, 1), k, j, :]
                    e.dma_start(rkB[k * SQ:(k + 1) * SQ, 2 * j:2 * j + 2, :].rearrange("p b n -> p (b n)"),
                                src.to_broadcast([SQ, 2 * SKV])).then_inc(rkB_in[j], 16)

            for j in range(JB):
                rk_load(0, j)
            with e.Fori(1, HP) as p:
                e.wait_ge(wq_ready, p)
                e.dma_start(wq_raw[:, :, :], wq_r[bass.ds(p, 1)].rearrange("h p c n -> p (h c) n")).then_inc(wq_in, 16)
                e.wait_ge(wkT_ready, p)
                e.dma_start(wkT_raw[:, :, :], wkT_r[bass.ds(p, 1)].rearrange("h p k c -> p (h k) c")).then_inc(wkT_in, 16)
                e.wait_ge(wv_ready, p)
                e.dma_start(wv_raw[:, :, :], wv_r[bass.ds(p, 1)].rearrange("h p c n -> p (h c) n")).then_inc(wv_in, 16)
                for j in range(JB):
                    e.wait_ge(s_ready, p * 4 + (j - 3))
                    rk_load(p, j)
            def lw_load(n):
                e.dma_start(lw_raw[n][:, :, :], lw_r[n][0]).then_inc(lw_in[n], 16)

            def lin_small():
                e.dma_start(kq_b[:, 0, :], k_b.rearrange("(h p) -> p h", p=P), allow_slow_non_contiguous=True).then_inc(lin_in, 16)
                e.dma_start(kq_b[:, 1, :], q_b.rearrange("(h p) -> p h", p=P), allow_slow_non_contiguous=True).then_inc(lin_in, 16)
                e.dma_start(bb_B[:, :], b_b.rearrange("(a n) -> a n", a=1).to_broadcast([P, H])).then_inc(lin_in, 16)
                e.dma_start(bw_raw[:, :, :], bwT.rearrange("(c p) h -> p c h", p=P)).then_inc(lin_in, 16)

            def lin_rows():
                e.dma_start(v_bias[:, :], v_b.rearrange("(a n) -> a n", a=1).to_broadcast([P, INNER])).then_inc(lin_in, 16)
                e.dma_start(ob_B[:, :], o_b.rearrange("(a n) -> a n", a=1).to_broadcast([P, D])).then_inc(lin_in, 16)

            wo_load(e, 0, Wo, [lambda: lw_load(0), lambda: lw_load(1), lin_small, lambda: lw_load(2), lambda: lw_load(3), lin_rows])
            with e.Fori(1, HP) as p:
                for n in range(4):
                    e.wait_ge(lw_ready[n], p)
                    e.dma_start(lw_raw[n][:, :, :], lw_r[n][bass.ds(p, 1)].rearrange("h p c n -> p (h c) n"))\
                        .then_inc(lw_in[n], 16)
            def shared_load(k):
                load_w13(e, k, 0, w1_r[E + k])
                load_w13(e, k, 1, w3_r[E + k])

            def shared_rest():
                for k in range(2):
                    load_w2(e, k, w2_r[E + k], w2_t[E + k])
                e.dma_start(gw_raw[:, :, :], gwT.rearrange("(c p) e -> p c e", p=P)).then_inc(moe_in, 16)

            wo_load(e, 1, owT, [lambda: shared_load(0), lambda: shared_load(1), shared_rest])
            e.wait_ge(xn_ready, 3 * TT)
            e.wait_ge(scratch_io, IO_SPARE)
            e.dma_start(xn_dram.ap()[0:T, :].rearrange("(t p) d -> p t d", p=P), xn_c[:, :, :]).then_inc(scratch_io, 16)
            last_i = last_turn(e)
            ex_load_w13(e, 0, 0)
            ex_load_w2(e, 0, 0)
            ex_load_w13(e, 1, 1)
            ex_load_w2(e, 1, 1)
            ex_load_w13(e, 2, 0)
            for m in range(2):
                ex_load_w13(e, m + 3, 1 - m)
                ex_load_w2(e, m + 2, m)
            for t in range(TT):
                e.wait_ge(sh_x, TT + t + 1)
                e.dma_start(y_dram.ap()[t * P:(t + 1) * P, :], x[:, t, :]).then_inc(y_in, 16)
            with e.Fori(1, last_i + 1) as i:
                for k in range(2):
                    ex_load_w13(e, i * 2 + (k + 3), 1 - k)
                    ex_load_w2(e, i * 2 + (k + 2), k)
            e.wait_ge(acc_done, last_i * 32 + 32)
            e.dma_start(out, y_dram.ap()[0:T, :]).then_inc(out_done, 16)
            for k in range(2):
                for s, n, uses in ((w13_in[k][0], 16, 4 - k), (w13_in[k][1], 16, 4 - k), (w2_in[k], 32, 3)):
                    e.wait_ge(s, last_i * n + uses * n)
                    e.sem_inc(past_loads, 1)
            e.wait_ge(past_loads, 6)
            e.wait_ge(out_done, 16)

        @block.gpsimd
        def _(e):
            e.memset(ident[:, :], 0.0).then_inc(consts, 1)
            e.memset(ones[:, :], 1.0).then_inc(consts, 1)
            e.memset(zeros[:, :], 0.0).then_inc(consts, 1)
            e.memset(eps[:, :], LN_EPS).then_inc(consts, 1)
            e.wait_ge(consts, 4)
            e.affine_select(out=ident[:, :], in_=ident[:, :], compare_op=ALU.not_equal, fill=1.0, base=0,
                            pattern=[[-1, P]], channel_multiplier=1).then_inc(consts, 1)
            for g in range(1, 4):
                wk_lo(e, g)
            xa_pool_weights(e, 0)
            with e.Fori(0, HP - 1) as i:
                xa_pool_weights(e, i + 1)
                xa_pool_wv(e, i)
            wo_first(e, 0, wo_pool_head)
            xa_pool_wv(e, HP - 1)
            wo_pool(e, 0)

            e.wait_ge(ao_ready, H)
            e.memset(mask[:, :], 1.0).then_inc(consts, 1)
            e.wait_ge(consts, 6)
            e.affine_select(out=mask[:, :], in_=mask[:, :], compare_op=ALU.is_ge, fill=0.0, base=0,
                            pattern=[[1, P]], channel_multiplier=-1).then_inc(consts, 1)
            e.wait_ge(consts, 7)
            e.affine_select(out=mask[:, SQ:P], in_=mask[:, SQ:P], compare_op=ALU.is_ge, fill=0.0, base=-SQ,
                            pattern=[[0, P - SQ]], channel_multiplier=1).then_inc(mask_ready, 1)
            e.wait_ge(small_hi, SP_BETA)
            e.tensor_tensor(bw_l[:, :, :], bw_raw[:, :, :], bw_h[:, :, :], ALU.subtract).then_inc(small_lo, 1)
            for n in range(4):
                la_pool_split(e, n, 0)
            with e.Fori(0, HP - 1) as i:
                for n in range(4):
                    la_pool_split(e, n, i + 1)
            wo_first(e, 1, wo_pool_head)
            e.wait_ge(ao_ready, 2 * H)
            e.wait_ge(wo_ready, H + 2)
            e.memset(w2_raw[FW[-1]:P, :, FC - 1, :], 0.0).then_inc(consts, 1)
            e.wait_ge(consts, 8)
            wo_pool(e, 1)

            e.wait_ge(x_ready, 2 * TT)
            e.memset(below[:, :], 1.0).then_inc(pool_consts, 1)
            e.iota(iota_e[:, :], [[1, P]], base=0, channel_multiplier=0, allow_small_or_imprecise_dtypes=True).then_inc(pool_consts, 1)
            e.iota(part_i[:, 0:1], [[0, 1]], base=0, channel_multiplier=1).then_inc(pool_consts, 1)
            e.iota(spare[:, :], [[0, 1]], base=T + 1, channel_multiplier=1, allow_small_or_imprecise_dtypes=True).then_inc(pool_consts, 1)
            e.iota(tok_1[:, :], [[P, TT]], base=1, channel_multiplier=1, allow_small_or_imprecise_dtypes=True).then_inc(pool_consts, 1)
            e.memset(strict[:, :], 1.0).then_inc(pool_consts, 1)
            e.wait_ge(pool_consts, 6)
            e.affine_select(out=below[:, :], in_=below[:, :], compare_op=ALU.is_gt, fill=0.0, base=0,
                            pattern=[[CT, E]], channel_multiplier=-1).then_inc(pool_consts, 1)
            e.affine_select(out=strict[:, :], in_=strict[:, :], compare_op=ALU.is_gt, fill=0.0, base=0,
                            pattern=[[1, P]], channel_multiplier=-1).then_inc(pool_consts, 1)
            e.wait_ge(small_hi, SP_ROUTER)
            e.tensor_tensor(gw_l[:, :, :], gw_raw[:, :, :], gw_h[:, :, :], ALU.subtract).then_inc(small_lo, 1)
            ex_pool_w2(e, 0, 1)
            ex_pool_w2(e, 1, 2)
            last_i = last_turn(e)
            e.wait_ge(scratch_io, IO_TOKENS)
            e.wait_ge(small_dve, DV_TOKENS)
            for k in range(2):
                ex_rows(e, take, k, k)
            e.wait_ge(idx_ready, 2)
            for k in range(2):
                ex_gather(e, k)
            e.wait_ge(xeT_ps, 1)
            ex_rows(e, take, 2, 0)
            e.wait_ge(idx_ready, 3)
            ex_gather(e, 0)
            for m in range(4):
                ex_pool(e, m // 2, m % 2)
            with e.Fori(2, last_i + 1) as i:
                ex_pool(e, i, 0)
                ex_pool(e, i, 1)
            for k in range(2):
                m = last_i * 2 + k
                e.wait_ge(acc_done, m * 16)
                ex_rows(e, give, m, k)
                e.wait_ge(ob_ready, m + 1)
                e.wait_ge(idx_ready, last_i * 4 + (6 + k))
                e.sem_inc(acc_turn, 1)
                ex_scatter(e, k)

        @block.scalar
        def _(e):
            e.wait_ge(consts, 5)
            def ctxT_hi(g):
                kv = slice(g * G4, (g + 1) * G4)
                e.wait_ge(ctxT_arrived[g], 16)
                e.activation(cT_h[:, :, kv], ctxT[:, :, kv], ACT.Copy).then_inc(cT_hi_s, 1)

            def wk_hi(g):
                kv = slice(g * G4, (g + 1) * G4)
                e.wait_ge(wk_arrived[g], 16)
                e.activation(wk_h[:, :, kv], wk_raw[:, :, kv], ACT.Copy).then_inc(wk_hi_s, 1)

            def squares(g, t):
                e.wait_ge(k_ps, g * KT + (t + 1))
                e.wait_ge(sqk_free, g * KT + (t + 3))
                e.activation(sqk[:, t % 2, :], ps[:, 4 + t % 4, :], ACT.Square, scale=RSD).then_inc(sqk_ready, 1)

            e.activation(rms[:, 0:1], eps[:, :], ACT.Copy)
            wk_hi(0)
            ctxT_hi(0)
            ctxT_hi(1)
            for t in range(KT):
                squares(0, t)
                if t in (1, 4):
                    ctxT_hi(2 + t // 4)
                if t in (6, 8, 10):
                    wk_hi(t // 2 - 2)
            layernorm_act_std(e, 0)
            xa_act_weights(e, 0)
            with e.Fori(1, 3) as g:
                for t in range(KT):
                    squares(g, t)
            layernorm_act_hi(e, 0)
            for t in range(KT):
                squares(3, t)
            e.wait_ge(small_dve, DV_SSK)
            e.activation(rk_rms[:, :, :], ssk[:, :, :], ACT.Sqrt, bias=eps[:, 0:1]).then_inc(rk_sqrt, 1)
            xa_act_q(e, 0, 0)
            e.wait_ge(small_ps, PS_RKT)
            for n in range(2):
                e.activation(rkT[:, n, :], ps[:, 6 + n, 0:P], ACT.Copy).then_inc(rkT_ready, 1)
            xa_act_q(e, 0, 1)
            xa_act_rms(e, 0)
            xa_act_qp(e, 0)

            def pair(i, more):
                if more:
                    xa_act_weights(e, i + 1)
                xa_act_exp(e, i, 0)
                xa_act_wv(e, i)
                for j in range(1, JB):
                    xa_act_exp(e, i, j)
                if more:
                    xa_act_q(e, i + 1, 0)
                    xa_act_q(e, i + 1, 1)
                xa_act_pT(e, i, 0)
                xa_act_pT(e, i, 1)
                if more:
                    xa_act_rms(e, i + 1)
                xa_act_u(e, i, 0)
                xa_act_pT(e, i, 2)
                xa_act_u(e, i, 1)
                xa_act_pT(e, i, 3)
                xa_act_u(e, i, 2)
                xa_act_u(e, i, 3)
                if more:
                    xa_act_qp(e, i + 1)
            with e.Fori(0, HP - 1) as i:
                pair(i, True)
            wo_first(e, 0, wo_act_head)
            pair(HP - 1, False)

            wo_act(e, 0)
            e.wait_ge(lin_in, 96)
            e.activation(bw_h[:, :, :], bw_raw[:, :, :], ACT.Copy).then_inc(small_hi, 1)
            for n in range(4):
                la_act_split(e, n, 0)
            layernorm_act_std(e, 1)
            layernorm_act_hi(e, 1)
            e.wait_ge(small_ps, PS_BETAT)
            e.activation(betaT[:, :], ps[0:H, 4, :], ACT.Copy).then_inc(small_act, 1)
            e.wait_ge(sp_dve, 1)
            e.activation(sp[:, 1, :], sp[:, 1, :], ACT.Exp).then_inc(sp_act, 1)
            e.wait_ge(sp_dve, 2)
            e.activation(sp[:, 3, :], sp[:, 2, :], ACT.Ln).then_inc(sp_act, 1)
            e.wait_ge(small_dve, DV_KQB)
            with e.Fori(0, HP - 1) as i:
                la_act(e, i, True)
            wo_first(e, 1, wo_act_head)
            la_act(e, HP - 1, False)

            wo_act(e, 1)
            e.wait_ge(x_ready, 2 * TT)
            e.wait_ge(moe_in, 16)
            e.activation(gw_h[:, :, :], gw_raw[:, :, :], ACT.Copy).then_inc(small_hi, 1)
            layernorm_act_std(e, 2)
            layernorm_act_hi(e, 2)
            e.wait_ge(consts, 8)
            ex_act_w2(e, 0, 1)
            e.wait_ge(small_ps, PS_LOGITST)
            e.activation(gateT[:, :], ps[0:E, 4, :], ACT.Copy).then_inc(small_act, 1)
            ex_act_w2(e, 1, 1)
            for u in range(NSH):
                if u >= 1:
                    ex_act_hT(e, (u - 1) % 2, u - 1)
                ex_act_silu(e, u % 2, u)
                if u == 0:
                    e.wait_ge(rt_dve, 1)
                    for t in range(TT):
                        last = e.activation(gate[:, t, :], ps[:, 4, t * E:(t + 1) * E], ACT.Exp, bias=r_small[:, 0, t:t + 1],
                                            accum_out=r_small[:, 1, t:t + 1])
                    last.then_inc(rt_act, 1)
                if u == NSH - 2:
                    last_act = last_turn(e)
                    ex_act_w13(e, 0, 0, 2)
                    ex_act_w13(e, 0, 1, 2)
            ex_act_xT(e, 0, 0)
            ex_act(e, 0, 0)
            ex_act(e, 0, 1)
            with e.Fori(1, last_act + 1) as i:
                ex_act(e, i, 0)
                ex_act(e, i, 1)
            ex_act_hT(e, 1, last_act * 2 + (NSH + 1))

        @block.vector
        def _(e):
            def ctxT_lo(g):
                kv = slice(g * G4, (g + 1) * G4)
                e.wait_ge(cT_hi_s, g + 1)
                e.tensor_tensor(cT_l[:, :, kv], ctxT[:, :, kv], cT_h[:, :, kv], ALU.subtract).then_inc(cT_ready, 1)

            def sums(g, t):
                e.wait_ge(sqk_ready, g * KT + (t + 1))
                e.tensor_reduce(ssk[:, t, bass.ds(g * 4, 4)], sqk[:, t % 2, :].rearrange("p (h n) -> p h n", n=P),
                                AX.X, ALU.add).then_inc(sqk_free, 1)

            e.sem_inc(sqk_free, 4)
            wk_lo(e, 0)
            ctxT_lo(0)
            ctxT_lo(1)
            for t in range(KT):
                sums(0, t)
                if t in (1, 4):
                    ctxT_lo(2 + t // 4)
                if t == KT // 2 - 1:
                    e.wait_ge(x_in_s, 16)
                if KT // 2 <= t < KT // 2 + TT:
                    ln_stats(e, t - KT // 2)
            ln_mean_var(e)
            e.wait_ge(g_in_s, 32)
            e.tensor_tensor(gqk[:, 2:3], gqk[:, 0:1], gqk[:, 1:2], ALU.mult).then_inc(small_dve, 1)
            ln_scale(e, 0, xn_a)
            with e.Fori(1, 3) as g:
                for t in range(KT):
                    sums(g, t)
            layernorm_split_dve(e, 0)
            for t in range(KT):
                sums(3, t)
            e.wait_ge(sqk_free, 4 * KT + 4)
            e.sem_inc(small_dve, 1)
            e.wait_ge(rk_sqrt, 1)
            e.reciprocal(ssk[:, :, :], rk_rms[:, :, :]).then_inc(dve_step, 1)
            steps[0] += 1
            e.wait_ge(dve_step, steps[0])
            e.tensor_scalar(ssk[:, :, :], ssk[:, :, :], RSD, None, ALU.mult).then_inc(small_dve, 1)
            for k in range(2):
                xa_dve_qsplit(e, 0, k)
            xa_dve_rq(e, 0)

            def pair(i, more):
                e.wait_ge(rq_ready, i + 1)
                xa_dve_scores(e, i, 0)
                xa_dve_scores(e, i, 1)
                xa_dve_norm(e, i, 0)
                xa_dve_scores(e, i, 2)
                xa_dve_norm(e, i, 1)
                xa_dve_scores(e, i, 3)
                xa_dve_norm(e, i, 2)
                xa_dve_norm(e, i, 3)
                if more:
                    xa_dve_qsplit(e, i + 1, 0)
                    xa_dve_qsplit(e, i + 1, 1)
                    xa_dve_rq(e, i + 1)
                xa_dve_u(e, i, 0)
                for j in range(1, JB):
                    xa_dve_u(e, i, j)
                xa_dve_ao(e, i)
            with e.Fori(0, HP - 1) as i:
                pair(i, True)
            wo_first(e, 0, wo_dve_head)
            pair(HP - 1, False)
            wo_dve(e, 0)

            def add_y(n):
                for t in range(TT):
                    e.wait_ge(y_ps, TT * n + t + 1)
                    e.tensor_tensor(x[:, t, :], x[:, t, :], ps[:, t, :], ALU.add).then_inc(x_ready, 1)
                e.wait_ge(x_ready, TT * (n + 1))

            def step(ins):
                steps[0] += 1
                ins.then_inc(dve_step, 1)
                e.wait_ge(dve_step, steps[0])

            add_y(0)
            layernorm_dve(e, 1, xn_b)
            layernorm_split_dve(e, 1)
            e.wait_ge(lin_in, 96)
            e.tensor_scalar(kq_b[:, :, :], kq_b[:, :, :], RSD, None, ALU.mult).then_inc(small_dve, 1)
            e.wait_ge(small_ps, PS_BETA)
            step(e.tensor_tensor(sp[:, 0, :].rearrange("p (t h) -> p t h", h=H), ps[:, 5, 0:TT * H].rearrange("p (t h) -> p t h", h=H),
                                 bb_B[:, :].unsqueeze(1).to_broadcast([P, TT, H]), ALU.add))
            e.scalar_tensor_tensor(sp[:, 1, :], sp[:, 0, :], -1.0, sp[:, 0, :], ALU.mult, ALU.min).then_inc(sp_dve, 1)
            e.wait_ge(sp_act, 1)
            e.tensor_scalar(sp[:, 2, :], sp[:, 1, :], 1.0, None, ALU.add).then_inc(sp_dve, 1)
            e.wait_ge(sp_dve, 2)
            step(e.tensor_scalar(sp[:, 4, :], sp[:, 2, :], 1.0, None, ALU.subtract))
            step(e.scalar_tensor_tensor(sp[:, 5, :], sp[:, 4, :], 0.0, sp[:, 1, :], ALU.is_equal, ALU.mult))
            step(e.tensor_scalar(sp[:, 4, :], sp[:, 4, :], 1e-30, None, ALU.max))
            step(e.reciprocal(sp[:, 4, :], sp[:, 4, :]))
            step(e.tensor_tensor(sp[:, 4, :], sp[:, 4, :], sp[:, 1, :], ALU.mult))
            e.wait_ge(sp_act, 2)
            step(e.tensor_tensor(sp[:, 4, :], sp[:, 4, :], sp[:, 3, :], ALU.mult))
            step(e.tensor_tensor(sp[:, 4, :], sp[:, 4, :], sp[:, 5, :], ALU.add))
            step(e.scalar_tensor_tensor(beta[:, :, :].rearrange("p t h -> p (t h)"), sp[:, 0, :], 0.0, sp[:, 4, :], ALU.max, ALU.add))
            for t in range(TT):
                e.tensor_tensor(x[:, t, :], x[:, t, :], ob_B[:, :], ALU.add).then_inc(dve_step, 1)
            steps[0] += TT
            e.wait_ge(dve_step, steps[0])
            step(e.tensor_copy(ones_r[:, :], ones[:, :]))
            e.wait_ge(mask_ready, 1)
            with e.Fori(0, HP - 1) as i:
                la_dve(e, i)
            wo_first(e, 1, wo_dve_head)
            la_dve(e, HP - 1)
            wo_dve(e, 1)
            add_y(1)

            layernorm_dve(e, 2, xn_c)
            layernorm_split_dve(e, 2)
            def router():
                lg = ps[:, 4, 0:TT * E].rearrange("p (t n) -> p t n", n=E)
                e.wait_ge(small_ps, PS_LOGITS)
                e.tensor_reduce(r_small[:, 0, :], lg, AX.X, ALU.max, negate=True).then_inc(rt_dve, 1)
                e.wait_ge(rt_act, 1)
                step(e.reciprocal(r_small[:, 2, :], r_small[:, 1, :]))
                step(e.tensor_tensor(gate[:, :, :], gate[:, :, :], r_small[:, 2, :].unsqueeze(2).to_broadcast([P, TT, E]), ALU.mult))
                for t in range(TT):
                    e.max(top_w[:, t, :], gate[:, t, :]).then_inc(dve_step, 1)
                steps[0] += TT
                e.wait_ge(dve_step, steps[0])
                for t in range(TT):
                    e.max_index(top_i[:, t, :], top_w[:, t, :], gate[:, t, :]).then_inc(dve_step, 1)
                steps[0] += TT
                e.wait_ge(dve_step, steps[0])

            def choices():
                step(e.tensor_copy(top_f[:, :, :], top_i[:, :, :]))
                e.wait_ge(pool_consts, 8)
                for t in range(TT):
                    e.tensor_tensor(hot[:, t, :, :], iota_e[:, 0:E].unsqueeze(1).to_broadcast([P, TOP_K, E]),
                                    top_f[:, t, 0:TOP_K].unsqueeze(2).to_broadcast([P, TOP_K, E]), ALU.is_equal).then_inc(dve_step, 1)
                steps[0] += TT
                e.wait_ge(dve_step, steps[0])
                for t in range(TT):
                    e.tensor_reduce(chosen[:, t, :], hot[:, t, :, :].rearrange("p k n -> p n k"), AX.X, ALU.add).then_inc(dve_step, 1)
                steps[0] += TT
                e.wait_ge(dve_step, steps[0])
                step(e.memset(before[:, 0, :], 0.0))
                for t in range(TT):
                    step(e.tensor_tensor(before[:, t + 1, :], before[:, t, :], chosen[:, t, :], ALU.add))
                e.tensor_copy(chosen4[:, :, :], before[:, TT, :].unsqueeze(2).to_broadcast([P, E, CT])).then_inc(rt_dve, 1)

            def counts():
                e.wait_ge(small_ps, PS_POS)
                step(e.tensor_copy(pos[:, :, :], ps[:, 4, P:P + TT * E].rearrange("p (t n) -> p t n", n=E)))
                step(e.tensor_copy(cnt[:, 0:1], ps[:, 4, 2 * P:2 * P + 1]))
                step(e.tensor_scalar(part_i[:, 1:2], part_i[:, 0:1], 2, None, ALU.arith_shift_right))
                step(e.tensor_scalar(part_i[:, 2:3], part_i[:, 0:1], CT - 1, 7, ALU.bitwise_and, ALU.arith_shift_left))
                step(e.tensor_copy(part[:, 0:2], part_i[:, 1:3]))
                step(e.tensor_scalar(part[:, 2:3], part[:, 1:2], 0.0, None, ALU.is_equal))
                step(e.tensor_tensor(cnt[:, 1:2], cnt[:, 0:1], part[:, 1:2], ALU.is_gt))
                e.tensor_scalar(valid_B[:, :], ones[:, :], cnt[:, 1:2], None, ALU.mult).then_inc(small_dve, 1)

            def places():
                e.wait_ge(small_ps, PS_PREFIX)
                step(e.tensor_copy(cnt[:, 2:4], ps[:, 4, 2 * P + 1:2 * P + 3]))
                step(e.tensor_copy(start[:, :], ps[:, 4, 2 * P + 3:2 * P + 3 + E]))
                e.tensor_scalar(m_hot[:, :], iota_e[:, 0:ML], cnt[:, 2:3], cnt[:, 1:2], ALU.is_equal, ALU.mult).then_inc(small_dve, 1)
                step(e.scalar_tensor_tensor(pos[:, :, :], start[:, :].unsqueeze(1).to_broadcast([P, TT, E]), float(P),
                                            pos[:, :, :], ALU.mult, ALU.add))
                for t in range(TT):
                    e.tensor_tensor(hotp[:, t, :, :], hot[:, t, :, :], pos[:, t, :].unsqueeze(1).to_broadcast([P, TOP_K, E]),
                                    ALU.mult).then_inc(dve_step, 1)
                steps[0] += TT
                e.wait_ge(dve_step, steps[0])
                step(e.tensor_reduce(slot_f[:, :, :].rearrange("p t k -> p (t k)"), hotp[:, :, :, :].rearrange("p t k n -> p (t k) n"),
                                     AX.X, ALU.add))
                step(e.tensor_copy(slot_i[:, 0, :], slot_f[:, :, :].rearrange("p t k -> p (t k)")))
                step(e.tensor_scalar(slot_i[:, 1, :], slot_i[:, 0, :], P - 1, None, ALU.bitwise_and))
                step(e.tensor_scalar(slot_i[:, 2, :], slot_i[:, 0, :], 7, None, ALU.arith_shift_right))
                step(e.tensor_copy(slot_rm[:, :, :], slot_i[:, 1:3, :]))

            def lists():
                e.wait_ge(small_ps, PS_LIST)
                step(e.memset(lst_f[:, :, :], 0.0))
                step(e.tensor_copy(lst_f[0:1, EXPERT, 0:ML], ps[0:1, 4, LC:LC + ML]))
                step(e.tensor_scalar(lst_j[0:1, 0:ML], ps[0:1, 4, LC + ML:LC + 2 * ML], 1.0 / P, None, ALU.mult))
                step(e.tensor_scalar(lst_f[0:1, EXPERT, ML:ML + 1], cnt[0:1, 3:4], 1.0, None, ALU.subtract))
                step(e.tensor_copy(lst_f[0:1, LOADED, 0:ML], ps[0:1, 4, 2 * P:2 * P + ML]))
                step(e.tensor_tensor(lst_f[0:1, SLOT, 0:ML], iota_e[0:1, 0:ML], lst_j[0:1, 0:ML], ALU.subtract))
                step(e.tensor_copy(lst_f[0:1, ODD, 1:ML + 1], lst_j[0:1, 0:ML]))
                step(e.tensor_copy(lst[0:1, :, :], lst_f[0:1, :, :]))
                step(e.tensor_scalar(lst[0:1, EXPERT, ML:ML + 1], lst[0:1, EXPERT, ML:ML + 1], 1, None, ALU.arith_shift_right))
                e.tensor_scalar(lst[0:1, SLOT:ODD + 1, :], lst[0:1, SLOT:ODD + 1, :], 1, None, ALU.bitwise_and).then_inc(small_dve, 1)

            def seats():
                for t in range(TT):
                    q = slice(t * TOP_K, (t + 1) * TOP_K)
                    e.tensor_tensor(seat[:, q, :], iota_e[:, :].unsqueeze(1).to_broadcast([P, TOP_K, P]),
                                    slot_rm[:, 0, q].unsqueeze(2).to_broadcast([P, TOP_K, P]), ALU.is_equal).then_inc(dve_step, 1)
                steps[0] += TT

            def items():
                for t in range(TT):
                    q = slice(t * TOP_K, (t + 1) * TOP_K)
                    e.tensor_tensor(item[:, q, 0, :], iota_e[:, 0:ML].unsqueeze(1).to_broadcast([P, TOP_K, ML]),
                                    slot_rm[:, 1, q].unsqueeze(2).to_broadcast([P, TOP_K, ML]), ALU.is_equal).then_inc(dve_step, 1)
                steps[0] += TT
                e.wait_ge(dve_step, steps[0])
                for t in range(TT):
                    q = slice(t * TOP_K, (t + 1) * TOP_K)
                    e.tensor_tensor(item[:, q, 1, :], item[:, q, 0, :],
                                    top_w[:, t, 0:TOP_K].unsqueeze(2).to_broadcast([P, TOP_K, ML]), ALU.mult).then_inc(dve_step, 1)
                steps[0] += TT
                e.wait_ge(dve_step, steps[0])
                for t in range(TT):
                    q = slice(t * TOP_K, (t + 1) * TOP_K)
                    e.tensor_scalar(item[:, q, 0, :], item[:, q, 0, :], tok_1[:, t:t + 1], None, ALU.mult).then_inc(dve_step, 1)
                steps[0] += TT
                e.wait_ge(dve_step, steps[0])
                e.sem_inc(small_dve, 1)

            def tokens():
                e.wait_ge(small_ps, PS_TOKENS)
                rows = ps[:, 4, LC:LC + 2 * ML]
                step(e.tensor_scalar(tl_f[:, 0, :], rows[:, 0:ML], 0.0, spare[:, 0:1], ALU.is_equal, ALU.mult))
                step(e.scalar_tensor_tensor(tl_f[:, 1, :], rows[:, 0:ML], 1.0, tl_f[:, 0, :], ALU.subtract, ALU.add))
                step(e.tensor_copy(wl[:, :], rows[:, ML:2 * ML]))
                e.tensor_copy(tl[:, :], tl_f[:, 1, :]).then_inc(small_dve, 1)

            router_steps = (router, choices, counts, places, lambda: (lists(), seats()), items, tokens)
            for u in range(NSH):
                if u >= 1:
                    ex_dve_hT(e, (u - 1) % 2, u - 1)
                if u >= 2:
                    ex_dve_x(e, u - 2)
                ex_dve_h(e, u % 2, u)
                if u < len(router_steps):
                    router_steps[u]()
                if u == NSH - 2:
                    for n in range(2):
                        ex_dve_w13(e, 0, n, 5 + n)
            last_i = last_turn(e)
            ex_dve_xT(e, 0, 0)
            for m in range(4):
                ex_dve(e, m // 2, m % 2)
            with e.Fori(2, last_i + 1) as i:
                ex_dve(e, i, 0)
                ex_dve(e, i, 1)
            ex_dve_hT(e, 1, last_i * 2 + (NSH + 1))
            e.wait_ge(acc_done, last_i * 32)
            ex_dve_ob(e, last_i * 2 + 2, 0, False)
            ex_dve_ob(e, last_i * 2 + 3, 1, False)

        @block.tensor
        def _(e):
            e.wait_ge(consts, 5)
            def keys(g, t, first=False):
                if t % 4 == 0 and first:
                    e.wait_ge(cT_ready, t // 4 + 1)
                if t == 0:
                    e.wait_ge(wk_ready, g + 1)
                e.wait_ge(sqk_free, g * KT + (t + 1))
                tk = slice(t * P, (t + 1) * P)
                for c in range(CC):
                    m = mm3(ps[:, 4 + t % 4, :], cT_h[:, c, tk], cT_l[:, c, tk],
                            wk_h[:, c, bass.ds(g * G4, G4)], wk_l[:, c, bass.ds(g * G4, G4)], c == 0, c == CC - 1)
                m.then_inc(k_ps, 1)

            for t in range(KT):
                keys(0, t, True)
            with e.Fori(1, 3) as g:
                for t in range(KT):
                    keys(g, t)
            layernorm_pe(e, 0, xn_a)
            for t in range(KT):
                keys(3, t)
            e.wait_ge(xT_ready, TT)
            xa_pe_q(e, 0, 0)
            e.wait_ge(small_dve, DV_RK)
            for n in range(2):
                e.transpose(ps[:, 6 + n, 0:P], ssk[:, n * KT // 2:(n + 1) * KT // 2, :].rearrange("p t h -> p (t h)"),
                            ident[:, :]).then_inc(small_ps, 1)
            xa_pe_q(e, 0, 1)
            xa_pe_ss(e, 0)
            e.wait_ge(rkT_ready, 2)
            xa_pe_qp(e, 0)
            e.wait_ge(ctx_in_s, 16)

            def pair(i, more):
                for j in range(JB):
                    xa_pe_scores(e, i, j)
                if more:
                    xa_pe_q(e, i + 1, 0)
                    xa_pe_q(e, i + 1, 1)
                else:
                    wo_pe_first(e, 0)
                xa_pe_pT(e, i, 0)
                xa_pe_pT(e, i, 1)
                if more:
                    xa_pe_ss(e, i + 1)
                xa_pe_u(e, i, 0)
                xa_pe_pT(e, i, 2)
                xa_pe_u(e, i, 1)
                xa_pe_pT(e, i, 3)
                xa_pe_u(e, i, 2)
                xa_pe_u(e, i, 3)
                if more:
                    xa_pe_qp(e, i + 1)
                xa_pe_ao(e, i)
            with e.Fori(0, HP - 1) as i:
                pair(i, True)
            pair(HP - 1, False)
            wo_pe(e, 0)

            layernorm_pe(e, 1, xn_b)
            e.wait_ge(small_lo, SP_BETA)
            e.wait_ge(xT_ready, 2 * TT)
            for c in range(DC):
                m = mm3(ps[0:H, 4, :], bw_h[:, c, :], bw_l[:, c, :], xT_hi[:, c, :], xT_lo[:, c, :], c == 0, c == DC - 1)
            m.then_inc(small_ps, 1)
            e.wait_ge(small_act, AC_BETA)
            for t in range(TT):
                m = e.transpose(ps[:, 5, t * H:(t + 1) * H], betaT[:, t * P:(t + 1) * P], ident[0:H, 0:H])
            m.then_inc(small_ps, 1)
            with e.Fori(0, HP) as i:
                la_pe(e, i)
            wo_pe_first(e, 1)
            wo_pe(e, 1)

            layernorm_pe(e, 2, xn_c)
            e.wait_ge(small_lo, SP_ROUTER)
            e.wait_ge(xT_ready, 3 * TT)
            for c in range(DC):
                m = mm3(ps[0:E, 4, :], gw_h[:, c, :], gw_l[:, c, :], xT_hi[:, c, :], xT_lo[:, c, :], c == 0, c == DC - 1)
            m.then_inc(small_ps, 1)

            def logits():
                e.wait_ge(small_act, AC_LOGITS)
                for t in range(TT):
                    m = e.transpose(ps[:, 4, t * E:(t + 1) * E], gateT[:, t * P:(t + 1) * P], ident[0:E, 0:E])
                m.then_inc(small_ps, 1)

            def running():
                e.wait_ge(rt_dve, 2)
                e.wait_ge(pool_consts, 8)
                at = slice(P, P + TT * E)
                e.matmul(ps[:, 4, at], strict[:, :], chosen[:, :, :].rearrange("p t n -> p (t n)"), start=True, stop=False)
                e.matmul(ps[:, 4, at], ones[:, :], before[:, 0:TT, :].rearrange("p t n -> p (t n)"), start=False, stop=True)
                m = e.matmul(ps[:, 4, 2 * P:2 * P + 1], chosen4[:, :, :].rearrange("p n j -> p (n j)"), ones[:, 0:1],
                             start=True, stop=True)
                m.then_inc(small_ps, 1)

            def prefix():
                e.wait_ge(small_dve, DV_VALID)
                c = 2 * P + 1
                e.matmul(ps[:, 4, c:c + 1], strict[:, :], cnt[:, 1:2], start=True, stop=True)
                e.matmul(ps[:, 4, c + 1:c + 2], ones[:, :], cnt[:, 1:2], start=True, stop=True)
                e.matmul(ps[:, 4, c + 2:c + 2 + E], valid_B[:, :], below[:, :], start=True, stop=True).then_inc(small_ps, 1)

            def order():
                e.wait_ge(small_dve, DV_ORDER)
                for n, at in enumerate((LC, LC + ML, 2 * P)):
                    m = e.matmul(ps[0:1, 4, at:at + ML], part[:, n:n + 1], m_hot[:, :], start=True, stop=True)
                m.then_inc(small_ps, 1)

            def tokens():
                e.wait_ge(small_dve, DV_SEATS)
                for q in range(TT * TOP_K):
                    m = e.matmul(ps[:, 4, LC:LC + 2 * ML], seat[:, q, :], item[:, q, :, :].rearrange("p a n -> p (a n)"),
                                 start=q == 0, stop=q == TT * TOP_K - 1)
                m.then_inc(small_ps, 1)

            router_steps = {0: logits, 2: running, 3: prefix, 4: order, 6: tokens}
            for u in range(NSH):
                t, w = u % TT, u // TT
                tk = slice(t * P, (t + 1) * P)
                if u >= 2:
                    e.wait_ge(h_ready, u - 1)
                ex_up(lambda c: xT_hi[:, c, tk], lambda c: xT_lo[:, c, tk], u % 2, w, 2 * w + 2)
                if u in router_steps:
                    router_steps[u]()
                if u >= 1:
                    ex_down(e, (u - 1) % 2, u - 1, (u - 1) // TT, (u - 1) // TT + 1)
                if u == NSH - 1:
                    last_i = last_turn(e)
                    e.wait_ge(small_dve, DV_TOKENS)
                    ex_pe_xT(e, 0, 1)
                ex_hT(e, u % 2, u)
            ex_pe(e, 0, 0, True)
            ex_pe(e, 0, 1)
            with e.Fori(1, last_i + 1) as i:
                ex_pe(e, i, 0)
                ex_pe(e, i, 1)
            ex_down(e, 1, last_i * 2 + (NSH + 1), item_value(e, SLOT, last_i * 2 + 1), last_i * 2 + 4)


def kernel(x, ctx_1024, L0_xattn_Wq, L0_xattn_Wk, L0_xattn_Wv, L0_xattn_Wo, L0_xattn_gq, L0_xattn_gk,
           L0_attn_q_w, L0_attn_q_b, L0_attn_k_w, L0_attn_k_b, L0_attn_v_w, L0_attn_v_b, L0_attn_a_w, L0_attn_a_b,
           L0_attn_b_w, L0_attn_b_b, L0_attn_og_w, L0_attn_o_w, L0_attn_o_b, L0_ffn_gate_w, L0_ffn_w1, L0_ffn_w2,
           L0_ffn_w3, L0_ffn_sw1, L0_ffn_sw2, L0_ffn_sw3):
    import numpy as np
    import concourse.bacc as bacc
    from concourse import mybir
    from concourse.bass_utils import run_bass_kernel_spmd

    x, ctx = np.asarray(x), np.asarray(ctx_1024)
    tokens, ctx = x.reshape(-1, x.shape[-1]), ctx.reshape(-1, ctx.shape[-1])
    w1, w2, w3 = (np.asarray(w) for w in (L0_ffn_w1, L0_ffn_w2, L0_ffn_w3))
    dim, inter = w1.shape[1:]
    halves = np.asarray(L0_ffn_sw1).shape[1] // inter

    def halved(w):
        return np.asarray(w).reshape(dim, halves, inter).transpose(1, 0, 2)

    host = {
        "x_in": tokens, "ctx_in": ctx, "ctxT_in": ctx.T,
        "Wq": L0_xattn_Wq, "Wk": L0_xattn_Wk, "WkT": np.asarray(L0_xattn_Wk).T, "Wv": L0_xattn_Wv, "Wo": L0_xattn_Wo,
        "gq": L0_xattn_gq, "gk": L0_xattn_gk,
        "qwT": np.asarray(L0_attn_q_w).T, "q_b": L0_attn_q_b, "kwT": np.asarray(L0_attn_k_w).T, "k_b": L0_attn_k_b,
        "vwT": np.asarray(L0_attn_v_w).T, "v_b": L0_attn_v_b, "bwT": np.asarray(L0_attn_b_w).T, "b_b": L0_attn_b_b,
        "ogwT": np.asarray(L0_attn_og_w).T, "owT": np.asarray(L0_attn_o_w).T, "o_b": L0_attn_o_b,
        "gwT": np.asarray(L0_ffn_gate_w).T,
        "w1": np.concatenate([w1, halved(L0_ffn_sw1)]),
        "w2": np.concatenate([w2, np.asarray(L0_ffn_sw2).reshape(halves, inter, dim)]),
        "w3": np.concatenate([w3, halved(L0_ffn_sw3)]),
    }
    nc = bacc.Bacc("TRN2", target_bir_lowering=False, num_devices=1)
    arrays, args = {}, {}
    for name, a in host.items():
        a = np.ascontiguousarray(a)
        arrays[f"in_{name}"] = a
        args[name] = nc.dram_tensor(f"in_{name}", a.shape, mybir.dt.from_np(a.dtype), kind="ExternalInput").ap()
    out = nc.dram_tensor("out_0", tokens.shape, mybir.dt.from_np(tokens.dtype), kind="ExternalOutput").ap()
    perceiver_block(nc, **args, out=out)
    result = run_bass_kernel_spmd(nc, [arrays], core_ids=[0])
    return result.results[0]["out_0"].reshape(x.shape)
```
